# Optimizing a Trainium2 kernel written in Bass

```python
import numpy as np
import jax
import jax.numpy as jnp

def _softmax(x, axis=-1):
    return jax.nn.softmax(x, axis=axis)

def _gelu(x):
    return jax.nn.gelu(x, approximate=True)

def _silu(x):
    return jax.nn.silu(x)

def _sigmoid(x):
    return jax.nn.sigmoid(x)

def _layernorm(x, axis=-1, eps=1e-05):
    m = jnp.mean(x, axis=axis, keepdims=True)
    v = jnp.var(x, axis=axis, keepdims=True)
    return (x - m) / jnp.sqrt(v + eps)

def _scatter_add(tgt, idx, src, axis=0):
    return tgt.at[idx].add(src)

def _segment_sum(src, seg, n):
    return jax.ops.segment_sum(src, seg, n)
kernel_name = 'mk_seq_preln_d4_jaxref_r8_87b3b8'

def setup_inputs(seed: int=0):
    np.random.seed(seed)
    _w = jnp.asarray

    def _L0_attn_setup():
        import jax, jax.numpy as jnp
        import numpy as np
        HEAD_NUM = 16
        key = jax.random.key(seed)
        ks = jax.random.split(key, 9)
        B, S, D = (4, 256, 128)

        def xavier(k, shape):
            limit = jnp.sqrt(6.0 / (shape[0] + shape[1]))
            return jax.random.uniform(k, shape, jnp.float32, -limit, limit)
        return {'x': jax.random.normal(ks[0], (B, S, D), jnp.float32), 'Wq': xavier(ks[1], (D, D)), 'bq': jnp.zeros((D,), jnp.float32), 'Wk': xavier(ks[2], (D, D)), 'bk': jnp.zeros((D,), jnp.float32), 'Wv': xavier(ks[3], (D, D)), 'bv': jnp.zeros((D,), jnp.float32), 'Wo': xavier(ks[4], (D, D)), 'bo': jnp.zeros((D,), jnp.float32)}
    _L0_attn_in = _L0_attn_setup()

    def _L0_ffn_setup():
        import jax, jax.numpy as jnp
        import numpy as np
        TAU = 10.0
        EPS = 1e-06
        TOP_K = 8

        def _layernorm(x, g, b):
            mu = jnp.mean(x, axis=-1, keepdims=True)
            var = jnp.var(x, axis=-1, keepdims=True)
            return (x - mu) * jax.lax.rsqrt(var + 1e-05) * g + b

        def _unit_rows(W):
            n = jnp.linalg.norm(W, axis=1, keepdims=True)
            return W / jnp.maximum(n, EPS)
        key = jax.random.key(seed)
        ks = jax.random.split(key, 5)
        D, NB, H = (128, 64, 512)
        B, S = (4, 256)
        x = jax.random.normal(ks[0], (B, S, D), dtype=jnp.float32)
        W1 = jax.random.normal(ks[1], (H, D), dtype=jnp.float32) * (1.0 / np.sqrt(D))
        W2 = jax.random.normal(ks[2], (D, H), dtype=jnp.float32) * (1.0 / np.sqrt(H))
        ln_g = jnp.ones((D,), jnp.float32)
        ln_b = jnp.zeros((D,), jnp.float32)
        router_W = jax.random.normal(ks[3], (NB, D), dtype=jnp.float32) * 0.01
        router_b = jnp.zeros((NB,), jnp.float32)
        raw_U = jax.random.normal(ks[4], (NB, D), dtype=jnp.float32) * 0.02
        raw_V = jax.random.normal(jax.random.fold_in(key, 7), (NB, D), dtype=jnp.float32) * 0.02
        gamma = jnp.ones((1, 1, D), jnp.float32) * 0.1
        return {'x': x, 'W1': W1, 'W2': W2, 'ln_g': ln_g, 'ln_b': ln_b, 'router_W': router_W, 'router_b': router_b, 'raw_U': raw_U, 'raw_V': raw_V, 'gamma': gamma}
    _L0_ffn_in = _L0_ffn_setup()

    def _L1_attn_setup():
        import jax, jax.numpy as jnp
        import numpy as np
        from math import sqrt
        EMBED_DIM = 128
        NUM_HEADS = 16
        HEAD_DIM = EMBED_DIM // NUM_HEADS
        SCALE = sqrt(HEAD_DIM)

        def _rotate_half(x):
            x1 = x[..., 0::2]
            x2 = x[..., 1::2]
            return jnp.stack((-x2, x1), axis=-1).reshape(x.shape)

        def _apply_rope(x, seq_len):
            inv_freq = 1.0 / 10000.0 ** (jnp.arange(0, HEAD_DIM, 2, dtype=jnp.float32) / HEAD_DIM)
            pos = jnp.arange(seq_len, dtype=jnp.float32)
            freqs = jnp.outer(pos, inv_freq)
            emb = jnp.concatenate([freqs, freqs], -1)
            cos = jnp.cos(emb)[None, None].astype(x.dtype)
            sin = jnp.sin(emb)[None, None].astype(x.dtype)
            return x * cos + _rotate_half(x) * sin
        key = jax.random.key(seed)
        ks = jax.random.split(key, 9)
        B, S, E = (2, 256, EMBED_DIM)
        s = 1.0 / np.sqrt(E)
        return {'x': jax.random.normal(ks[0], (B, S, E), jnp.float32), 'Wq': jax.random.uniform(ks[1], (E, E), jnp.float32, -s, s), 'bq': jnp.zeros((E,), jnp.float32), 'Wk': jax.random.uniform(ks[2], (E, E), jnp.float32, -s, s), 'bk': jnp.zeros((E,), jnp.float32), 'Wv': jax.random.uniform(ks[3], (E, E), jnp.float32, -s, s), 'bv': jnp.zeros((E,), jnp.float32), 'Wo': jax.random.uniform(ks[4], (E, E), jnp.float32, -s, s), 'bo': jnp.zeros((E,), jnp.float32)}
    _L1_attn_in = _L1_attn_setup()

    def _L1_ffn_setup():
        import jax, jax.numpy as jnp
        import numpy as np
        N_EMBD = 128
        N_STATE = 512
        key = jax.random.key(seed)
        k_x, k_w1, k_b1, k_w2, k_b2 = jax.random.split(key, 5)
        x = jax.random.normal(k_x, (4, 256, N_EMBD), dtype=jnp.float32)
        w1 = jax.random.normal(k_w1, (N_EMBD, N_STATE), dtype=jnp.float32) * (1.0 / np.sqrt(N_EMBD))
        b1 = jax.random.normal(k_b1, (N_STATE,), dtype=jnp.float32) * 0.02
        w2 = jax.random.normal(k_w2, (N_STATE, N_EMBD), dtype=jnp.float32) * (1.0 / np.sqrt(N_STATE))
        b2 = jax.random.normal(k_b2, (N_EMBD,), dtype=jnp.float32) * 0.02
        return {'x': x, 'w1': w1, 'b1': b1, 'w2': w2, 'b2': b2}
    _L1_ffn_in = _L1_ffn_setup()

    def _L2_attn_setup():
        import jax, jax.numpy as jnp
        import numpy as np
        H, KV, DH = (16, 4, 64)

        def _rotate_half(t):
            t1, t2 = (t[..., :DH // 2], t[..., DH // 2:])
            return jnp.concatenate([-t2, t1], axis=-1)
        key = jax.random.key(seed)
        k1, k2, k3, k4, k5 = jax.random.split(key, 5)
        B, L, D = (1, 512, 128)
        s = 0.02
        return {'x': jax.random.normal(k1, (B, L, D), dtype=jnp.float32), 'Wq': jax.random.normal(k2, (D, H * DH), dtype=jnp.float32) * s, 'Wk': jax.random.normal(k3, (D, KV * DH), dtype=jnp.float32) * s, 'Wv': jax.random.normal(k4, (D, KV * DH), dtype=jnp.float32) * s, 'Wo': jax.random.normal(k5, (H * DH, D), dtype=jnp.float32) * s}
    _L2_attn_in = _L2_attn_setup()

    def _L2_ffn_setup():
        import jax, jax.numpy as jnp
        import numpy as np
        B, L, D, H, E, TOP_K = (4, 256, 128, 512, 8, 2)
        LN_EPS = 1e-05
        key = jax.random.key(seed)
        ks = jax.random.split(key, 8)
        x = jax.random.normal(ks[0], (B, L, D), dtype=jnp.float32)
        gate_w = jax.random.normal(ks[1], (D, E), dtype=jnp.float32) / np.sqrt(D)
        w1 = jax.random.normal(ks[2], (E, D, H), dtype=jnp.float32) / np.sqrt(D)
        b1 = jnp.zeros((E, H), dtype=jnp.float32)
        w2 = jax.random.normal(ks[3], (E, H, D), dtype=jnp.float32) / np.sqrt(H)
        b2 = jnp.zeros((E, D), dtype=jnp.float32)
        gamma = jnp.ones((D,), dtype=jnp.float32)
        beta = jnp.zeros((D,), dtype=jnp.float32)
        return {'x': x, 'gate_w': gate_w, 'w1': w1, 'b1': b1, 'w2': w2, 'b2': b2, 'gamma': gamma, 'beta': beta}
    _L2_ffn_in = _L2_ffn_setup()

    def _L3_attn_setup():
        import jax, jax.numpy as jnp
        import numpy as np
        B, T, E, H = (2, 256, 128, 16)
        D = E // H
        key = jax.random.key(seed)
        k = jax.random.split(key, 6)
        return {'x': jax.random.normal(k[0], (B, T, E), dtype=jnp.float32), 'w_att_val': jax.random.normal(k[1], (H, D, D), dtype=jnp.float32) * (6.0 / D) ** 0.5, 'wv_w': jax.random.normal(k[2], (E, E), dtype=jnp.float32) * E ** (-0.5), 'wv_b': jnp.zeros((E,), dtype=jnp.float32), 'out_w': jax.random.normal(k[3], (E, E), dtype=jnp.float32) * E ** (-0.5), 'out_b': jnp.zeros((E,), dtype=jnp.float32)}
    _L3_attn_in = _L3_attn_setup()

    def _L3_ffn_setup():
        import jax, jax.numpy as jnp
        import numpy as np
        B, S, D = (1, 256, 128)
        I = 256
        E = 8
        K = 2
        LIMIT = 7.0
        ALPHA = 1.702
        EPS = 1e-05

        def _swiglu(h):
            x_glu = jnp.minimum(h[..., ::2], LIMIT)
            x_lin = jnp.clip(h[..., 1::2], -LIMIT, LIMIT)
            return x_glu * jax.nn.sigmoid(ALPHA * x_glu) * (x_lin + 1.0)

        def _moe(t, gate_w, gate_b, mlp1_w, mlp1_b, mlp2_w, mlp2_b):
            T = t.shape[0]
            logits = t @ gate_w + gate_b
            top_v, top_i = jax.lax.top_k(logits, K)
            probs = jax.nn.softmax(top_v, axis=-1)
            w = jnp.zeros((T, E), t.dtype).at[jnp.arange(T)[:, None], top_i].set(probs)

            def body(acc, ew):
                w1, b1, w2, b2, we = ew
                h = _swiglu(t @ w1 + b1)
                y = h @ w2 + b2
                return (acc + we[:, None] * y, None)
            acc0 = jnp.zeros((T, t.shape[1]), t.dtype)
            acc, _ = jax.lax.scan(body, acc0, (mlp1_w, mlp1_b, mlp2_w, mlp2_b, w.T))
            return acc
        key = jax.random.key(seed)
        ks = jax.random.split(key, 4)
        s = 0.02
        return {'x': jax.random.normal(ks[0], (B, S, D), jnp.float32), 'norm_scale': jnp.ones((D,), jnp.float32), 'gate_w': jax.random.normal(ks[1], (D, E), jnp.float32) * s, 'gate_b': jnp.zeros((E,), jnp.float32), 'mlp1_w': jax.random.normal(ks[2], (E, D, 2 * I), jnp.float32) * s, 'mlp1_b': jnp.zeros((E, 2 * I), jnp.float32), 'mlp2_w': jax.random.normal(ks[3], (E, I, D), jnp.float32) * s, 'mlp2_b': jnp.zeros((E, D), jnp.float32)}
    _L3_ffn_in = _L3_ffn_setup()
    _d = {'L0_attn_x': _L0_attn_in['x'], 'L0_attn_Wq': _L0_attn_in['Wq'], 'L0_attn_bq': _L0_attn_in['bq'], 'L0_attn_Wk': _L0_attn_in['Wk'], 'L0_attn_bk': _L0_attn_in['bk'], 'L0_attn_Wv': _L0_attn_in['Wv'], 'L0_attn_bv': _L0_attn_in['bv'], 'L0_attn_Wo': _L0_attn_in['Wo'], 'L0_attn_bo': _L0_attn_in['bo'], 'L0_ffn_W1': _L0_ffn_in['W1'], 'L0_ffn_W2': _L0_ffn_in['W2'], 'L0_ffn_ln_g': _L0_ffn_in['ln_g'], 'L0_ffn_ln_b': _L0_ffn_in['ln_b'], 'L0_ffn_router_W': _L0_ffn_in['router_W'], 'L0_ffn_router_b': _L0_ffn_in['router_b'], 'L0_ffn_raw_U': _L0_ffn_in['raw_U'], 'L0_ffn_raw_V': _L0_ffn_in['raw_V'], 'L0_ffn_gamma': _L0_ffn_in['gamma'], 'L1_attn_Wq': _L1_attn_in['Wq'], 'L1_attn_bq': _L1_attn_in['bq'], 'L1_attn_Wk': _L1_attn_in['Wk'], 'L1_attn_bk': _L1_attn_in['bk'], 'L1_attn_Wv': _L1_attn_in['Wv'], 'L1_attn_bv': _L1_attn_in['bv'], 'L1_attn_Wo': _L1_attn_in['Wo'], 'L1_attn_bo': _L1_attn_in['bo'], 'L1_ffn_w1': _L1_ffn_in['w1'], 'L1_ffn_b1': _L1_ffn_in['b1'], 'L1_ffn_w2': _L1_ffn_in['w2'], 'L1_ffn_b2': _L1_ffn_in['b2'], 'L2_attn_Wq': _L2_attn_in['Wq'], 'L2_attn_Wk': _L2_attn_in['Wk'], 'L2_attn_Wv': _L2_attn_in['Wv'], 'L2_attn_Wo': _L2_attn_in['Wo'], 'L2_ffn_gate_w': _L2_ffn_in['gate_w'], 'L2_ffn_w1': _L2_ffn_in['w1'], 'L2_ffn_b1': _L2_ffn_in['b1'], 'L2_ffn_w2': _L2_ffn_in['w2'], 'L2_ffn_b2': _L2_ffn_in['b2'], 'L2_ffn_gamma': _L2_ffn_in['gamma'], 'L2_ffn_beta': _L2_ffn_in['beta'], 'L3_attn_w_att_val': _L3_attn_in['w_att_val'], 'L3_attn_wv_w': _L3_attn_in['wv_w'], 'L3_attn_wv_b': _L3_attn_in['wv_b'], 'L3_attn_out_w': _L3_attn_in['out_w'], 'L3_attn_out_b': _L3_attn_in['out_b'], 'L3_ffn_norm_scale': _L3_ffn_in['norm_scale'], 'L3_ffn_gate_w': _L3_ffn_in['gate_w'], 'L3_ffn_gate_b': _L3_ffn_in['gate_b'], 'L3_ffn_mlp1_w': _L3_ffn_in['mlp1_w'], 'L3_ffn_mlp1_b': _L3_ffn_in['mlp1_b'], 'L3_ffn_mlp2_w': _L3_ffn_in['mlp2_w'], 'L3_ffn_mlp2_b': _L3_ffn_in['mlp2_b']}
    _x0 = _d['L0_attn_x']
    _d['L0_attn_x'] = jax.random.normal(jax.random.fold_in(jax.random.key(seed), 1), (1, 2048, 128), dtype=_x0.dtype)
    del _x0
    return _d

def reference(L0_attn_x, L0_attn_Wq, L0_attn_bq, L0_attn_Wk, L0_attn_bk, L0_attn_Wv, L0_attn_bv, L0_attn_Wo, L0_attn_bo, L0_ffn_W1, L0_ffn_W2, L0_ffn_ln_g, L0_ffn_ln_b, L0_ffn_router_W, L0_ffn_router_b, L0_ffn_raw_U, L0_ffn_raw_V, L0_ffn_gamma, L1_attn_Wq, L1_attn_bq, L1_attn_Wk, L1_attn_bk, L1_attn_Wv, L1_attn_bv, L1_attn_Wo, L1_attn_bo, L1_ffn_w1, L1_ffn_b1, L1_ffn_w2, L1_ffn_b2, L2_attn_Wq, L2_attn_Wk, L2_attn_Wv, L2_attn_Wo, L2_ffn_gate_w, L2_ffn_w1, L2_ffn_b1, L2_ffn_w2, L2_ffn_b2, L2_ffn_gamma, L2_ffn_beta, L3_attn_w_att_val, L3_attn_wv_w, L3_attn_wv_b, L3_attn_out_w, L3_attn_out_b, L3_ffn_norm_scale, L3_ffn_gate_w, L3_ffn_gate_b, L3_ffn_mlp1_w, L3_ffn_mlp1_b, L3_ffn_mlp2_w, L3_ffn_mlp2_b):

    def _L0_attn_ref(x, Wq, bq, Wk, bk, Wv, bv, Wo, bo):
        import jax, jax.numpy as jnp
        import numpy as np
        HEAD_NUM = 16
        B, S, D = x.shape
        H = HEAD_NUM
        hd = D // H

        def proj(W, b):
            return (x @ W.T + b).reshape(B, S, H, hd).transpose(0, 2, 1, 3)
        Q, K, V = (proj(Wq, bq), proj(Wk, bk), proj(Wv, bv))
        scale = 1.0 / jnp.sqrt(jnp.float32(hd))
        scores = jnp.einsum('bhqd,bhkd->bhqk', Q, K) * scale
        attn = jax.nn.softmax(scores, axis=-1)
        out = jnp.einsum('bhqk,bhkd->bhqd', attn, V)
        out = out.transpose(0, 2, 1, 3).reshape(B, S, D)
        return out @ Wo.T + bo

    def _L0_ffn_ref(x, W1, W2, ln_g, ln_b, router_W, router_b, raw_U, raw_V, gamma):
        import jax, jax.numpy as jnp
        import numpy as np
        TAU = 10.0
        EPS = 1e-06
        TOP_K = 8

        def _layernorm(x, g, b):
            mu = jnp.mean(x, axis=-1, keepdims=True)
            var = jnp.var(x, axis=-1, keepdims=True)
            return (x - mu) * jax.lax.rsqrt(var + 1e-05) * g + b

        def _unit_rows(W):
            n = jnp.linalg.norm(W, axis=1, keepdims=True)
            return W / jnp.maximum(n, EPS)
        B, S, D = x.shape
        x_flat = x.reshape(-1, D)
        r_raw = _layernorm(x_flat, ln_g, ln_b) @ router_W.T + router_b
        r = jnp.clip(r_raw, -TAU, TAU)
        alpha = jax.nn.softplus(r)
        phi, idx = jax.lax.top_k(alpha, TOP_K)
        S_sum = jnp.sum(phi, axis=-1, keepdims=True)
        Z = phi / (S_sum + EPS) * jnp.tanh(S_sum)
        U_sel = _unit_rows(raw_U)[idx]
        V_sel = _unit_rows(raw_V)[idx]
        h_lat = jnp.einsum('nd,nkd->nk', x_flat, U_sel)
        dyn = jnp.einsum('nk,nkd->nd', h_lat * Z, V_sel).reshape(B, S, D) * gamma
        static = (jax.nn.gelu(x_flat @ W1.T, approximate=False) @ W2.T).reshape(B, S, D)
        return static + dyn

    def _L1_attn_ref(x, Wq, bq, Wk, bk, Wv, bv, Wo, bo):
        import jax, jax.numpy as jnp
        import numpy as np
        from math import sqrt
        EMBED_DIM = 128
        NUM_HEADS = 16
        HEAD_DIM = EMBED_DIM // NUM_HEADS
        SCALE = sqrt(HEAD_DIM)

        def _rotate_half(x):
            x1 = x[..., 0::2]
            x2 = x[..., 1::2]
            return jnp.stack((-x2, x1), axis=-1).reshape(x.shape)

        def _apply_rope(x, seq_len):
            inv_freq = 1.0 / 10000.0 ** (jnp.arange(0, HEAD_DIM, 2, dtype=jnp.float32) / HEAD_DIM)
            pos = jnp.arange(seq_len, dtype=jnp.float32)
            freqs = jnp.outer(pos, inv_freq)
            emb = jnp.concatenate([freqs, freqs], -1)
            cos = jnp.cos(emb)[None, None].astype(x.dtype)
            sin = jnp.sin(emb)[None, None].astype(x.dtype)
            return x * cos + _rotate_half(x) * sin
        B, S, E = x.shape
        H, D = (NUM_HEADS, HEAD_DIM)
        q = (x @ Wq.T + bq).reshape(B, S, H, D).transpose(0, 2, 1, 3)
        k = (x @ Wk.T + bk).reshape(B, S, H, D).transpose(0, 2, 1, 3)
        v = (x @ Wv.T + bv).reshape(B, S, H, D).transpose(0, 2, 1, 3)
        q = _apply_rope(q, S)
        k = _apply_rope(k, S)
        attn = jnp.einsum('bhqd,bhkd->bhqk', q, k) / SCALE
        attn = jax.nn.softmax(attn, axis=-1)
        out = jnp.einsum('bhqk,bhkd->bhqd', attn, v)
        out = out.transpose(0, 2, 1, 3).reshape(B, S, E)
        return out @ Wo.T + bo

    def _L1_ffn_ref(x, w1, b1, w2, b2):
        import jax, jax.numpy as jnp
        import numpy as np
        N_EMBD = 128
        N_STATE = 512
        h = jax.nn.gelu(jnp.einsum('bse,eh->bsh', x, w1) + b1, approximate=False)
        return jnp.einsum('bsh,he->bse', h, w2) + b2

    def _L2_attn_ref(x, Wq, Wk, Wv, Wo):
        import jax, jax.numpy as jnp
        import numpy as np
        H, KV, DH = (16, 4, 64)

        def _rotate_half(t):
            t1, t2 = (t[..., :DH // 2], t[..., DH // 2:])
            return jnp.concatenate([-t2, t1], axis=-1)
        B, L, D = x.shape
        G = H // KV
        q = (x @ Wq).reshape(B, L, H, DH)
        k = (x @ Wk).reshape(B, L, KV, DH)
        v = (x @ Wv).reshape(B, L, KV, DH)
        inv_freq = 1.0 / 10000.0 ** (jnp.arange(0, DH, 2, dtype=jnp.float32) / DH)
        t = jnp.arange(L, dtype=jnp.float32)
        freqs = t[:, None] * inv_freq[None, :]
        emb = jnp.concatenate([freqs, freqs], axis=-1)[None, :, None, :]
        cos, sin = (jnp.cos(emb), jnp.sin(emb))
        q = q * cos + _rotate_half(q) * sin
        k = k * cos + _rotate_half(k) * sin
        qg = q.reshape(B, L, KV, G, DH)
        scale = DH ** (-0.5)
        attn = jnp.einsum('bqkgd,bskd->bkgqs', qg, k) * scale
        attn = jax.nn.softmax(attn, axis=-1)
        out = jnp.einsum('bkgqs,bskd->bqkgd', attn, v).reshape(B, L, H * DH)
        return out @ Wo

    def _L2_ffn_ref(x, gate_w, w1, b1, w2, b2, gamma, beta):
        import jax, jax.numpy as jnp
        import numpy as np
        B, L, D, H, E, TOP_K = (4, 256, 128, 512, 8, 2)
        LN_EPS = 1e-05
        residual = x
        mu = jnp.mean(x, axis=-1, keepdims=True)
        var = jnp.mean(jnp.square(x - mu), axis=-1, keepdims=True)
        xn = (x - mu) * jax.lax.rsqrt(var + LN_EPS) * gamma + beta
        probs = jax.nn.softmax(jnp.einsum('bld,de->ble', xn, gate_w), axis=-1)
        w, idx = jax.lax.top_k(probs, TOP_K)
        w = w / jnp.sum(w, axis=-1, keepdims=True)
        cw = jnp.sum(w[..., None] * jax.nn.one_hot(idx, E, dtype=x.dtype), axis=2)
        h = jax.nn.gelu(jnp.einsum('bld,edh->eblh', xn, w1) + b1[:, None, None, :], approximate=False)
        out_e = jnp.einsum('eblh,ehd->ebld', h, w2) + b2[:, None, None, :]
        output = jnp.einsum('ble,ebld->bld', cw, out_e)
        return output + residual

    def _L3_attn_ref(x, w_att_val, wv_w, wv_b, out_w, out_b):
        import jax, jax.numpy as jnp
        import numpy as np
        B, T, E, H = (2, 256, 128, 16)
        D = E // H
        b, t, e = x.shape
        h, d, _ = w_att_val.shape
        x_h = x.reshape(b, t, h, d).transpose(0, 2, 1, 3)
        xw = jnp.einsum('bhtd,hde->bhte', x_h, w_att_val)
        att = jnp.einsum('bhte,bhse->bhts', xw, x_h) / jnp.sqrt(jnp.asarray(d, x.dtype))
        att = jax.nn.softmax(att, axis=-1)
        vx = x @ wv_w.T + wv_b
        vx = vx.reshape(b, t, h, d).transpose(0, 2, 1, 3)
        o = jnp.einsum('bhts,bhsd->bhtd', att, vx)
        o = o.transpose(0, 2, 1, 3).reshape(b, t, e)
        return o @ out_w.T + out_b

    def _L3_ffn_ref(x, norm_scale, gate_w, gate_b, mlp1_w, mlp1_b, mlp2_w, mlp2_b):
        import jax, jax.numpy as jnp
        import numpy as np
        B, S, D = (1, 256, 128)
        I = 256
        E = 8
        K = 2
        LIMIT = 7.0
        ALPHA = 1.702
        EPS = 1e-05

        def _swiglu(h):
            x_glu = jnp.minimum(h[..., ::2], LIMIT)
            x_lin = jnp.clip(h[..., 1::2], -LIMIT, LIMIT)
            return x_glu * jax.nn.sigmoid(ALPHA * x_glu) * (x_lin + 1.0)

        def _moe(t, gate_w, gate_b, mlp1_w, mlp1_b, mlp2_w, mlp2_b):
            T = t.shape[0]
            logits = t @ gate_w + gate_b
            top_v, top_i = jax.lax.top_k(logits, K)
            probs = jax.nn.softmax(top_v, axis=-1)
            w = jnp.zeros((T, E), t.dtype).at[jnp.arange(T)[:, None], top_i].set(probs)

            def body(acc, ew):
                w1, b1, w2, b2, we = ew
                h = _swiglu(t @ w1 + b1)
                y = h @ w2 + b2
                return (acc + we[:, None] * y, None)
            acc0 = jnp.zeros((T, t.shape[1]), t.dtype)
            acc, _ = jax.lax.scan(body, acc0, (mlp1_w, mlp1_b, mlp2_w, mlp2_b, w.T))
            return acc
        Bx, Sx, Dx = x.shape
        ms = jnp.mean(x * x, axis=-1, keepdims=True)
        t = (x * jax.lax.rsqrt(ms + EPS) * norm_scale).reshape(Bx * Sx, Dx)
        y = _moe(t, gate_w, gate_b, mlp1_w, mlp1_b, mlp2_w, mlp2_b)
        return x + y.reshape(Bx, Sx, Dx)
    x = L0_attn_x
    x = x + _L0_attn_ref(_layernorm(x, axis=-1), L0_attn_Wq, L0_attn_bq, L0_attn_Wk, L0_attn_bk, L0_attn_Wv, L0_attn_bv, L0_attn_Wo, L0_attn_bo)
    x = x + _L0_ffn_ref(_layernorm(x, axis=-1), L0_ffn_W1, L0_ffn_W2, L0_ffn_ln_g, L0_ffn_ln_b, L0_ffn_router_W, L0_ffn_router_b, L0_ffn_raw_U, L0_ffn_raw_V, L0_ffn_gamma)
    x = x + _L1_attn_ref(_layernorm(x, axis=-1), L1_attn_Wq, L1_attn_bq, L1_attn_Wk, L1_attn_bk, L1_attn_Wv, L1_attn_bv, L1_attn_Wo, L1_attn_bo)
    x = x + _L1_ffn_ref(_layernorm(x, axis=-1), L1_ffn_w1, L1_ffn_b1, L1_ffn_w2, L1_ffn_b2)
    x = x + _L2_attn_ref(_layernorm(x, axis=-1), L2_attn_Wq, L2_attn_Wk, L2_attn_Wv, L2_attn_Wo)
    x = x + _L2_ffn_ref(_layernorm(x, axis=-1), L2_ffn_gate_w, L2_ffn_w1, L2_ffn_b1, L2_ffn_w2, L2_ffn_b2, L2_ffn_gamma, L2_ffn_beta)
    x = x + _L3_attn_ref(_layernorm(x, axis=-1), L3_attn_w_att_val, L3_attn_wv_w, L3_attn_wv_b, L3_attn_out_w, L3_attn_out_b)
    x = x + _L3_ffn_ref(_layernorm(x, axis=-1), L3_ffn_norm_scale, L3_ffn_gate_w, L3_ffn_gate_b, L3_ffn_mlp1_w, L3_ffn_mlp1_b, L3_ffn_mlp2_w, L3_ffn_mlp2_b)
    return x

_drawn_inputs = setup_inputs


def setup_inputs(seed=0):
    import zlib

    import numpy as np

    out = dict(_drawn_inputs(seed))
    spreads = {'L0_attn_bq': (0.0, 0.424),
     'L0_attn_bk': (0.0, 0.8),
     'L0_attn_bv': (0.0, 0.1),
     'L0_attn_bo': (0.0, 0.1),
     'L0_ffn_ln_g': (1.0, 0.6),
     'L0_ffn_ln_b': (0.0, 0.8),
     'L0_ffn_router_b': (0.0, 0.8),
     'L0_ffn_gamma': (0.10000000149011612, 0.6),
     'L1_attn_bq': (0.0, 0.8),
     'L1_attn_bk': (0.0, 0.8),
     'L1_attn_bv': (0.0, 0.1),
     'L1_attn_bo': (0.0, 0.1),
     'L2_ffn_b1': (0.0, 0.374),
     'L2_ffn_b2': (0.0, 0.1),
     'L2_ffn_gamma': (1.0, 0.2),
     'L2_ffn_beta': (0.0, 0.1),
     'L3_attn_wv_b': (0.0, 0.1),
     'L3_attn_out_b': (0.0, 0.1),
     'L3_ffn_norm_scale': (1.0, 0.6),
     'L3_ffn_gate_b': (0.0, 0.539),
     'L3_ffn_mlp1_b': (0.0, 0.8),
     'L3_ffn_mlp2_b': (0.0, 0.401)}
    factors = {'L0_ffn_router_W': 6.559,
     'L0_ffn_raw_U': 8.0,
     'L0_ffn_raw_V': 6.54,
     'L1_attn_Wq': 4.915,
     'L1_attn_Wk': 5.353,
     'L1_ffn_b1': 3.372,
     'L2_attn_Wq': 8.0,
     'L2_attn_Wk': 8.0,
     'L3_ffn_gate_w': 3.035,
     'L3_ffn_mlp1_w': 6.577,
     'L3_ffn_mlp2_w': 5.972}
    for name, (base, spread) in spreads.items():
        noise = np.random.default_rng([zlib.crc32(name.encode()), seed]).standard_normal(out[name].shape)
        drawn = base * np.exp(spread * noise) if base else spread * noise
        out[name] = jnp.asarray(drawn.astype(out[name].dtype))
    for name, factor in factors.items():
        out[name] = (out[name] * factor).astype(out[name].dtype)
    return out
```

```python
from contextlib import ExitStack

import numpy as np

import concourse.bass as bass
from concourse import mybir

ALU = mybir.AluOpType
ACT = mybir.ActivationFunctionType
AX = mybir.AxisListType
F32 = mybir.dt.float32
BF16 = mybir.dt.bfloat16

P = 128
S = 2048
H = 16
CW = 512
CH = S // CW
TT = S // P
LEAD = 6
FULL = TT - LEAD
TURN = FULL + 1


def stage_semaphores(nc, ctx, name):
    taken = []

    def clear():
        nc.clear_and_free_semaphores(taken)
        nc.all_engine_barrier()

    def sem(n):
        taken.append(nc.alloc_semaphore(f"{name}_{n}"))
        return taken[-1]

    ctx.callback(clear)
    return sem


class Shape:

    def __init__(self, scale, ident, group, groups, q_blocks, k_blocks, v_cols, v_dims, score_pairs, max_pairs,
                 max_block, max_row0, max_bank0, max_banks, out_bank0, out_banks, sum_bank, q_loads, k_loads,
                 o_stores):
        self.scale = scale
        self.ident = ident
        self.group = group
        self.groups = groups
        self.q_blocks = q_blocks
        self.k_blocks = k_blocks
        self.v_cols = v_cols
        self.v_dims = v_dims
        self.score_pairs = score_pairs
        self.max_pairs = max_pairs
        self.max_block = max_block
        self.max_row0 = max_row0
        self.max_bank0 = max_bank0
        self.max_banks = max_banks
        self.out_bank0 = out_bank0
        self.out_banks = out_banks
        self.sum_bank = sum_bank
        self.q_loads = q_loads
        self.k_loads = k_loads
        self.o_stores = o_stores


def attention_core(nc, psum, cfg, q_ring, k_res, k_ones, v_all, load_k, load_q, store_o, name):
    with ExitStack() as ctx:
        def sb(n, shape, dt):
            return ctx.enter_context(nc.sbuf_tensor(f"{name}_{n}", shape, dt))

        sem = stage_semaphores(nc, ctx, name)

        probs = sb("probs", [P, 2 * CH, CW], F32)
        v_head = sb("v_head", [P, TT, cfg.v_cols], F32)
        tile_max = sb("tile_max", [P, TT * CH], F32)
        neg_max = sb("neg_max", [P, TT], F32)
        max_row = sb("max_row", [TT, P], F32)
        max_rest = sb("max_rest", [TT, P], F32)
        max_rest2 = sb("max_rest2", [TT, P], F32)
        ones_row = sb("ones_row", [TT, P], F32)
        max_parts = sb("max_parts", [TT, 3, P], BF16)
        out_sb = sb("out_sb", [P, cfg.out_banks, CW], F32)
        ones_v = sb("ones_v", [P, 32], F32) if cfg.sum_bank is not None else None

        k_loaded = [sem(f"k_loaded{g}") for g in range(cfg.groups)]
        q_loaded = sem("q_loaded")
        scores_ready = sem("scores_ready")
        exp_done = sem("exp_done")
        pv_done = sem("pv_done")
        max_ready = sem("max_ready")
        max_taken = sem("max_taken")
        head_max = sem("head_max")
        max_turned = sem("max_turned")
        max_copied = sem("max_copied")
        split_step = sem("split_step")
        max_rows_in = sem("max_rows_in")
        v_zeroed = sem("v_zeroed")
        v_ready = sem("v_ready")
        out_copied = sem("out_copied")
        out_stored = sem("out_stored")

        MB = cfg.max_banks
        block = ctx.enter_context(nc.Block())

        def max_unit_of(h, kt):
            u = kt + LEAD
            return (1, u) if u < TT else (2, u - TT)

        @block.tensor
        def _(pe):
            def max_tile(hm, qt, c):
                n = hm * (TT * CH) + (CH * qt + c)
                if qt == 0 and c == 0:
                    pe.wait_ge(q_loaded, (hm + 1) * (16 * cfg.q_loads))
                if not (isinstance(n, int) and n < MB):
                    pe.wait_ge(max_taken, n - MB + 1)
                bank = psum[:, cfg.max_bank0 + c % MB, :]
                pairs = cfg.max_pairs
                for j, (qb, kb) in enumerate(pairs):
                    mm = nc.tensor.matmul(
                        bank, q_ring[:, bass.ds((hm % 4) * (cfg.q_blocks * S) + (qb * S + qt * P), P)],
                        k_res[:, bass.ds((hm // cfg.group) * (cfg.k_blocks * S) + (kb * S + c * CW), CW)],
                        start=j == 0, stop=j == len(pairs) - 1)
                mm.then_inc(max_ready, 1)

            def turn_max(hm, later_tiles):
                pe.wait_ge(head_max, hm + 1)
                pe.wait_ge(max_taken, (hm + 1) * (TT * CH) + later_tiles)
                nc.tensor.transpose(psum[0:TT, cfg.max_bank0, 0:P], neg_max[:, :],
                                    cfg.ident[:, :]).then_inc(max_turned, 1)

            def score_tile(h, kt, c):
                if kt == 0 and c == 0:
                    pe.wait_ge(max_rows_in, (h + 1) * 48)
                n = h * (TT * CH) + (CH * kt + c)
                if not (isinstance(n, int) and n < CH):
                    pe.wait_ge(exp_done, n - CH + 1)
                pairs = cfg.score_pairs
                for j, (qb, kb) in enumerate(pairs):
                    if kb is None:
                        w = k_ones[:, :]
                    else:
                        w = k_res[:, bass.ds((h // cfg.group) * (cfg.k_blocks * S) + (kb * S + kt * P), P)]
                    mm = nc.tensor.matmul(
                        psum[:, c, :], w,
                        q_ring[:, bass.ds((h % 4) * (cfg.q_blocks * S) + (qb * S + c * CW), CW)],
                        start=j == 0, stop=j == len(pairs) - 1)
                mm.then_inc(scores_ready, 1)

            def pv(h, kt):
                if kt == 0:
                    pe.wait_ge(v_ready, h + 1)
                    if not (isinstance(h, int) and h == 0):
                        pe.wait_ge(out_copied, h)
                pe.wait_ge(exp_done, h * (TT * CH) + CH * (kt + 1))
                w = cfg.v_cols
                if cfg.sum_bank is not None:
                    for c in range(CH):
                        nc.tensor.matmul(psum[32 * c:32 * c + 32, cfg.sum_bank, :], ones_v[:, :],
                                         probs[:, CH * (kt % 2) + c, :], start=kt == 0, stop=kt == TT - 1)
                for c in range(CH):
                    per = P // w
                    out = psum[w * (c % per):w * (c % per) + w, cfg.out_bank0 + c // per, :]
                    mm = nc.tensor.matmul(out, v_head[:, kt, :], probs[:, CH * (kt % 2) + c, :],
                                          start=kt == 0, stop=kt == TT - 1)
                mm.then_inc(pv_done, 1)

            def head(h, ahead, first=False):
                for kt in range(TT):
                    d, qt = max_unit_of(h, kt)
                    for c in range(CH):
                        score_tile(h, kt, c)
                        if d <= ahead:
                            max_tile(h + d, qt, c)
                    if kt == TURN and ahead >= 1:
                        turn_max(h + 1, CH * (TURN - FULL + 1) if ahead == 2 else 0)
                    if kt > 0:
                        pv(h, kt - 1)
                    elif not first:
                        pv(h - 1, TT - 1)
                    if kt == TURN and ahead >= 1:
                        pe.wait_ge(max_copied, h + 2)

            pe.wait_ge(k_loaded[0], 16 * cfg.k_loads)
            for qt in range(TT):
                for c in range(CH):
                    max_tile(0, qt, c)
            if cfg.groups > 1 and cfg.group == 1:
                pe.wait_ge(k_loaded[1], 16 * cfg.k_loads)
            for qt in range(LEAD):
                for c in range(CH):
                    max_tile(1, qt, c)
                if qt == TURN - FULL:
                    turn_max(0, CH * (TURN - FULL + 1))
                    pe.wait_ge(max_copied, 1)
            for g in range(1, cfg.groups):
                pe.wait_ge(k_loaded[g], 16 * cfg.k_loads)
            head(0, 2, first=True)
            with pe.Fori(1, H - 2) as h:
                head(h, 2)
            head(H - 2, 1)
            head(H - 1, 0)
            pv(H - 1, TT - 1)

        @block.scalar
        def _(act):
            def head(h):
                for kt in range(TT):
                    for c in range(CH):
                        act.wait_ge(scores_ready, h * (TT * CH) + (CH * kt + c + 1))
                        if c == 0 and not (isinstance(h, int) and h == 0 and kt < 2):
                            act.wait_ge(pv_done, h * TT + kt - 1)
                        nc.scalar.activation(probs[:, CH * (kt % 2) + c, :], psum[:, c, :], ACT.Exp,
                                             scale=cfg.scale).then_inc(exp_done, 1)

            head(0)
            with act.Fori(1, H) as h:
                head(h)

        @block.vector
        def _(dve):
            def take_max(hm, qt, c):
                n = hm * (TT * CH) + (CH * qt + c)
                dve.wait_ge(max_ready, n + 1)
                if qt == 0 and c == 0 and not (isinstance(hm, int) and hm == 0):
                    dve.wait_ge(head_max, hm)
                nc.vector.reduce_max(tile_max[:, CH * qt + c:CH * qt + c + 1],
                                     psum[:, cfg.max_bank0 + c % MB, :], AX.X).then_inc(max_taken, 1)
                if qt == TT - 1 and c == CH - 1:
                    dve.wait_ge(max_taken, n + 1)
                    if not (isinstance(hm, int) and hm == 0):
                        dve.wait_ge(max_turned, hm)
                    nc.vector.tensor_reduce(
                        neg_max[:, :], tile_max[:, :].rearrange("p (t c) -> p t c", c=CH),
                        AX.X, ALU.max, negate=True).then_inc(head_max, 1)

            def copy_row(hm):
                dve.wait_ge(max_turned, hm + 1)
                if not (isinstance(hm, int) and hm == 0):
                    dve.wait_ge(split_step, hm * 5)
                nc.vector.tensor_copy(max_row[:, :], psum[0:TT, cfg.max_bank0, 0:P]).then_inc(max_copied, 1)

            def copy_out(h):
                dve.wait_ge(pv_done, (h + 1) * TT)
                if not (isinstance(h, int) and h == 0):
                    dve.wait_ge(out_stored, h * (16 * cfg.o_stores))
                nc.vector.tensor_copy(out_sb[:, :, :], psum[:, cfg.out_bank0:cfg.out_bank0 + cfg.out_banks, :]
                                      ).then_inc(out_copied, 1)

            def head(h, ahead, first=False):
                for kt in range(TT):
                    d, qt = max_unit_of(h, kt)
                    if d <= ahead:
                        for c in range(CH):
                            take_max(h + d, qt, c)
                    if kt == TURN and ahead >= 1:
                        copy_row(h + 1)
                    if kt == 0 and not first:
                        copy_out(h - 1)

            for qt in range(TT):
                for c in range(CH):
                    take_max(0, qt, c)
            for qt in range(LEAD):
                for c in range(CH):
                    take_max(1, qt, c)
                if qt == TURN - FULL:
                    copy_row(0)
            head(0, 2, first=True)
            with dve.Fori(1, H - 2) as h:
                head(h, 2)
            head(H - 2, 1)
            head(H - 1, 0)
            copy_out(H - 1)

        @block.gpsimd
        def _(pool):
            nc.gpsimd.memset(v_head[:, :, :], 0.0).then_inc(v_zeroed, 1)
            if ones_v is not None:
                nc.gpsimd.memset(ones_v[:, :], 1.0).then_inc(v_zeroed, 1)
            else:
                pool.wait_ge(v_zeroed, 1)
                nc.gpsimd.memset(v_head[:, :, cfg.v_dims:cfg.v_dims + 1], 1.0).then_inc(v_zeroed, 1)
            nc.gpsimd.memset(ones_row[:, :], 1.0).then_inc(v_zeroed, 1)
            pool.wait_ge(v_zeroed, 3)

            def fill_v(h):
                if not (isinstance(h, int) and h == 0):
                    pool.wait_ge(pv_done, h * TT)
                nc.gpsimd.tensor_copy(v_head[:, :, 0:cfg.v_dims],
                                      v_all[:, :, bass.ds((h // cfg.group) * cfg.v_dims, cfg.v_dims)]
                                      ).then_inc(v_ready, 1)

            def split_max(hm):
                k = hm * 5
                pool.wait_ge(max_copied, hm + 1)
                if not (isinstance(hm, int) and hm == 0):
                    pool.wait_ge(max_rows_in, hm * 48)
                nc.gpsimd.tensor_tensor(max_parts[:, 0, :], max_row[:, :], ones_row[:, :],
                                        ALU.mult).then_inc(split_step, 1)
                pool.wait_ge(split_step, k + 1)
                nc.gpsimd.tensor_tensor(max_rest[:, :], max_row[:, :], max_parts[:, 0, :],
                                        ALU.subtract).then_inc(split_step, 1)
                pool.wait_ge(split_step, k + 2)
                nc.gpsimd.tensor_tensor(max_parts[:, 1, :], max_rest[:, :], ones_row[:, :],
                                        ALU.mult).then_inc(split_step, 1)
                pool.wait_ge(split_step, k + 3)
                nc.gpsimd.tensor_tensor(max_rest2[:, :], max_rest[:, :], max_parts[:, 1, :],
                                        ALU.subtract).then_inc(split_step, 1)
                pool.wait_ge(split_step, k + 4)
                nc.gpsimd.tensor_tensor(max_parts[:, 2, :], max_rest2[:, :], ones_row[:, :],
                                        ALU.mult).then_inc(split_step, 1)

            fill_v(0)
            split_max(0)
            split_max(1)
            with pool.Fori(1, H - 1) as h:
                fill_v(h)
                split_max(h + 1)
            fill_v(H - 1)

        @block.sync
        def _(sp):
            def put_max_rows(hm):
                sp.wait_ge(split_step, (hm + 1) * 5)
                for j in range(3):
                    dst = q_ring[cfg.max_row0 + j:cfg.max_row0 + j + 1,
                                 bass.ds((hm % 4) * (cfg.q_blocks * S) + cfg.max_block * S, S)]
                    sp.dma_start(dst, max_parts[:, j, :]).then_inc(max_rows_in, 16)

            def q_in(h):
                if not (isinstance(h, int) and h < 4):
                    sp.wait_ge(exp_done, (h - 3) * (TT * CH))
                if not (isinstance(h, int) and h == 0):
                    sp.wait_ge(q_loaded, h * (16 * cfg.q_loads))
                load_q(sp, h, q_loaded)

            def put_out(h):
                sp.wait_ge(out_copied, h + 1)
                store_o(sp, h, out_sb, out_stored)

            for g in range(cfg.groups):
                load_k(sp, g, k_loaded[g])
                if g < 4:
                    q_in(g)
            put_max_rows(0)
            put_max_rows(1)
            with sp.Fori(1, H - 3) as h:
                q_in(h + 3)
                put_out(h - 1)
                put_max_rows(h + 1)
            for h in range(H - 3, H - 1):
                put_out(h - 1)
                put_max_rows(h + 1)
            put_out(H - 2)
            put_out(H - 1)
            sp.wait_ge(out_stored, H * 16 * cfg.o_stores)


def attend(nc, psum, ident, v_all, q_dram, k_dram, o_dram, kind, scale, name):
    wide = kind == "wide"
    d = 64 if wide else 8
    q_blocks, k_blocks = (4, 2) if wide else (1, 1)
    group = 4 if wide else 1
    with ExitStack() as ctx:
        sem = stage_semaphores(nc, ctx, name + "_set")
        q_ring = ctx.enter_context(nc.sbuf_tensor(f"q_ring_{name}", [P, 4 * q_blocks * S], BF16))
        k_res = ctx.enter_context(nc.sbuf_tensor(f"k_res_{name}", [P, H // group * k_blocks * S], BF16))
        k_ones = ctx.enter_context(nc.sbuf_tensor(f"k_ones_{name}", [P, P], BF16))
        k_cleared = sem("k_cleared")
        ones_cleared = sem("ones_cleared")
        with nc.Block() as block:
            @block.gpsimd
            def _(pool):
                if not wide:
                    nc.gpsimd.memset(k_res[:, :].bitcast(F32), 0.0).then_inc(k_cleared, 1)
                    pool.wait_ge(k_cleared, 1)
                    nc.gpsimd.memset(k_res[32:64, :], 1.0)

            @block.vector
            def _(dve):
                nc.vector.memset(q_ring[:, :].bitcast(F32), 0.0)
                nc.vector.memset(k_ones[:, :], 0.0).then_inc(ones_cleared, 1)
                dve.wait_ge(ones_cleared, 1)
                nc.vector.memset(k_ones[0:32, :], 1.0)
        if wide:
            cfg = Shape(
                scale=scale, ident=ident, group=group, groups=4, q_blocks=4, k_blocks=2, v_cols=64, v_dims=64,
                score_pairs=[(0, 0), (1, 0), (2, 1), (3, None)], max_pairs=[(0, 0), (1, 0)],
                max_block=3, max_row0=0, max_bank0=4, max_banks=1, out_bank0=5, out_banks=3, sum_bank=7,
                q_loads=3, k_loads=3, o_stores=5)

            def load_q(sp, h, loaded):
                at = (h % 4) * (4 * S)
                rows = bass.ds(h * 64, 64)
                sp.dma_start(q_ring[:, bass.ds(at, S)],
                             q_dram[0:1, rows, :].broadcast_to([2, 64, S])).then_inc(loaded, 16)
                sp.dma_start(q_ring[:, bass.ds(at + S, S)],
                             q_dram[1:2, rows, :].broadcast_to([2, 64, S])).then_inc(loaded, 16)
                sp.dma_start(q_ring[:, bass.ds(at + 2 * S, S)], q_dram[0:3:2, rows, :]).then_inc(loaded, 16)

            def load_k(sp, g, loaded):
                at = g * 2 * S
                rows = slice(g * 64, g * 64 + 64)
                sp.dma_start(k_res[:, at:at + S], k_dram[0:2, rows, :]).then_inc(loaded, 16)
                sp.dma_start(k_res[0:64, at + S:at + 2 * S], k_dram[2, rows, :]).then_inc(loaded, 16)
                sp.dma_start(k_res[64:128, at + S:at + 2 * S], k_dram[0, rows, :]).then_inc(loaded, 16)

            def store_o(sp, h, out_sb, stored):
                for c in range(CH):
                    sp.dma_start(o_dram[bass.ds(h, 1), 0:64, c * CW:(c + 1) * CW],
                                 out_sb[64 * (c % 2):64 * (c % 2) + 64, c // 2, :]).then_inc(stored, 16)
                sp.dma_start(o_dram[bass.ds(h, 1), 64, :], out_sb[0:128:32, 2, :]).then_inc(stored, 16)
        else:
            cfg = Shape(
                scale=scale, ident=ident, group=1, groups=H, q_blocks=1, k_blocks=1, v_cols=32, v_dims=8,
                score_pairs=[(0, 0)], max_pairs=[(0, 0)], max_block=0, max_row0=48,
                max_bank0=4, max_banks=2, out_bank0=6, out_banks=1, sum_bank=None,
                q_loads=4, k_loads=3, o_stores=4)

            def load_q(sp, h, loaded):
                at = (h % 4) * S
                rows = bass.ds(h * 8, 8)
                for part, n, r in ((0, 3, 0), (1, 2, 24), (2, 1, 40)):
                    sp.dma_start(q_ring[r:r + 8 * n, bass.ds(at, S)],
                                 q_dram[part:part + 1, rows, :].broadcast_to([n, 8, S])).then_inc(loaded, 16)
                sp.dma_start(q_ring[48:51, bass.ds(at, S)], q_ring[64:67, bass.ds(at, S)]).then_inc(loaded, 16)

            def load_k(sp, h, loaded):
                rows = slice(h * 8, h * 8 + 8)
                for n, r in ((3, 0), (2, 24), (1, 40)):
                    sp.dma_start(k_res[r:r + 8 * n, h * S:(h + 1) * S],
                                 k_dram[0:n, rows, :]).then_inc(loaded, 16)

            def store_o(sp, h, out_sb, stored):
                for c in range(CH):
                    sp.dma_start(o_dram[bass.ds(h, 1), :, c * CW:(c + 1) * CW],
                                 out_sb[32 * c:32 * c + 9, 0, :]).then_inc(stored, 16)
        attention_core(nc, psum, cfg, q_ring, k_res, k_ones, v_all, load_k, load_q, store_o, name)


def after(eng, sem, value):
    if not (isinstance(value, int) and value <= 0):
        eng.wait_ge(sem, value)


def normalise(nc, psum, name, src, dst, mean_w, eps, centre=True, gain=None, shift=None):
    with ExitStack() as ctx:
        def sb(n, shape, dt=F32):
            return ctx.enter_context(nc.sbuf_tensor(f"{name}_{n}", shape, dt))

        sem = stage_semaphores(nc, ctx, name)

        centred = sb("centred", [P, S]) if centre else src
        squares = sb("squares", [P, S])
        spread = sb("spread", [P, S])
        scale = sb("scale", [P, S])
        eps_col = sb("eps_col", [P, 1])
        affine = sb("affine", [P, 2])
        unit = sb("unit", [P, S]) if gain is not None else dst
        affine_in = sem("affine_in")
        eps_set = sem("eps_set")
        mean_ready = sem("mean_ready")
        centred_ready = sem("centred_ready")
        squares_ready = sem("squares_ready")
        var_ready = sem("var_ready")
        spread_ready = sem("spread_ready")
        scale_ready = sem("scale_ready")
        unit_ready = sem("unit_ready")
        block = ctx.enter_context(nc.Block())

        def part(t, c):
            return t[:, c * CW:(c + 1) * CW]

        @block.sync
        def _(sp):
            if gain is not None:
                sp.dma_start(affine[:, 0:1], gain).then_inc(affine_in, 16)
                if shift is not None:
                    sp.dma_start(affine[:, 1:2], shift).then_inc(affine_in, 16)

        @block.tensor
        def _(pe):
            if centre:
                for c in range(CH):
                    nc.tensor.matmul(psum[:, c, :], mean_w[:, :], part(src, c), start=True,
                                     stop=True).then_inc(mean_ready, 1)
            for c in range(CH):
                pe.wait_ge(squares_ready, c + 1)
                nc.tensor.matmul(psum[:, CH + c, :], mean_w[:, :], part(squares, c), start=True,
                                 stop=True).then_inc(var_ready, 1)

        @block.scalar
        def _(act):
            for c in range(CH):
                if centre:
                    act.wait_ge(centred_ready, c + 1)
                nc.scalar.activation(part(squares, c), part(centred, c), ACT.Square).then_inc(squares_ready, 1)
            act.wait_ge(eps_set, 1)
            for c in range(CH):
                act.wait_ge(var_ready, c + 1)
                nc.scalar.activation(part(spread, c), psum[:, CH + c, :], ACT.Sqrt,
                                     bias=eps_col[:, :]).then_inc(spread_ready, 1)

        @block.vector
        def _(dve):
            nc.vector.memset(eps_col[:, :], eps).then_inc(eps_set, 1)
            if centre:
                for c in range(CH):
                    dve.wait_ge(mean_ready, c + 1)
                    nc.vector.tensor_tensor(part(centred, c), part(src, c), psum[:, c, :],
                                            ALU.subtract).then_inc(centred_ready, 1)
            for c in range(CH):
                dve.wait_ge(spread_ready, c + 1)
                nc.vector.reciprocal(part(scale, c), part(spread, c)).then_inc(scale_ready, 1)

        @block.gpsimd
        def _(pool):
            if gain is not None:
                pool.wait_ge(affine_in, 16 if shift is None else 32)
            for c in range(CH):
                pool.wait_ge(scale_ready, c + 1)
                nc.gpsimd.tensor_tensor(part(unit, c), part(centred, c), part(scale, c),
                                        ALU.mult).then_inc(unit_ready, 1)
                if gain is not None:
                    pool.wait_ge(unit_ready, c + 1)
                    if shift is not None:
                        nc.gpsimd.tensor_scalar(part(dst, c), part(unit, c), affine[:, 0:1], affine[:, 1:2],
                                                ALU.mult, ALU.add)
                    else:
                        nc.gpsimd.tensor_scalar(part(dst, c), part(unit, c), affine[:, 0:1], None, ALU.mult)


def project(nc, psum, name, xn, jobs, rope):
    J = len(jobs)
    assert J % 2 == 0
    with ExitStack() as ctx:
        def sb(n, shape, dt=F32):
            return ctx.enter_context(nc.sbuf_tensor(f"{name}_{n}", shape, dt))

        sem = stage_semaphores(nc, ctx, name)

        w = sb("w", [P, J, P])
        b = sb("b", [P, J])
        w_in = sem("w_in")
        if rope is not None:
            w_turned = sb("w_turned", [P, J, P])
            b_turned = sb("b_turned", [P, J])
            cos = sb("cos", [P, S])
            sin = sb("sin", [P, S])
            by_cos = sb("by_cos", [P, 2, CW])
            by_sin = sb("by_sin", [P, 2, CW])
        value = sb("value", [P, 2, CW])
        rest = sb("rest", [P, 2, CW])
        parts = sb("parts", [P, 2, 3, CW], BF16)
        proj_ready = sem("proj_ready")
        turned_done = sem("turned_done")
        value_ready = sem("value_ready")
        high_ready = sem("high_ready")
        rest_ready = sem("rest_ready")
        mid_ready = sem("mid_ready")
        low_ready = sem("low_ready")
        stored = [sem("stored0"), sem("stored1")]
        block = ctx.enter_context(nc.Block())

        def over_chunks(eng, body):
            body(0)
            with eng.Fori(1, CH) as c:
                body(c)

        loads = [(w[:, j, :], jobs[j][0]) for j in range(J)] + [(b[:, j:j + 1], jobs[j][1]) for j in range(J)]
        if rope is not None:
            loads += [(w_turned[:, j, :], jobs[j][2]) for j in range(J)]
            loads += [(b_turned[:, j:j + 1], jobs[j][3]) for j in range(J)]
            loads += [(cos[:, :], rope[0]), (sin[:, :], rope[1])]

        @block.sync
        def _(sp):
            for dst, src in loads:
                sp.dma_start(dst, src).then_inc(w_in, 16)

            def store(c):
                for j in range(J):
                    sp.wait_ge(low_ready, c * J + (j + 1))
                    sp.dma_start(jobs[j][4][:, :, bass.ds(c * CW, CW)].rearrange("n p w -> p n w"),
                                 parts[:, j % 2, :, :]).then_inc(stored[j % 2], 16)
            over_chunks(sp, store)
            for k in range(2):
                sp.wait_ge(stored[k], 16 * CH * J // 2)

        @block.tensor
        def _(pe):
            pe.wait_ge(w_in, 16 * len(loads))

            def chunk(c):
                for j in range(J):
                    after(pe, turned_done if rope is not None else value_ready, c * J + (j - 1))
                    x_c = xn[:, bass.ds(c * CW, CW)]
                    mm = nc.tensor.matmul(psum[:, j % 2, :], w[:, j, :], x_c, start=True, stop=True)
                    if rope is not None:
                        mm = nc.tensor.matmul(psum[:, 2 + j % 2, :], w_turned[:, j, :], x_c, start=True, stop=True)
                    mm.then_inc(proj_ready, 1)
            over_chunks(pe, chunk)

        @block.scalar
        def _(act):
            act.wait_ge(w_in, 16 * len(loads))

            def chunk(c):
                for j in range(J):
                    k = j % 2
                    u = c * J + j
                    if rope is None:
                        act.wait_ge(proj_ready, u + 1)
                        after(act, rest_ready, u - 1)
                        nc.scalar.activation(value[:, k, :], psum[:, k, :], ACT.Identity,
                                             bias=b[:, j:j + 1]).then_inc(value_ready, 1)
                    act.wait_ge(value_ready, u + 1)
                    after(act, stored[k], c * (16 * J // 2) + 16 * (j // 2))
                    nc.scalar.copy(parts[:, k, 0, :], value[:, k, :]).then_inc(high_ready, 1)
                    act.wait_ge(rest_ready, u + 1)
                    nc.scalar.copy(parts[:, k, 1, :], rest[:, k, :]).then_inc(mid_ready, 1)
            over_chunks(act, chunk)

        @block.vector
        def _(dve):
            dve.wait_ge(w_in, 16 * len(loads))

            def chunk(c):
                for j in range(J):
                    k = j % 2
                    u = c * J + j
                    if rope is not None:
                        dve.wait_ge(proj_ready, u + 1)
                        after(dve, value_ready, u - 1)
                        at = bass.ds(c * CW, CW)
                        nc.vector.scalar_tensor_tensor(by_cos[:, k, :], psum[:, k, :], b[:, j:j + 1], cos[:, at],
                                                       ALU.add, ALU.mult)
                        nc.vector.scalar_tensor_tensor(by_sin[:, k, :], psum[:, 2 + k, :], b_turned[:, j:j + 1],
                                                       sin[:, at], ALU.add, ALU.mult).then_inc(turned_done, 1)
                    dve.wait_ge(mid_ready, u + 1)
                    nc.vector.tensor_tensor(parts[:, k, 2, :], rest[:, k, :], parts[:, k, 1, :],
                                            ALU.subtract).then_inc(low_ready, 1)
            over_chunks(dve, chunk)

        @block.gpsimd
        def _(pool):
            def chunk(c):
                for j in range(J):
                    k = j % 2
                    u = c * J + j
                    if rope is not None:
                        pool.wait_ge(turned_done, u + 1)
                        after(pool, rest_ready, u - 1)
                        nc.gpsimd.tensor_tensor(value[:, k, :], by_cos[:, k, :], by_sin[:, k, :],
                                                ALU.add).then_inc(value_ready, 1)
                    pool.wait_ge(high_ready, u + 1)
                    after(pool, low_ready, u - 1)
                    nc.gpsimd.tensor_tensor(rest[:, k, :], value[:, k, :], parts[:, k, 0, :],
                                            ALU.subtract).then_inc(rest_ready, 1)
            over_chunks(pool, chunk)


def values(nc, psum, name, xn, w_dram, b_dram, v_all, width):
    with ExitStack() as ctx:
        w = ctx.enter_context(nc.sbuf_tensor(f"{name}_w", [P, width], F32))
        b = ctx.enter_context(nc.sbuf_tensor(f"{name}_b", [P, width], F32))
        sem = stage_semaphores(nc, ctx, name)
        w_in = sem("w_in")
        v_ready = sem("v_ready")
        v_taken = sem("v_taken")
        block = ctx.enter_context(nc.Block())
        n_loads = 1 if b_dram is None else 2

        @block.sync
        def _(sp):
            sp.dma_start(w[:, :], w_dram).then_inc(w_in, 16)
            if b_dram is not None:
                sp.dma_start(b[:, :], b_dram.partition_broadcast(P)).then_inc(w_in, 16)

        @block.tensor
        def _(pe):
            pe.wait_ge(w_in, 16 * n_loads)
            for t in range(TT):
                after(pe, v_taken, t - 7)
                nc.tensor.matmul(psum[:, t % 8, 0:width], xn[:, t * P:(t + 1) * P], w[:, :], start=True,
                                 stop=True).then_inc(v_ready, 1)

        @block.vector
        def _(dve):
            dve.wait_ge(w_in, 16 * n_loads)
            for t in range(TT):
                dve.wait_ge(v_ready, t + 1)
                if b_dram is None:
                    ins = nc.vector.tensor_copy(v_all[:, t, :], psum[:, t % 8, 0:width])
                else:
                    ins = nc.vector.tensor_tensor(v_all[:, t, :], psum[:, t % 8, 0:width], b[:, :], ALU.add)
                ins.then_inc(v_taken, 1)


def project_out(nc, psum, name, o_dram, d, w_dram, b_dram, spread_dram, x):
    groups = H * d // P
    per = P // d
    with ExitStack() as ctx:
        def sb(n, shape, dt=F32):
            return ctx.enter_context(nc.sbuf_tensor(f"{name}_{n}", shape, dt))

        sem = stage_semaphores(nc, ctx, name)

        w = sb("w", [P, groups, P])
        b = sb("b", [P, 1])
        spread = sb("spread", [H, groups * P])
        sums = sb("sums", [H, S])
        inverse = sb("inverse", [H, S])
        o = sb("o", [P, groups, S])
        o_unit = sb("o_unit", [P, 2, CW])
        consts_in = sem("consts_in")
        o_in = [sem(f"o_in{g}") for g in range(groups)]
        inverse_ready = sem("inverse_ready")
        spread_ready = sem("spread_ready")
        o_ready = sem("o_ready")
        y_part = sem("y_part")
        y_ready = sem("y_ready")
        x_ready = sem("x_ready")
        n_loads = 3 + (b_dram is not None)
        block = ctx.enter_context(nc.Block())

        @block.sync
        def _(sp):
            sp.dma_start(sums[:, :], o_dram[:, d, :]).then_inc(consts_in, 16)
            sp.dma_start(spread[:, :], spread_dram).then_inc(consts_in, 16)
            sp.dma_start(w[:, :, :], w_dram).then_inc(consts_in, 16)
            if b_dram is not None:
                sp.dma_start(b[:, :], b_dram).then_inc(consts_in, 16)
            for g in range(groups):
                sp.dma_start(o[:, g, :], o_dram[g * per:(g + 1) * per, 0:d, :]).then_inc(o_in[g], 16)

        @block.tensor
        def _(pe):
            pe.wait_ge(inverse_ready, 1)
            units = [(c, g) for c in range(CH) for g in range(groups)]

            def spread_sums(n):
                c, g = units[n]
                after(pe, o_ready, n - 1)
                nc.tensor.matmul(psum[:, n % 2, :], spread[:, g * P:(g + 1) * P],
                                 inverse[:, c * CW:(c + 1) * CW], start=True, stop=True).then_inc(spread_ready, 1)

            def out(n):
                c, g = units[n]
                pe.wait_ge(o_ready, n + 1)
                mm = nc.tensor.matmul(psum[:, CH + c, :], w[:, g, :], o_unit[:, n % 2, :],
                                      start=g == 0, stop=g == groups - 1)
                mm.then_inc(y_part, 1)
                if g == groups - 1:
                    return

            spread_sums(0)
            for n in range(len(units)):
                if n + 1 < len(units):
                    spread_sums(n + 1)
                out(n)

        @block.vector
        def _(dve):
            dve.wait_ge(consts_in, 16 * n_loads)
            if b_dram is None:
                nc.vector.memset(b[:, :], 0.0).then_inc(y_ready, 1)
            nc.vector.reciprocal(inverse[:, :], sums[:, :]).then_inc(inverse_ready, 1)
            n = 0
            for c in range(CH):
                for g in range(groups):
                    dve.wait_ge(o_in[g], 16)
                    dve.wait_ge(spread_ready, n + 1)
                    after(dve, y_part, n - 1)
                    nc.vector.tensor_tensor(o_unit[:, n % 2, :], o[:, g, c * CW:(c + 1) * CW], psum[:, n % 2, :],
                                            ALU.mult).then_inc(o_ready, 1)
                    n += 1
            if b_dram is None:
                dve.wait_ge(y_ready, 1)
            for c in range(CH):
                dve.wait_ge(y_part, groups * (c + 1))
                at = slice(c * CW, (c + 1) * CW)
                nc.vector.scalar_tensor_tensor(x[:, at], psum[:, CH + c, :], b[:, 0:1], x[:, at],
                                               ALU.add, ALU.add).then_inc(x_ready, 1)


def mlp(nc, psum, name, xn, w1_dram, b1_dram, w2_dram, b2_dram, x):
    HB = 4
    with ExitStack() as ctx:
        def sb(n, shape, dt=F32):
            return ctx.enter_context(nc.sbuf_tensor(f"{name}_{n}", shape, dt))

        sem = stage_semaphores(nc, ctx, name)

        w1 = sb("w1", [P, HB * P])
        w2 = sb("w2", [P, HB, P])
        b1 = sb("b1", [P, HB])
        b2 = sb("b2", [P, 1])
        hidden = sb("hidden", [P, HB, CW])
        w_in = sem("w_in")
        b_clear = sem("b_clear")
        h_ready = sem("h_ready")
        h_done = sem("h_done")
        y_ready = sem("y_ready")
        y_part = sem("y_part")
        x_ready = sem("x_ready")
        loads = [(w1[:, :], w1_dram), (w2[:, :, :], w2_dram)]
        if b1_dram is not None:
            loads += [(b1[:, :], b1_dram), (b2[:, :], b2_dram)]
        block = ctx.enter_context(nc.Block())

        @block.sync
        def _(sp):
            for dst, src in loads:
                sp.dma_start(dst, src).then_inc(w_in, 16)

        @block.tensor
        def _(pe):
            pe.wait_ge(w_in, 16 * len(loads))
            units = [(c, j) for c in range(CH) for j in range(HB)]

            def out(n):
                c, j = units[n]
                pe.wait_ge(h_done, n + 1)
                nc.tensor.matmul(psum[:, CH + c, :], w2[:, j, :], hidden[:, j, :], start=j == 0,
                                 stop=j == HB - 1).then_inc(y_part, 1)

            for n, (c, j) in enumerate(units):
                after(pe, h_done, n - 1)
                nc.tensor.matmul(psum[:, n % 2, :], w1[:, j * P:(j + 1) * P], xn[:, c * CW:(c + 1) * CW],
                                 start=True, stop=True).then_inc(h_ready, 1)
                if n:
                    out(n - 1)
            out(len(units) - 1)

        @block.scalar
        def _(act):
            act.wait_ge(w_in, 16 * len(loads))
            if b1_dram is None:
                act.wait_ge(b_clear, 1)
            n = 0
            for c in range(CH):
                for j in range(HB):
                    act.wait_ge(h_ready, n + 1)
                    after(act, y_part, n - HB + 1)
                    nc.scalar.activation(hidden[:, j, :], psum[:, n % 2, :], ACT.Gelu,
                                         bias=b1[:, j:j + 1]).then_inc(h_done, 1)
                    n += 1

        @block.vector
        def _(dve):
            dve.wait_ge(w_in, 16 * len(loads))
            if b1_dram is None:
                nc.vector.memset(b2[:, :], 0.0).then_inc(y_ready, 1)
                nc.vector.memset(b1[:, :], 0.0).then_inc(b_clear, 1)
                dve.wait_ge(y_ready, 1)
            for c in range(CH):
                dve.wait_ge(y_part, HB * (c + 1))
                at = slice(c * CW, (c + 1) * CW)
                nc.vector.scalar_tensor_tensor(x[:, at], psum[:, CH + c, :], b2[:, 0:1], x[:, at],
                                               ALU.add, ALU.add).then_inc(x_ready, 1)


def route(nc, psum, name, t, w_dram, b_dram, E, gates_t, ident, kind):
    with ExitStack() as ctx:
        def sb(n, shape, dt=F32):
            return ctx.enter_context(nc.sbuf_tensor(f"{name}_{n}", shape, dt))

        sem = stage_semaphores(nc, ctx, name)

        w = sb("w", [P, E])
        b = sb("b", [P, E])
        logits = sb("logits", [P, TT, E])
        gates = sb("gates", [P, TT, E])
        top = sb("top", [P, TT, 8])
        t1 = sb("t1", [P, TT, E])
        t2 = sb("t2", [P, TT, E])
        t3 = sb("t3", [P, TT, E])
        col = sb("col", [P, TT])
        col2 = sb("col2", [P, TT])
        col3 = sb("col3", [P, TT])
        index = sb("index", [P, TT, 8], mybir.dt.uint32)
        index_f = sb("index_f", [P, TT, 8])
        expert = sb("expert", [P, E])
        w_in = sem("w_in")
        expert_ready = sem("expert_ready")
        logit_ready = sem("logit_ready")
        logit_taken = sem("logit_taken")
        step = sem("step")
        act_in = sem("act_in")
        act_out = sem("act_out")
        gates_ready = sem("gates_ready")
        turned = sem("turned")
        turned_out = sem("turned_out")
        n_loads = 1 + (b_dram is not None)
        block = ctx.enter_context(nc.Block())

        @block.sync
        def _(sp):
            sp.dma_start(w[:, :], w_dram).then_inc(w_in, 16)
            if b_dram is not None:
                sp.dma_start(b[:, :], b_dram.partition_broadcast(P)).then_inc(w_in, 16)

        @block.gpsimd
        def _(pool):
            nc.gpsimd.iota(expert[:, :], pattern=[[1, E]], base=0, channel_multiplier=0,
                           allow_small_or_imprecise_dtypes=True).then_inc(expert_ready, 1)

        @block.tensor
        def _(pe):
            pe.wait_ge(w_in, 16 * n_loads)
            for i in range(TT):
                after(pe, logit_taken, i - 3)
                nc.tensor.matmul(psum[:, i % 4, 0:E], t[:, i * P:(i + 1) * P], w[:, :], start=True,
                                 stop=True).then_inc(logit_ready, 1)
            pe.wait_ge(gates_ready, 1)
            for i in range(TT):
                nc.tensor.transpose(psum[0:E, 4 + i // 4, (i % 4) * P:(i % 4 + 1) * P], gates[:, i, :],
                                    ident[:, :]).then_inc(turned, 1)

        @block.vector
        def _(dve):
            count = [0]

            def link(ins):
                count[0] += 1
                ins.then_inc(step, 1)
                dve.wait_ge(step, count[0])

            dve.wait_ge(w_in, 16 * n_loads)
            for i in range(TT):
                dve.wait_ge(logit_ready, i + 1)
                if b_dram is None:
                    ins = nc.vector.tensor_copy(logits[:, i, :], psum[:, i % 4, 0:E])
                else:
                    ins = nc.vector.tensor_tensor(logits[:, i, :], psum[:, i % 4, 0:E], b[:, :], ALU.add)
                ins.then_inc(logit_taken, 1)
            dve.wait_ge(logit_taken, TT)
            full = [P, TT, E]
            if kind == "latent":
                link(nc.vector.tensor_scalar(t1[:, :, :], logits[:, :, :], 10.0, -10.0, ALU.min, ALU.max))
                link(nc.vector.tensor_scalar(t2[:, :, :], t1[:, :, :], -1.0, None, ALU.mult))
                nc.vector.tensor_tensor(t3[:, :, :], t1[:, :, :], t2[:, :, :], ALU.min).then_inc(act_in, 1)
                dve.wait_ge(act_out, 1)
                link(nc.vector.tensor_scalar(t3[:, :, :], t2[:, :, :], 1.0, None, ALU.add))
                nc.vector.tensor_scalar(logits[:, :, :], t3[:, :, :], -1.0, None, ALU.add).then_inc(act_in, 1)
                dve.wait_ge(act_in, 2)
                link(nc.vector.reciprocal(gates[:, :, :], logits[:, :, :]))
                link(nc.vector.tensor_tensor(logits[:, :, :], t2[:, :, :], gates[:, :, :], ALU.mult))
                dve.wait_ge(act_out, 2)
                link(nc.vector.tensor_tensor(t2[:, :, :], logits[:, :, :], t3[:, :, :], ALU.mult))
                link(nc.vector.tensor_scalar(t3[:, :, :], t1[:, :, :], 0.0, None, ALU.max))
                link(nc.vector.tensor_tensor(t1[:, :, :], t3[:, :, :], t2[:, :, :], ALU.add))
                for i in range(TT):
                    last = nc.vector.max(top[:, i, :], t1[:, i, :])
                link(last)
                for i in range(TT):
                    last = nc.vector.match_replace(t2[:, i, :], top[:, i, :], t1[:, i, :], -1.0)
                link(last)
                link(nc.vector.tensor_tensor(t3[:, :, :], t1[:, :, :], t2[:, :, :], ALU.not_equal))
                link(nc.vector.tensor_tensor(t2[:, :, :], t1[:, :, :], t3[:, :, :], ALU.mult))
                nc.vector.tensor_reduce(col[:, :], top[:, :, :], AX.X, ALU.add).then_inc(act_in, 1)
                dve.wait_ge(act_in, 3)
                link(nc.vector.tensor_scalar(col2[:, :], col[:, :], 1e-6, None, ALU.add))
                link(nc.vector.reciprocal(col3[:, :], col2[:, :]))
                dve.wait_ge(act_out, 3)
                link(nc.vector.tensor_tensor(col2[:, :], col3[:, :], index_f[:, :, 0], ALU.mult))
                nc.vector.tensor_tensor(gates[:, :, :], t2[:, :, :],
                                        col2[:, :].unsqueeze(2).broadcast_to(full), ALU.mult).then_inc(gates_ready, 1)
            else:
                link(nc.vector.tensor_reduce(col[:, :], logits[:, :, :], AX.X, ALU.max))
                nc.vector.tensor_tensor(t1[:, :, :], logits[:, :, :], col[:, :].unsqueeze(2).broadcast_to(full),
                                        ALU.subtract).then_inc(act_in, 1)
                dve.wait_ge(act_out, 1)
                chosen = logits
                if kind == "probs":
                    link(nc.vector.tensor_reduce(col2[:, :], t2[:, :, :], AX.X, ALU.add))
                    link(nc.vector.reciprocal(col3[:, :], col2[:, :]))
                    link(nc.vector.tensor_tensor(t3[:, :, :], t2[:, :, :],
                                                 col3[:, :].unsqueeze(2).broadcast_to(full), ALU.mult))
                    chosen = t3
                for i in range(TT):
                    last = nc.vector.max(top[:, i, :], chosen[:, i, :])
                link(last)
                for i in range(TT):
                    last = nc.vector.max_index(index[:, i, :], top[:, i, :], chosen[:, i, :])
                link(last)
                link(nc.vector.tensor_copy(index_f[:, :, :], index[:, :, :]))
                dve.wait_ge(expert_ready, 1)
                names = expert[:, :].unsqueeze(1).broadcast_to(full)
                link(nc.vector.tensor_tensor(t1[:, :, :], names, index_f[:, :, 0:1].broadcast_to(full),
                                             ALU.is_equal))
                link(nc.vector.tensor_tensor(t3[:, :, :], names, index_f[:, :, 1:2].broadcast_to(full),
                                             ALU.is_equal))
                link(nc.vector.tensor_tensor(logits[:, :, :], t1[:, :, :], t3[:, :, :], ALU.add))
                link(nc.vector.tensor_tensor(t1[:, :, :], logits[:, :, :], t2[:, :, :], ALU.mult))
                link(nc.vector.tensor_reduce(col2[:, :], t1[:, :, :], AX.X, ALU.add))
                link(nc.vector.reciprocal(col3[:, :], col2[:, :]))
                nc.vector.tensor_tensor(gates[:, :, :], t1[:, :, :],
                                        col3[:, :].unsqueeze(2).broadcast_to(full), ALU.mult).then_inc(gates_ready, 1)
            for k in range(4):
                dve.wait_ge(turned, 4 * (k + 1))
                nc.vector.tensor_copy(gates_t[0:E, k * CW:(k + 1) * CW], psum[0:E, 4 + k, :]
                                      ).then_inc(turned_out, 1)

        @block.scalar
        def _(act):
            act.wait_ge(act_in, 1)
            if kind == "latent":
                nc.scalar.activation(t2[:, :, :], t3[:, :, :], ACT.Exp).then_inc(act_out, 1)
                act.wait_ge(act_in, 2)
                nc.scalar.activation(t3[:, :, :], t3[:, :, :], ACT.Ln).then_inc(act_out, 1)
                act.wait_ge(act_in, 3)
                nc.scalar.activation(index_f[:, :, 0], col[:, :], ACT.Tanh).then_inc(act_out, 1)
            else:
                nc.scalar.activation(t2[:, :, :], t1[:, :, :], ACT.Exp).then_inc(act_out, 1)


def latent(nc, psum, name, xn, u_t_dram, u_dram, v_dram, gamma_dram, gates_t, x):
    E = 64
    with ExitStack() as ctx:
        def sb(n, shape, dt=F32):
            return ctx.enter_context(nc.sbuf_tensor(f"{name}_{n}", shape, dt))

        sem = stage_semaphores(nc, ctx, name)

        u_t = sb("u_t", [P, E])
        uv = sb("uv", [E, 2, P])
        squares = sb("squares", [E, 2, P])
        length = sb("length", [E, 2])
        root = sb("root", [E, 2])
        inverse = sb("inverse", [E, 2])
        both = sb("both", [E, 1])
        gamma = sb("gamma", [P, 1])
        mixed = sb("mixed", [E, CH, CW])
        w_in = sem("w_in")
        step = sem("step")
        length_ready = sem("length_ready")
        root_ready = sem("root_ready")
        h_ready = sem("h_ready")
        mixed_ready = sem("mixed_ready")
        y_ready = sem("y_ready")
        x_ready = sem("x_ready")
        block = ctx.enter_context(nc.Block())

        @block.sync
        def _(sp):
            for dst, src in ((u_t[:, :], u_t_dram), (uv[:, 0, :], u_dram), (uv[:, 1, :], v_dram),
                             (gamma[:, :], gamma_dram)):
                sp.dma_start(dst, src).then_inc(w_in, 16)

        @block.tensor
        def _(pe):
            pe.wait_ge(w_in, 64)
            for c in range(CH):
                nc.tensor.matmul(psum[0:E, c, :], u_t[:, :], xn[:, c * CW:(c + 1) * CW], start=True,
                                 stop=True).then_inc(h_ready, 1)
            for c in range(CH):
                pe.wait_ge(mixed_ready, c + 1)
                nc.tensor.matmul(psum[:, CH + c, :], uv[:, 1, :], mixed[:, c, :], start=True,
                                 stop=True).then_inc(y_ready, 1)

        @block.scalar
        def _(act):
            act.wait_ge(length_ready, 1)
            nc.scalar.activation(root[:, :], length[:, :], ACT.Sqrt).then_inc(root_ready, 1)

        @block.vector
        def _(dve):
            count = [0]

            def link(ins):
                count[0] += 1
                ins.then_inc(step, 1)
                dve.wait_ge(step, count[0])

            dve.wait_ge(w_in, 64)
            link(nc.vector.tensor_tensor(squares[:, :, :], uv[:, :, :], uv[:, :, :], ALU.mult))
            nc.vector.tensor_reduce(length[:, :], squares[:, :, :], AX.X, ALU.add).then_inc(length_ready, 1)
            dve.wait_ge(root_ready, 1)
            link(nc.vector.tensor_scalar(length[:, :], root[:, :], 1e-6, None, ALU.max))
            link(nc.vector.reciprocal(inverse[:, :], length[:, :]))
            link(nc.vector.tensor_tensor(both[:, :], inverse[:, 0:1], inverse[:, 1:2], ALU.mult))
            for c in range(CH):
                dve.wait_ge(h_ready, c + 1)
                nc.vector.scalar_tensor_tensor(mixed[:, c, :], psum[0:E, c, :], both[:, 0:1],
                                               gates_t[0:E, c * CW:(c + 1) * CW], ALU.mult,
                                               ALU.mult).then_inc(mixed_ready, 1)
            for c in range(CH):
                dve.wait_ge(y_ready, c + 1)
                at = slice(c * CW, (c + 1) * CW)
                nc.vector.scalar_tensor_tensor(x[:, at], psum[:, CH + c, :], gamma[:, 0:1], x[:, at],
                                               ALU.mult, ALU.add).then_inc(x_ready, 1)


def experts(nc, psum, name, t, residual, gates_t, gates_dram, w1_dram, b1_dram, w2_dram, b2_dram, x, kind):
    E, HB = 8, 4
    OB = 4 if kind == "gelu" else 2
    with ExitStack() as ctx:
        def sb(n, shape, dt=F32):
            return ctx.enter_context(nc.sbuf_tensor(f"{name}_{n}", shape, dt))

        sem = stage_semaphores(nc, ctx, name)

        w1 = sb("w1", [P, E, HB * P])
        w2 = sb("w2", [P, E, OB, P])
        b1 = sb("b1", [P, E * HB])
        b2 = sb("b2", [E, P])
        gate = sb("gate", [P, E, CW])
        hidden = sb("hidden", [P, OB, CW])
        gated = sb("gated", [P, 2, CW])
        total = sb("total", [P, CW])
        extra = sb("extra", [P, CW])
        glu = sb("glu", [P, 2, CW])
        sig = sb("sig", [P, 2, CW])
        lin = sb("lin", [P, 2, CW])
        prod = sb("prod", [P, 2, CW])
        w_in = [sem(f"w_in{e}") for e in range(E)]
        b_in = sem("b_in")
        gates_out = sem("gates_out")
        gate_in = sem("gate_in")
        h_ready = sem("h_ready")
        h_taken = sem("h_taken")
        h_done = sem("h_done")
        y_part = sem("y_part")
        y_taken = sem("y_taken")
        bias_ready = sem("bias_ready")
        total_step = sem("total_step")
        extra_ready = sem("extra_ready")
        x_ready = sem("x_ready")
        glu_ready = sem("glu_ready")
        sig_ready = sem("sig_ready")
        lin_ready = sem("lin_ready")
        prod_ready = sem("prod_ready")
        block = ctx.enter_context(nc.Block())
        order = [0, 1, 2, 3] if kind == "gelu" else [0, 2, 1, 3]
        NY = E * OB
        NH = E * HB

        def over_chunks(eng, body):
            body(0)
            with eng.Fori(1, CH) as c:
                body(c)

        @block.sync
        def _(sp):
            sp.dma_start(gates_dram[:, :], gates_t[0:E, :]).then_inc(gates_out, 16)
            sp.dma_start(b1[:, :], b1_dram).then_inc(b_in, 16)
            sp.dma_start(b2[:, :], b2_dram).then_inc(b_in, 16)
            for e in range(E):
                sp.dma_start(w1[:, e, :], w1_dram[:, e, :]).then_inc(w_in[e], 16)
                sp.dma_start(w2[:, e, :, :], w2_dram[:, e, :, :]).then_inc(w_in[e], 16)
            sp.wait_ge(gates_out, 16)

            def chunk(c):
                after(sp, y_taken, c * E)
                sp.dma_start(gate[:, :, :], gates_dram[:, bass.ds(c * CW, CW)].partition_broadcast(P)
                             ).then_inc(gate_in, 16)
            over_chunks(sp, chunk)

        @block.tensor
        def _(pe):
            def out(c, e, j):
                pe.wait_ge(h_done, c * NY + (e * OB + j + 1))
                if j == 0:
                    after(pe, y_taken, c * E + (e - 1))
                nc.tensor.matmul(psum[:, 4 + e % 2, :], w2[:, e, j, :], hidden[:, j, :], start=j == 0,
                                 stop=j == OB - 1).then_inc(y_part, 1)

            def chunk(c):
                pe.wait_ge(b_in, 32)
                after(pe, extra_ready, c)
                nc.tensor.matmul(psum[:, 6, :], b2[:, :], gates_t[0:E, bass.ds(c * CW, CW)], start=True,
                                 stop=True).then_inc(bias_ready, 1)
                waiting = []
                for e in range(E):
                    pe.wait_ge(w_in[e], 32)
                    for i, j in enumerate(order):
                        k = e * HB + i
                        if kind == "gelu":
                            after(pe, h_done, c * NH + (k - 3))
                        else:
                            after(pe, h_taken, c * (NH // 2) + (k // 2 - 1))
                        nc.tensor.matmul(psum[:, k % 4, :], w1[:, e, j * P:(j + 1) * P],
                                         t[:, bass.ds(c * CW, CW)], start=True, stop=True).then_inc(h_ready, 1)
                        if kind == "gelu":
                            waiting.append((e, j))
                            if len(waiting) > 2:
                                out(c, *waiting.pop(0))
                        else:
                            if j >= 2:
                                waiting.append((e, j - 2))
                                if len(waiting) > 2:
                                    out(c, *waiting.pop(0))
                for e, j in waiting:
                    out(c, e, j)
            over_chunks(pe, chunk)

        @block.scalar
        def _(act):
            act.wait_ge(b_in, 32)

            def chunk(c):
                for e in range(E):
                    if kind == "gelu":
                        for j in range(HB):
                            n = c * NH + (e * HB + j)
                            act.wait_ge(h_ready, n + 1)
                            after(act, y_part, n - HB + 1)
                            nc.scalar.activation(hidden[:, j, :], psum[:, j, :], ACT.Gelu,
                                                 bias=b1[:, e * HB + j:e * HB + j + 1]).then_inc(h_done, 1)
                    else:
                        for j in range(2):
                            n = c * NY + (e * 2 + j)
                            act.wait_ge(glu_ready, n + 1)
                            after(act, prod_ready, n - 1)
                            nc.scalar.activation(sig[:, j, :], glu[:, j, :], ACT.Sigmoid,
                                                 scale=1.702).then_inc(sig_ready, 1)
            over_chunks(act, chunk)

        @block.vector
        def _(dve):
            dve.wait_ge(b_in, 32)

            def take(c, e):
                dve.wait_ge(y_part, c * NY + (e * OB + OB))
                after(dve, total_step, c * E + (e - 1))
                nc.vector.tensor_tensor(gated[:, e % 2, :], psum[:, 4 + e % 2, :], gate[:, e, :],
                                        ALU.mult).then_inc(y_taken, 1)

            def chunk(c):
                at = bass.ds(c * CW, CW)
                dve.wait_ge(bias_ready, c + 1)
                after(dve, total_step, c * E)
                nc.vector.tensor_tensor(extra[:, :], psum[:, 6, :], residual[:, at],
                                        ALU.add).then_inc(extra_ready, 1)
                dve.wait_ge(gate_in, (c + 1) * 16)
                for e in range(E):
                    if kind == "swiglu":
                        for j in range(2):
                            n = c * NY + (e * 2 + j)
                            m = c * NH + (e * HB + 2 * j)
                            bank = (e * HB + 2 * j) % 4
                            dve.wait_ge(h_ready, m + 1)
                            after(dve, prod_ready, n - 1)
                            nc.vector.tensor_scalar(glu[:, j, :], psum[:, bank, :],
                                                    b1[:, e * HB + j:e * HB + j + 1], 7.0, ALU.add,
                                                    ALU.min).then_inc(glu_ready, 1)
                            dve.wait_ge(h_ready, m + 2)
                            dve.wait_ge(glu_ready, n + 1)
                            after(dve, h_done, n - 1)
                            nc.vector.tensor_scalar(lin[:, j, :], psum[:, bank + 1, :],
                                                    b1[:, e * HB + 2 + j:e * HB + 3 + j], 7.0, ALU.add,
                                                    ALU.min).then_inc(h_taken, 1)
                            dve.wait_ge(h_taken, n + 1)
                            nc.vector.tensor_scalar(lin[:, j, :], lin[:, j, :], -7.0, 1.0, ALU.max,
                                                    ALU.add).then_inc(lin_ready, 1)
                            dve.wait_ge(sig_ready, n + 1)
                            nc.vector.tensor_tensor(prod[:, j, :], glu[:, j, :], sig[:, j, :],
                                                    ALU.mult).then_inc(prod_ready, 1)
                    if e:
                        take(c, e - 1)
                take(c, E - 1)
            over_chunks(dve, chunk)

        @block.gpsimd
        def _(pool):
            def add_up(c, e):
                pool.wait_ge(y_taken, c * E + (e + 1))
                if e == 0:
                    pool.wait_ge(extra_ready, c + 1)
                    after(pool, x_ready, c)
                    nc.gpsimd.tensor_tensor(total[:, :], extra[:, :], gated[:, 0, :],
                                            ALU.add).then_inc(total_step, 1)
                else:
                    pool.wait_ge(total_step, c * E + e)
                    nc.gpsimd.tensor_tensor(total[:, :], total[:, :], gated[:, e % 2, :],
                                            ALU.add).then_inc(total_step, 1)

            def chunk(c):
                for e in range(E):
                    if kind == "swiglu":
                        for j in range(2):
                            n = c * NY + (e * 2 + j)
                            pool.wait_ge(prod_ready, n + 1)
                            pool.wait_ge(lin_ready, n + 1)
                            after(pool, y_part, n - 1)
                            nc.gpsimd.tensor_tensor(hidden[:, j, :], prod[:, j, :], lin[:, j, :],
                                                    ALU.mult).then_inc(h_done, 1)
                    if e:
                        add_up(c, e - 1)
                add_up(c, E - 1)
                at = bass.ds(c * CW, CW)
                pool.wait_ge(total_step, (c + 1) * E)
                nc.gpsimd.tensor_tensor(x[:, at], x[:, at], total[:, :], ALU.add).then_inc(x_ready, 1)
            over_chunks(pool, chunk)


def block_stack(nc, a, out):
    with ExitStack() as ctx:
        psum = ctx.enter_context(nc.psum_tensor("psum", [P, 8, CW], F32))
        x = ctx.enter_context(nc.sbuf_tensor("x", [P, S], F32))
        xn = ctx.enter_context(nc.sbuf_tensor("xn", [P, S], F32))
        ident = ctx.enter_context(nc.sbuf_tensor("ident", [P, P], F32))
        mean_w = ctx.enter_context(nc.sbuf_tensor("mean_w", [P, P], F32))
        loaded = ctx.enter_context(nc.semaphore("loaded"))

        def dram(name, shape, dt=F32):
            return nc.dram_tensor(name, shape, dt).ap()

        with nc.Block() as block:
            @block.sync
            def _(sp):
                sp.dma_start(x[:, :], a["x_t"]).then_inc(loaded, 16)
                sp.dma_start(ident[:, :], a["identity"]).then_inc(loaded, 16)
                sp.wait_ge(loaded, 32)

            @block.vector
            def _(dve):
                nc.vector.memset(mean_w[:, :], 1.0 / P)

        def attention(n, jobs, rope, v_w, v_b, w_o, b_o, kind, scale, q_dram, k_dram):
            d = 64 if kind == "wide" else 8
            kv = 256 if kind == "wide" else P
            o_dram = dram(f"o{n}", (H, d + 1, S))
            project(nc, psum, f"proj{n}", xn, jobs, rope)
            with nc.sbuf_tensor(f"v_all{n}", [P, TT, kv], F32) as v_all:
                values(nc, psum, f"val{n}", xn, v_w, v_b, v_all, kv)
                attend(nc, psum, ident, v_all, q_dram, k_dram, o_dram, kind, scale, f"att{n}")
            project_out(nc, psum, f"out{n}", o_dram, d, w_o, b_o, a["spread_" + kind], x)

        normalise(nc, psum, "norm0a", x, xn, mean_w, 1e-5)
        q, k = dram("q0", (3, P, S), BF16), dram("k0", (3, P, S), BF16)
        attention(0, [(a["l0_wq"], a["l0_bq"], None, None, q), (a["l0_wk"], a["l0_bk"], None, None, k)],
                  None, a["l0_wv"], a["l0_bv"], a["l0_wo"], a["l0_bo"], "narrow", 8 ** -0.5, q, k)
        normalise(nc, psum, "norm0f", x, xn, mean_w, 1e-5)
        with nc.sbuf_tensor("gates0", [64, S], F32) as gates_t:
            with nc.sbuf_tensor("router_in0", [P, S], F32) as router_in:
                normalise(nc, psum, "norm0r", xn, router_in, mean_w, 1e-5, gain=a["l0_ln_g"], shift=a["l0_ln_b"])
                route(nc, psum, "route0", router_in, a["l0_router"], a["l0_router_b"], 64, gates_t, ident, "latent")
            latent(nc, psum, "latent0", xn, a["l0_u_t"], a["l0_u"], a["l0_v"], a["l0_gamma"], gates_t, x)
        mlp(nc, psum, "mlp0", xn, a["l0_w1"], None, a["l0_w2"], None, x)

        normalise(nc, psum, "norm1a", x, xn, mean_w, 1e-5)
        q, k = dram("q1", (3, P, S), BF16), dram("k1", (3, P, S), BF16)
        attention(1, [(a["l1_wq"], a["l1_bq"], a["l1_wq_turned"], a["l1_bq_turned"], q),
                      (a["l1_wk"], a["l1_bk"], a["l1_wk_turned"], a["l1_bk_turned"], k)],
                  (a["l1_cos"], a["l1_sin"]), a["l1_wv"], a["l1_bv"], a["l1_wo"], a["l1_bo"], "narrow",
                  8 ** -0.5, q, k)
        normalise(nc, psum, "norm1f", x, xn, mean_w, 1e-5)
        mlp(nc, psum, "mlp1", xn, a["l1_w1"], a["l1_b1"], a["l1_w2"], a["l1_b2"], x)

        normalise(nc, psum, "norm2a", x, xn, mean_w, 1e-5)
        q, k = dram("q2", (3, 8 * P, S), BF16), dram("k2", (3, 2 * P, S), BF16)
        jobs = [(a["l2_wq"][:, i * P:(i + 1) * P], a["zero_col"], a["l2_wq_turned"][:, i * P:(i + 1) * P],
                 a["zero_col"], q[:, i * P:(i + 1) * P, :]) for i in range(8)]
        jobs += [(a["l2_wk"][:, i * P:(i + 1) * P], a["zero_col"], a["l2_wk_turned"][:, i * P:(i + 1) * P],
                  a["zero_col"], k[:, i * P:(i + 1) * P, :]) for i in range(2)]
        attention(2, jobs, (a["l2_cos"], a["l2_sin"]), a["l2_wv"], None, a["l2_wo"], None, "wide", 0.125, q, k)
        normalise(nc, psum, "norm2f", x, xn, mean_w, 1e-5)
        with nc.sbuf_tensor("gates2", [8, S], F32) as gates_t, nc.sbuf_tensor("expert_in2", [P, S], F32) as t:
            normalise(nc, psum, "norm2e", xn, t, mean_w, 1e-5, gain=a["l2_gamma"], shift=a["l2_beta"])
            route(nc, psum, "route2", t, a["l2_gate"], None, 8, gates_t, ident, "probs")
            experts(nc, psum, "moe2", t, xn, gates_t, dram("gates2_dram", (8, S)), a["l2_w1"], a["l2_b1"], a["l2_w2"],
                    a["l2_b2"], x, "gelu")

        normalise(nc, psum, "norm3a", x, xn, mean_w, 1e-5)
        q, k = dram("q3", (3, P, S), BF16), dram("k3", (3, P, S), BF16)
        attention(3, [(a["l3_wq"], a["zero_col"], None, None, q), (a["identity"], a["zero_col"], None, None, k)],
                  None, a["l3_wv"], a["l3_bv"], a["l3_wo"], a["l3_bo"], "narrow", 8 ** -0.5, q, k)
        normalise(nc, psum, "norm3f", x, xn, mean_w, 1e-5)
        with nc.sbuf_tensor("gates3", [8, S], F32) as gates_t, nc.sbuf_tensor("expert_in3", [P, S], F32) as t:
            normalise(nc, psum, "norm3e", xn, t, mean_w, 1e-5, centre=False, gain=a["l3_norm"])
            route(nc, psum, "route3", t, a["l3_gate"], a["l3_gate_b"], 8, gates_t, ident, "logits")
            experts(nc, psum, "moe3", t, xn, gates_t, dram("gates3_dram", (8, S)), a["l3_w1"], a["l3_b1"], a["l3_w2"],
                    a["l3_b2"], x, "swiglu")

        stored = ctx.enter_context(nc.semaphore("stored"))
        with nc.Block() as block:
            @block.sync
            def _(sp):
                sp.dma_start(out, x[:, :]).then_inc(stored, 16)
                sp.wait_ge(stored, 16)


def rope_tables(dim, rows, turn):
    inv = (1.0 / 10000.0 ** (np.arange(0, dim, 2, dtype=np.float32) / np.float32(dim))).astype(np.float32)
    angle = np.outer(inv, np.arange(S, dtype=np.float32)).astype(np.float32)
    d = np.arange(rows) % dim
    sign = np.where(turn(d), np.float32(-1), np.float32(1))[:, None]
    angle = angle[d % (dim // 2)]
    return np.cos(angle).astype(np.float32), (np.sin(angle) * sign).astype(np.float32)


def layout(i):
    def rows(w):
        return np.ascontiguousarray(w)

    def col(b):
        return rows(np.reshape(b, (P, 1)))

    a = {"x_t": rows(i["L0_attn_x"][0].T), "identity": np.eye(P, dtype=np.float32),
         "zero_col": np.zeros((P, 1), np.float32)}
    h = np.arange(H)[:, None]
    a["spread_narrow"] = (np.arange(P)[None, :] // 8 == h).astype(np.float32)
    a["spread_wide"] = (np.arange(8 * P)[None, :] // 64 == h).astype(np.float32)
    for n in (0, 1):
        for s in "qkvo":
            a[f"l{n}_w{s}"] = rows(i[f"L{n}_attn_W{s}"].T)
            a[f"l{n}_b{s}"] = i[f"L{n}_attn_b{s}"] if s == "v" else col(i[f"L{n}_attn_b{s}"])
    a["l0_w1"] = rows(i["L0_ffn_W1"].T)
    a["l0_w2"] = rows(i["L0_ffn_W2"].T.reshape(4, P, P).transpose(1, 0, 2))
    a["l0_ln_g"], a["l0_ln_b"] = col(i["L0_ffn_ln_g"]), col(i["L0_ffn_ln_b"])
    a["l0_router"], a["l0_router_b"] = rows(i["L0_ffn_router_W"].T), i["L0_ffn_router_b"]
    a["l0_u_t"], a["l0_u"], a["l0_v"] = rows(i["L0_ffn_raw_U"].T), i["L0_ffn_raw_U"], i["L0_ffn_raw_V"]
    a["l0_gamma"] = col(i["L0_ffn_gamma"])
    pair = np.arange(P) ^ 1
    for s in "qk":
        a[f"l1_w{s}_turned"] = rows(i[f"L1_attn_W{s}"][pair].T)
        a[f"l1_b{s}_turned"] = col(i[f"L1_attn_b{s}"][pair])
    a["l1_cos"], a["l1_sin"] = rope_tables(8, P, lambda d: d % 2 == 0)
    a["l1_w1"] = i["L1_ffn_w1"]
    a["l1_b1"] = rows(i["L1_ffn_b1"].reshape(4, P).T)
    a["l1_w2"] = rows(i["L1_ffn_w2"].reshape(4, P, P).transpose(1, 0, 2))
    a["l1_b2"] = col(i["L1_ffn_b2"])
    for s in "qkv":
        a[f"l2_w{s}"] = i[f"L2_attn_W{s}"]
    for s, n in (("q", 1024), ("k", 256)):
        a[f"l2_w{s}_turned"] = rows(i[f"L2_attn_W{s}"][:, np.arange(n) ^ 32])
    a["l2_cos"], a["l2_sin"] = rope_tables(64, P, lambda d: d < 32)
    a["l2_wo"] = rows(i["L2_attn_Wo"].reshape(8, P, P).transpose(1, 0, 2))
    a["l2_gamma"], a["l2_beta"], a["l2_gate"] = col(i["L2_ffn_gamma"]), col(i["L2_ffn_beta"]), i["L2_ffn_gate_w"]
    a["l2_w1"] = rows(i["L2_ffn_w1"].transpose(1, 0, 2))
    a["l2_b1"] = rows(i["L2_ffn_b1"].reshape(8, 4, P).transpose(2, 0, 1).reshape(P, 32))
    a["l2_w2"] = rows(i["L2_ffn_w2"].reshape(8, 4, P, P).transpose(2, 0, 1, 3))
    a["l2_b2"] = i["L2_ffn_b2"]
    wq = np.zeros((P, P), np.float32)
    for n in range(H):
        wq[8 * n:8 * n + 8, 8 * n:8 * n + 8] = i["L3_attn_w_att_val"][n]
    a["l3_wq"] = wq
    a["l3_wv"], a["l3_bv"] = rows(i["L3_attn_wv_w"].T), i["L3_attn_wv_b"]
    a["l3_wo"], a["l3_bo"] = rows(i["L3_attn_out_w"].T), col(i["L3_attn_out_b"])
    a["l3_norm"], a["l3_gate"], a["l3_gate_b"] = col(i["L3_ffn_norm_scale"]), i["L3_ffn_gate_w"], i["L3_ffn_gate_b"]
    halves = np.concatenate([np.arange(0, 512, 2), np.arange(1, 512, 2)])
    a["l3_w1"] = rows(i["L3_ffn_mlp1_w"][:, :, halves].transpose(1, 0, 2))
    a["l3_b1"] = rows(i["L3_ffn_mlp1_b"][:, halves].reshape(8, 4, P).transpose(2, 0, 1).reshape(P, 32))
    a["l3_w2"] = rows(i["L3_ffn_mlp2_w"].reshape(8, 2, P, P).transpose(2, 0, 1, 3))
    a["l3_b2"] = i["L3_ffn_mlp2_b"]
    return a


def kernel(**inputs):
    import concourse.bacc as _bacc
    from concourse.bass_utils import run_bass_kernel_spmd as _run

    nc = _bacc.Bacc("TRN2", target_bir_lowering=False, num_devices=1)
    arrays, args = {}, {}
    for name, value in layout({k: np.asarray(v) for k, v in inputs.items()}).items():
        value = np.ascontiguousarray(value)
        arrays[f"in_{name}"] = value
        args[name] = nc.dram_tensor(f"in_{name}", value.shape, mybir.dt.from_np(value.dtype),
                                    kind="ExternalInput").ap()
    out = nc.dram_tensor("out_y_t", (P, S), F32, kind="ExternalOutput").ap()
    block_stack(nc, args, out)
    r = _run(nc, [arrays], core_ids=[0])
    return np.ascontiguousarray(r.results[0]["out_y_t"].T)[None]
```

```python
from contextlib import ExitStack

import numpy as np

import concourse.bass as bass
from concourse import mybir

ALU = mybir.AluOpType
ACT = mybir.ActivationFunctionType
AX = mybir.AxisListType
F32 = mybir.dt.float32
BF16 = mybir.dt.bfloat16
F16 = mybir.dt.float16

P = 128
S = 2048
H = 16
CW = 512
CH = S // CW
TT = S // P
LEAD = 5
FULL = TT - LEAD
TURN = FULL + 1
QK_BOUND = 2.0 ** 10
MAX_UNIT = 2.0 ** 12
ONE_PAIR = float(np.array([0x3F803F80], np.uint32).view(np.float32)[0])


def stage_semaphores(nc, ctx, name):
    taken = []

    def clear():
        nc.clear_and_free_semaphores(taken)
        nc.all_engine_barrier()

    def sem(n):
        taken.append(nc.alloc_semaphore(f"{name}_{n}"))
        return taken[-1]

    ctx.callback(clear)
    return sem


def after(eng, sem, value):
    if not (isinstance(value, int) and value <= 0):
        eng.wait_ge(sem, value)


class Shape:

    def __init__(self, wide, scale, ident, group, blocks, dtype, v_cols, v_dims, order, max_row0, max_scale,
                 max_bank0, max_banks, out_bank0, out_banks, o_rows, q_loads, k_loads):
        self.wide = wide
        self.scale = scale
        self.ident = ident
        self.group = group
        self.groups = H // group
        self.blocks = blocks
        self.dtype = dtype
        self.v_cols = v_cols
        self.v_dims = v_dims
        self.order = order
        self.max_row0 = max_row0
        self.max_scale = max_scale
        self.max_bank0 = max_bank0
        self.max_banks = max_banks
        self.out_bank0 = out_bank0
        self.out_banks = out_banks
        self.o_rows = o_rows
        self.q_loads = q_loads
        self.k_loads = k_loads


def attention_core(nc, psum, cfg, q_ring, k_res, xn, w_v, v_width, v_all, load_k, load_q, store_o, name):
    with ExitStack() as ctx:
        def sb(n, shape, dt):
            return ctx.enter_context(nc.sbuf_tensor(f"{name}_{n}", shape, dt))

        sem = stage_semaphores(nc, ctx, name)

        probs = sb("probs", [P, 2 * CH, CW], F32)
        v_head = sb("v_head", [P, TT, cfg.v_cols], F32)
        tile_max = sb("tile_max", [P, TT * CH], F32)
        neg_max = sb("neg_max", [P, TT], F32)
        max_row = sb("max_row", [TT, P], F32)
        max_rest = sb("max_rest", [TT, P], F32)
        max_rest2 = sb("max_rest2", [TT, P], F32)
        scale_row = sb("scale_row", [TT, P], F32)
        max_parts = sb("max_parts", [TT, 3, P], cfg.dtype)
        out_sb = sb("out_sb", [P, cfg.out_banks, CW], F32)
        if cfg.wide:
            ones_v = sb("ones_v", [P, 32], F32)
            sums = sb("sums", [P, CH, CW], F32)
            sum_sb = sb("sum_sb", [P, CW], F32)

        v_ready = sem("v_ready")
        v_copied = sem("v_copied")
        k_loaded = [sem(f"k_loaded{g}") for g in range(cfg.groups)]
        q_loaded = sem("q_loaded")
        scores_ready = sem("scores_ready")
        exp_done = sem("exp_done")
        pv_done = sem("pv_done")
        max_ready = sem("max_ready")
        max_taken = sem("max_taken")
        head_max = sem("head_max")
        max_turned = sem("max_turned")
        max_copied = sem("max_copied")
        split_step = sem("split_step")
        max_rows_in = sem("max_rows_in")
        consts_set = sem("consts_set")
        v_zeroed = sem("v_zeroed")
        v_head_ready = sem("v_head_ready")
        out_copied = sem("out_copied")
        out_stored = sem("out_stored")
        if cfg.wide:
            dve_added = sem("dve_added")
            pool_added = sem("pool_added")
            sum_ready = sem("sum_ready")
            sum_copied = sem("sum_copied")
            sum_stored = sem("sum_stored")

        MB = cfg.max_banks
        TURN_BANK = 7
        V_BANKS = (5, 6)
        FIRST = CH * (TT + LEAD)
        PER = P // cfg.v_cols
        block = ctx.enter_context(nc.Block())

        def max_unit_of(kt):
            u = kt + LEAD
            return (1, u) if u < TT else (2, u - TT)

        def max_bank(c, early):
            return c if early else cfg.max_bank0 + c % MB

        @block.tensor
        def _(pe):
            def max_tile(hm, qt, c, early=False):
                n = hm * (TT * CH) + (CH * qt + c)
                if qt == 0 and c == 0:
                    pe.wait_ge(q_loaded, (hm + 1) * (16 * cfg.q_loads))
                after(pe, max_taken, n - (CH if early else MB) + 1)
                for j in range(cfg.blocks):
                    mm = nc.tensor.matmul(
                        psum[:, max_bank(c, early), :],
                        q_ring[:, bass.ds((hm % 4) * (cfg.blocks * S) + (j * S + qt * P), P)],
                        k_res[:, bass.ds((hm // cfg.group) * (cfg.blocks * S) + (j * S + c * CW), CW)],
                        start=j == 0, stop=j == cfg.blocks - 1)
                mm.then_inc(max_ready, 1)

            def turn_max(hm):
                pe.wait_ge(head_max, hm + 1)
                if cfg.wide:
                    after(pe, sum_copied, hm - 1)
                nc.tensor.transpose(psum[0:TT, TURN_BANK, 0:P], neg_max[:, :],
                                    cfg.ident[:, :]).then_inc(max_turned, 1)

            def score_tile(h, kt, c):
                if kt == 0 and c == 0:
                    pe.wait_ge(max_rows_in, (h + 1) * 48)
                n = h * (TT * CH) + (CH * kt + c)
                after(pe, exp_done, n - CH + 1)
                for j in range(cfg.blocks):
                    mm = nc.tensor.matmul(
                        psum[:, c, :],
                        k_res[:, bass.ds((h // cfg.group) * (cfg.blocks * S) + (j * S + kt * P), P)],
                        q_ring[:, bass.ds((h % 4) * (cfg.blocks * S) + (j * S + c * CW), CW)],
                        start=j == 0, stop=j == cfg.blocks - 1)
                mm.then_inc(scores_ready, 1)

            def pv(h, kt, first):
                if kt == 0 and first == 0:
                    pe.wait_ge(v_head_ready, h + 1)
                    after(pe, out_copied, h)
                pe.wait_ge(exp_done, h * (TT * CH) + (CH * kt + first + PER))
                for c in range(first, first + PER):
                    at = cfg.v_cols * (c % PER)
                    mm = nc.tensor.matmul(psum[at:at + cfg.v_cols, cfg.out_bank0 + c // PER, :], v_head[:, kt, :],
                                          probs[:, CH * (kt % 2) + c, :], start=kt == 0, stop=kt == TT - 1)
                if first + PER == CH:
                    mm.then_inc(pv_done, 1)

            def sum_up(h, last=False):
                pe.wait_ge(dve_added, (h + 1) * (2 * (TT - 1)))
                pe.wait_ge(pool_added, (h + 1) * (2 * (TT - 1)))
                pe.wait_ge(max_copied, H if last else h + 2)
                for c in range(CH):
                    mm = nc.tensor.matmul(psum[32 * c:32 * c + 32, TURN_BANK, :], ones_v[:, :], sums[:, c, :],
                                          start=True, stop=True)
                mm.then_inc(sum_ready, 1)

            def head(h, ahead, first=False):
                for kt in range(TT):
                    d, qt = max_unit_of(kt)
                    for what, n in cfg.order:
                        if what == "max" and d <= ahead:
                            max_tile(h + d, qt, n)
                        elif what == "score":
                            score_tile(h, kt, n)
                        elif what == "pv" and kt > 0:
                            pv(h, kt - 1, n)
                        elif what == "pv" and not first:
                            pv(h - 1, TT - 1, n)
                    if cfg.wide and kt == 1 and not first:
                        sum_up(h - 1)
                    if kt == TURN and ahead >= 1:
                        turn_max(h + 1)

            pe.wait_ge(k_loaded[0], 16 * cfg.k_loads)
            for qt in range(TT):
                for c in range(CH):
                    max_tile(0, qt, c, early=True)
                after(pe, v_copied, qt - 1)
                nc.tensor.matmul(psum[:, V_BANKS[qt % 2], 0:v_width], xn[:, qt * P:(qt + 1) * P],
                                 w_v[:, :], start=True, stop=True).then_inc(v_ready, 1)
            if cfg.group == 1:
                pe.wait_ge(k_loaded[1], 16 * cfg.k_loads)
            for qt in range(LEAD):
                for c in range(CH):
                    max_tile(1, qt, c, early=True)
                if qt == TURN - FULL:
                    turn_max(0)
            for g in range(1, cfg.groups):
                pe.wait_ge(k_loaded[g], 16 * cfg.k_loads)
            pe.wait_ge(max_taken, FIRST)
            pe.wait_ge(v_copied, TT)
            head(0, 2, first=True)
            with pe.Fori(1, H - 2) as h:
                head(h, 2)
            head(H - 2, 1)
            head(H - 1, 0)
            for first in range(0, CH, PER):
                pv(H - 1, TT - 1, first)
            if cfg.wide:
                sum_up(H - 1, last=True)

        @block.scalar
        def _(act):
            for t in range(TT):
                act.wait_ge(v_ready, t + 1)
                nc.scalar.copy(v_all[:, t, :], psum[:, V_BANKS[t % 2], 0:v_width]).then_inc(v_copied, 1)

            def head(h):
                for kt in range(TT):
                    for c in range(CH):
                        act.wait_ge(scores_ready, h * (TT * CH) + (CH * kt + c + 1))
                        if c == 0 and not (isinstance(h, int) and h == 0 and kt < 2):
                            act.wait_ge(pv_done, h * TT + kt - 1)
                            if cfg.wide:
                                added = 2 * (max(kt - 2, 1) if kt > 1 else kt - 1)
                                act.wait_ge(dve_added, h * (2 * (TT - 1)) + added)
                                act.wait_ge(pool_added, h * (2 * (TT - 1)) + added)
                        nc.scalar.activation(probs[:, CH * (kt % 2) + c, :], psum[:, c, :], ACT.Exp,
                                             scale=cfg.scale).then_inc(exp_done, 1)

            head(0)
            with act.Fori(1, H) as h:
                head(h)

        def add_up(eng, engine, h, kt, c, added):
            if kt == 0:
                return
            if kt == 1 and c % 2 == 0:
                after(eng, sum_ready, h)
            eng.wait_ge(exp_done, h * (TT * CH) + (CH * kt + c + 1))
            after(eng, added, h * (2 * (TT - 1)) + 2 * (kt - 2) + c % 2 + 1)
            before = probs[:, c, :] if kt == 1 else sums[:, c, :]
            engine.tensor_tensor(sums[:, c, :], before, probs[:, CH * (kt % 2) + c, :], ALU.add).then_inc(added, 1)

        @block.vector
        def _(dve):
            def take_max(hm, qt, c, early=False):
                n = hm * (TT * CH) + (CH * qt + c)
                dve.wait_ge(max_ready, n + 1)
                if qt == 0 and c == 0:
                    after(dve, head_max, hm)
                nc.vector.reduce_max(tile_max[:, CH * qt + c:CH * qt + c + 1],
                                     psum[:, max_bank(c, early), :], AX.X).then_inc(max_taken, 1)
                if qt == TT - 1 and c == CH - 1:
                    dve.wait_ge(max_taken, n + 1)
                    after(dve, max_turned, hm)
                    nc.vector.tensor_reduce(
                        neg_max[:, :], tile_max[:, :].rearrange("p (t c) -> p t c", c=CH),
                        AX.X, ALU.max, negate=True).then_inc(head_max, 1)

            def copy_row(hm):
                dve.wait_ge(max_turned, hm + 1)
                after(dve, split_step, hm * 5)
                nc.vector.tensor_copy(max_row[:, :], psum[0:TT, TURN_BANK, 0:P]).then_inc(max_copied, 1)

            def copy_out(h):
                dve.wait_ge(pv_done, (h + 1) * TT)
                after(dve, out_stored, h * (16 * CH))
                nc.vector.tensor_copy(out_sb[:, :, :], psum[:, cfg.out_bank0:cfg.out_bank0 + cfg.out_banks, :]
                                      ).then_inc(out_copied, 1)

            def copy_sum(h):
                dve.wait_ge(sum_ready, h + 1)
                after(dve, sum_stored, h * 16)
                nc.vector.tensor_copy(sum_sb[:, :], psum[:, TURN_BANK, :]).then_inc(sum_copied, 1)

            def head(h, ahead, first=False):
                for kt in range(TT):
                    d, qt = max_unit_of(kt)
                    for c in range(CH):
                        if d <= ahead:
                            take_max(h + d, qt, c)
                        if cfg.wide and c < 2:
                            if kt > 0:
                                add_up(dve, nc.vector, h, kt - 1, c, dve_added)
                            elif not first:
                                add_up(dve, nc.vector, h - 1, TT - 1, c, dve_added)
                    if kt == TURN and ahead >= 1:
                        copy_row(h + 1)
                    if kt == 0 and not first:
                        copy_out(h - 1)
                    if cfg.wide and kt == 2 and not first:
                        copy_sum(h - 1)

            for qt in range(TT):
                for c in range(CH):
                    take_max(0, qt, c, early=True)
            for qt in range(LEAD):
                for c in range(CH):
                    take_max(1, qt, c, early=True)
                if qt == TURN - FULL:
                    copy_row(0)
            if cfg.wide:
                dve.wait_ge(consts_set, 2)
            head(0, 2, first=True)
            with dve.Fori(1, H - 2) as h:
                head(h, 2)
            head(H - 2, 1)
            head(H - 1, 0)
            if cfg.wide:
                for c in range(2):
                    add_up(dve, nc.vector, H - 1, TT - 1, c, dve_added)
            copy_out(H - 1)
            if cfg.wide:
                copy_sum(H - 1)

        @block.gpsimd
        def _(pool):
            nc.gpsimd.memset(scale_row[:, :], cfg.max_scale).then_inc(consts_set, 1)
            if cfg.wide:
                nc.gpsimd.memset(ones_v[:, :], 1.0).then_inc(consts_set, 1)
            else:
                nc.gpsimd.memset(v_head[:, :, :], 0.0).then_inc(v_zeroed, 1)
                pool.wait_ge(v_zeroed, 1)
                nc.gpsimd.memset(v_head[:, :, cfg.v_dims:cfg.v_dims + 1], 1.0).then_inc(consts_set, 1)
            pool.wait_ge(consts_set, 2)

            def fill_v(h):
                after(pool, pv_done, h * TT)
                nc.gpsimd.tensor_copy(v_head[:, :, 0:cfg.v_dims],
                                      v_all[:, :, bass.ds((h // cfg.group) * cfg.v_dims, cfg.v_dims)]
                                      ).then_inc(v_head_ready, 1)

            def split_max(hm):
                k = hm * 5
                pool.wait_ge(max_copied, hm + 1)
                after(pool, max_rows_in, hm * 48)
                nc.gpsimd.tensor_tensor(max_parts[:, 0, :], max_row[:, :], scale_row[:, :],
                                        ALU.mult).then_inc(split_step, 1)
                nc.gpsimd.tensor_tensor(max_rest[:, :], max_row[:, :], scale_row[:, :],
                                        ALU.mult).then_inc(split_step, 1)
                pool.wait_ge(split_step, k + 2)
                nc.gpsimd.tensor_tensor(max_rest2[:, :], max_rest[:, :], max_parts[:, 0, :],
                                        ALU.subtract).then_inc(split_step, 1)
                pool.wait_ge(split_step, k + 3)
                nc.gpsimd.tensor_tensor(max_parts[:, 1, :], max_rest[:, :], max_parts[:, 0, :],
                                        ALU.subtract).then_inc(split_step, 1)
                pool.wait_ge(split_step, k + 4)
                nc.gpsimd.tensor_tensor(max_parts[:, 2, :], max_rest2[:, :], max_parts[:, 1, :],
                                        ALU.subtract).then_inc(split_step, 1)

            def adds(h, kt):
                if cfg.wide:
                    for c in range(2, CH):
                        add_up(pool, nc.gpsimd, h, kt, c, pool_added)

            def head(h, ahead):
                for kt in range(TT):
                    adds(h, kt)
                    if kt == TURN and ahead >= 1:
                        split_max(h + 1)
                if ahead >= 1:
                    fill_v(h + 1)

            pool.wait_ge(v_copied, TT)
            fill_v(0)
            split_max(0)
            head(0, 1)
            with pool.Fori(1, H - 1) as h:
                head(h, 1)
            head(H - 1, 0)

        @block.sync
        def _(sp):
            def put_max_rows(hm):
                sp.wait_ge(split_step, (hm + 1) * 5)
                for j in range(3):
                    dst = q_ring[cfg.max_row0 + j:cfg.max_row0 + j + 1,
                                 bass.ds((hm % 4) * (cfg.blocks * S) + (cfg.blocks - 1) * S, S)]
                    sp.dma_start(dst, max_parts[:, j, :]).then_inc(max_rows_in, 16)

            def q_in(h):
                after(sp, exp_done, (h - 3) * (TT * CH))
                after(sp, q_loaded, h * (16 * cfg.q_loads))
                load_q(sp, h, q_loaded)

            def put_out(h):
                sp.wait_ge(out_copied, h + 1)
                for c in range(CH):
                    store_o(sp, h, c, out_sb[cfg.v_cols * (c % PER):cfg.v_cols * (c % PER) + cfg.o_rows,
                                             c // PER, :]).then_inc(out_stored, 16)
                if cfg.wide:
                    sp.wait_ge(sum_copied, h + 1)
                    store_o(sp, h, None, sum_sb[0:P:32, :]).then_inc(sum_stored, 16)

            load_k(sp, 0, k_loaded[0])
            q_in(0)
            load_k(sp, 1, k_loaded[1])
            q_in(1)
            for g in range(2, cfg.groups):
                load_k(sp, g, k_loaded[g])
            q_in(2)
            q_in(3)
            put_max_rows(0)
            put_max_rows(1)
            with sp.Fori(1, H - 3) as h:
                q_in(h + 3)
                put_out(h - 1)
                put_max_rows(h + 1)
            for h in range(H - 3, H - 1):
                put_out(h - 1)
                put_max_rows(h + 1)
            put_out(H - 2)
            put_out(H - 1)
            sp.wait_ge(out_stored, H * 16 * CH)
            if cfg.wide:
                sp.wait_ge(sum_stored, H * 16)


def attend(nc, psum, ident, xn, w_v, v_width, v_all, q_ring, k_res, q_dram, k_dram, o_dram, wide, scale, name):
    if wide:
        order = [("max", 0), ("score", 0), ("score", 1), ("max", 1), ("score", 2), ("score", 3), ("max", 2),
                 ("pv", 0), ("max", 3), ("pv", 2)]
        cfg = Shape(wide=True, scale=scale, ident=ident, group=4, blocks=2, dtype=F16, v_cols=64, v_dims=64,
                    order=order, max_row0=64, max_scale=1.0 / MAX_UNIT, max_bank0=4, max_banks=1, out_bank0=5,
                    out_banks=2, o_rows=64, q_loads=3, k_loads=3)

        def load_q(sp, h, loaded):
            at = (h % 4) * (2 * S)
            rows = bass.ds(h * 64, 64)
            sp.dma_start(q_ring[:, bass.ds(at, S)], q_dram[:, rows, :]).then_inc(loaded, 16)
            sp.dma_start(q_ring[0:64, bass.ds(at + S, S)], q_dram[0:1, rows, :]).then_inc(loaded, 16)
            sp.dma_start(q_ring[64:67, bass.ds(at + S, S)], q_ring[96:99, bass.ds(at + S, S)]).then_inc(loaded, 16)

        def load_k(sp, g, loaded):
            at = g * 2 * S
            rows = slice(g * 64, g * 64 + 64)
            sp.dma_start(k_res[0:64, at:at + S], k_dram[0, rows, :]).then_inc(loaded, 16)
            sp.dma_start(k_res[64:128, at:at + S], k_dram[0, rows, :]).then_inc(loaded, 16)
            sp.dma_start(k_res[0:64, at + S:at + 2 * S], k_dram[1, rows, :]).then_inc(loaded, 16)

        def store_o(sp, h, c, src):
            if c is None:
                return sp.dma_start(o_dram[bass.ds(h, 1), 64, :], src)
            return sp.dma_start(o_dram[bass.ds(h, 1), 0:64, c * CW:(c + 1) * CW], src)
    else:
        order = [("max", 0), ("score", 0), ("score", 1), ("max", 1), ("score", 2), ("score", 3), ("max", 2),
                 ("pv", 0), ("max", 3)]
        cfg = Shape(wide=False, scale=scale, ident=ident, group=1, blocks=1, dtype=BF16, v_cols=32, v_dims=8,
                    order=order, max_row0=48, max_scale=1.0, max_bank0=4, max_banks=2, out_bank0=6,
                    out_banks=1, o_rows=9, q_loads=4, k_loads=3)

        def load_q(sp, h, loaded):
            at = (h % 4) * S
            rows = bass.ds(h * 8, 8)
            for part, n, r in ((0, 3, 0), (1, 2, 24), (2, 1, 40)):
                sp.dma_start(q_ring[r:r + 8 * n, bass.ds(at, S)],
                             q_dram[part:part + 1, rows, :].broadcast_to([n, 8, S])).then_inc(loaded, 16)
            sp.dma_start(q_ring[48:51, bass.ds(at, S)], q_ring[64:67, bass.ds(at, S)]).then_inc(loaded, 16)

        def load_k(sp, h, loaded):
            rows = slice(h * 8, h * 8 + 8)
            for n, r in ((3, 0), (2, 24), (1, 40)):
                sp.dma_start(k_res[r:r + 8 * n, h * S:(h + 1) * S],
                             k_dram[0:n, rows, :]).then_inc(loaded, 16)

        def store_o(sp, h, c, src):
            return sp.dma_start(o_dram[bass.ds(h, 1), :, c * CW:(c + 1) * CW], src)
    attention_core(nc, psum, cfg, q_ring, k_res, xn, w_v, v_width, v_all, load_k, load_q, store_o, name)


def normalise(nc, psum, name, src, dst, mean_w, pick, eps, centre=True, gain=None, shift=None):
    with ExitStack() as ctx:
        def sb(n, shape, dt=F32):
            return ctx.enter_context(nc.sbuf_tensor(f"{name}_{n}", shape, dt))

        sem = stage_semaphores(nc, ctx, name)

        centred = sb("centred", [P, S]) if centre else src
        squares = sb("squares", [P, S])
        spread = sb("spread", [P, CW])
        scale = sb("scale", [P, CW])
        eps_col = sb("eps_col", [P, 1])
        affine = sb("affine", [P, 2])
        affine_in = sem("affine_in")
        eps_set = sem("eps_set")
        mean_ready = sem("mean_ready")
        centred_ready = sem("centred_ready")
        squares_ready = sem("squares_ready")
        var_ready = sem("var_ready")
        spread_ready = sem("spread_ready")
        scale_ready = sem("scale_ready")
        picked = sem("picked")
        unit_ready = sem("unit_ready")
        VAR_BANK = CH
        block = ctx.enter_context(nc.Block())

        def part(t, c):
            return t[:, c * CW:(c + 1) * CW]

        @block.sync
        def _(sp):
            if gain is not None:
                sp.dma_start(affine[:, 0:1], gain).then_inc(affine_in, 16)
                if shift is not None:
                    sp.dma_start(affine[:, 1:2], shift).then_inc(affine_in, 16)

        @block.tensor
        def _(pe):
            if centre:
                for c in range(CH):
                    nc.tensor.matmul(psum[:, c, :], mean_w[:, :], part(src, c), start=True,
                                     stop=True).then_inc(mean_ready, 1)
            for c in range(CH):
                pe.wait_ge(squares_ready, c + 1)
                nc.tensor.matmul(psum[32 * c:32 * c + 32, VAR_BANK, :], mean_w[:, 0:32], part(squares, c),
                                 start=True, stop=True).then_inc(var_ready, 1)
            pe.wait_ge(scale_ready, 1)
            for c in range(CH):
                if centre:
                    pe.wait_ge(centred_ready, c + 1)
                nc.tensor.matmul(psum[:, c, :], pick[:, c * P:(c + 1) * P], scale[:, :], start=True,
                                 stop=True).then_inc(picked, 1)

        @block.scalar
        def _(act):
            for c in range(CH):
                if centre:
                    act.wait_ge(centred_ready, c + 1)
                nc.scalar.activation(part(squares, c), part(centred, c), ACT.Square).then_inc(squares_ready, 1)
            act.wait_ge(eps_set, 1)
            act.wait_ge(var_ready, CH)
            nc.scalar.activation(spread[:, :], psum[:, VAR_BANK, :], ACT.Sqrt,
                                 bias=eps_col[:, :]).then_inc(spread_ready, 1)

        @block.vector
        def _(dve):
            nc.vector.memset(eps_col[:, :], eps).then_inc(eps_set, 1)
            if centre:
                for c in range(CH):
                    dve.wait_ge(mean_ready, c + 1)
                    nc.vector.tensor_tensor(part(centred, c), part(src, c), psum[:, c, :],
                                            ALU.subtract).then_inc(centred_ready, 1)
            dve.wait_ge(spread_ready, 1)
            nc.vector.reciprocal(scale[:, :], spread[:, :]).then_inc(scale_ready, 1)
            if gain is not None:
                dve.wait_ge(affine_in, 16 if shift is None else 32)
            if centre:
                dve.wait_ge(centred_ready, CH)
            for c in range(CH):
                dve.wait_ge(picked, c + 1)
                if gain is None:
                    nc.vector.tensor_tensor(part(dst, c), part(centred, c), psum[:, c, :],
                                            ALU.mult).then_inc(unit_ready, 1)
                else:
                    nc.vector.scalar_tensor_tensor(part(dst, c), part(centred, c), affine[:, 0:1], psum[:, c, :],
                                                   ALU.mult, ALU.mult).then_inc(unit_ready, 1)
            if shift is not None:
                for c in range(CH):
                    dve.wait_ge(unit_ready, c + 1)
                    nc.vector.tensor_scalar(part(dst, c), part(dst, c), affine[:, 1:2], None, ALU.add)


def preset(nc, name, q_ring, k_res, wide):
    with ExitStack() as ctx:
        sem = stage_semaphores(nc, ctx, name)
        dve_set = sem("dve_set")
        pool_set = sem("pool_set")
        block = ctx.enter_context(nc.Block())
        half = k_res.shape[1] // 2
        q_half = q_ring.shape[1] // 2

        def fill(eng, engine, n, done):
            engine.memset(q_ring[:, n * q_half:(n + 1) * q_half].bitcast(F32), 0.0).then_inc(done, 1)
            eng.wait_ge(done, 1)
            if wide:
                for i, at in enumerate(range(n * half + S, (n + 1) * half, 2 * S)):
                    engine.memset(k_res[64:P, at:at + S], MAX_UNIT).then_inc(done, 1)
                    eng.wait_ge(done, i + 2)
            else:
                engine.memset(k_res[:, n * half:(n + 1) * half].bitcast(F32), ONE_PAIR).then_inc(done, 1)

        @block.vector
        def _(dve):
            fill(dve, nc.vector, 0, dve_set)

        @block.gpsimd
        def _(pool):
            fill(pool, nc.gpsimd, 1, pool_set)


def project(nc, psum, name, xn, jobs, rope, w_v, w_v_dram, mean_w=None, exp_scale=None, q_jobs=0):
    J = len(jobs)
    narrow = exp_scale is None
    R = 5 if J % 5 == 0 else 4
    n_parts = 3 if narrow else 2
    LOW_LAG = 2
    with ExitStack() as ctx:
        def sb(n, shape, dt=F32):
            return ctx.enter_context(nc.sbuf_tensor(f"{name}_{n}", shape, dt))

        sem = stage_semaphores(nc, ctx, name)

        w = sb("w", [P, J, P])
        b = sb("b", [P, J])
        w_in = sem("w_in")
        if rope is not None:
            w_turned = sb("w_turned", [P, J, P])
            b_turned = sb("b_turned", [P, J])
            cos = sb("cos", [P, S])
            sin = sb("sin", [P, S])
            by_cos = sb("by_cos", [P, R, CW])
            by_sin = sb("by_sin", [P, R, CW])
        value = sb("value", [P, R, CW])
        if narrow:
            rest = sb("rest", [P, R, CW])
        else:
            squares = sb("squares", [P, J, P])
            bound = sb("bound", [P, 2])
            power = sb("power", [P, 2])
            inverse = sb("inverse", [P, 2])
            unit = sb("unit", [P, 2])
            factor = sb("factor", [P, 2])
            both = sb("both", [P, 1])
            step = sem("step")
            squares_ready = sem("squares_ready")
            norms_ready = sem("norms_ready")
            root_ready = sem("root_ready")
        parts = sb("parts", [P, R, n_parts, CW], BF16 if narrow else F16)
        proj_ready = sem("proj_ready")
        turned_done = sem("turned_done")
        value_ready = sem("value_ready")
        high_ready = sem("high_ready")
        rest_ready = sem("rest_ready")
        mid_ready = sem("mid_ready")
        low_ready = sem("low_ready")
        weights_ready = sem("weights_ready")
        stored = [sem(f"stored{k}") for k in range(R)]
        block = ctx.enter_context(nc.Block())

        def count(c, n):
            return c * J + n

        def slot(c, n):
            return (c * J + n) % R if isinstance(c, int) else n % R

        def turns(c, n):
            return (c * J + n) // R if isinstance(c, int) else c * (J // R) + n // R

        def over_values(eng, steps):
            def chunk(c):
                for n in range(J):
                    for do, lag in steps:
                        if not isinstance(c, int) or c * J + n >= lag:
                            do(c, n - lag)

            if J % R == 0:
                chunk(0)
                with eng.Fori(1, CH) as c:
                    chunk(c)
            else:
                for c in range(CH):
                    chunk(c)
            for n in range(max(lag for do, lag in steps)):
                for do, lag in steps:
                    if n < lag:
                        do(CH, n - lag)

        loads = [(w[:, j, :], jobs[j][0]) for j in range(J)] + [(w_v, w_v_dram)]
        if narrow:
            loads += [(b[:, j:j + 1], jobs[j][1]) for j in range(J)]
        if rope is not None:
            loads += [(w_turned[:, j, :], jobs[j][2]) for j in range(J)]
            if narrow:
                loads += [(b_turned[:, j:j + 1], jobs[j][3]) for j in range(J)]
            loads += [(cos[:, :], rope[0]), (sin[:, :], rope[1])]

        @block.sync
        def _(sp):
            for dst, src in loads:
                sp.dma_start(dst, src).then_inc(w_in, 16)

            def store(c, n):
                sp.wait_ge(low_ready, count(c, n + 1))
                sp.dma_start(jobs[n % J][4][:, :, bass.ds(c * CW, CW)].rearrange("n p w -> p n w"),
                             parts[:, slot(c, n), :, :]).then_inc(stored[slot(c, n)], 16)
            over_values(sp, [(store, 0)])
            for k in range(R):
                sp.wait_ge(stored[k], 16 * ((CH * J - k + R - 1) // R))

        @block.tensor
        def _(pe):
            pe.wait_ge(w_in, 16 * len(loads))
            if not narrow:
                pe.wait_ge(squares_ready, 1)
                for first in range(0, J, 4):
                    last = min(first + 4, J)
                    mm = nc.tensor.matmul(psum[:, first // 4, 0:(last - first) * P], mean_w[:, :],
                                          squares[:, first:last, :], start=True, stop=True)
                mm.then_inc(norms_ready, 1)
                pe.wait_ge(weights_ready, 4)

            def matmul(c, n):
                after(pe, turned_done if rope is not None else value_ready, count(c, n - 1))
                x_c = xn[:, bass.ds(c * CW, CW)]
                mm = nc.tensor.matmul(psum[:, n % 2, :], w[:, n, :], x_c, start=True, stop=True)
                if rope is not None:
                    mm = nc.tensor.matmul(psum[:, 2 + n % 2, :], w_turned[:, n, :], x_c, start=True, stop=True)
                mm.then_inc(proj_ready, 1)
            over_values(pe, [(matmul, 0)])

        @block.scalar
        def _(act):
            act.wait_ge(w_in, 16 * len(loads))
            if not narrow:
                nc.scalar.activation(squares[:, :, :], w[:, :, :], ACT.Square).then_inc(squares_ready, 1)
                act.wait_ge(step, 2)
                nc.scalar.activation(bound[:, :], bound[:, :], ACT.Sqrt, scale=2.0 * P * P).then_inc(root_ready, 1)

            def biased(c, n):
                act.wait_ge(proj_ready, count(c, n + 1))
                after(act, low_ready, count(c, n - R + 1))
                nc.scalar.activation(value[:, slot(c, n), :], psum[:, n % 2, :], ACT.Identity,
                                     bias=b[:, n:n + 1]).then_inc(value_ready, 1)

            def high(c, n):
                act.wait_ge(value_ready, count(c, n + 1))
                after(act, stored[slot(c, n)], turns(c, n) * 16)
                nc.scalar.copy(parts[:, slot(c, n), 0, :], value[:, slot(c, n), :]).then_inc(high_ready, 1)

            def mid(c, n):
                act.wait_ge(rest_ready, count(c, n + 1))
                nc.scalar.copy(parts[:, slot(c, n), 1, :], rest[:, slot(c, n), :]).then_inc(mid_ready, 1)

            over_values(act, ([(biased, 0)] if rope is None else []) + [(high, 0)] + ([(mid, 1)] if narrow else []))

        @block.vector
        def _(dve):
            if not narrow:
                done = [0]

                def link(ins):
                    done[0] += 1
                    ins.then_inc(step, 1)
                    dve.wait_ge(step, done[0])

                dve.wait_ge(norms_ready, 1)
                nc.vector.reduce_max(bound[:, 0:1], psum[:, 0:2, :], AX.XY).then_inc(step, 1)
                nc.vector.reduce_max(bound[:, 1:2], psum[:, 2, 0:(J - q_jobs) * P], AX.X).then_inc(step, 1)
                done[0] = 2
                dve.wait_ge(root_ready, 1)
                link(nc.vector.tensor_scalar(inverse[:, :], bound[:, :], 1e-15, None, ALU.max))
                link(nc.vector.reciprocal(power[:, :], inverse[:, :]))
                link(nc.vector.tensor_scalar(unit[:, :].bitcast(mybir.dt.uint32), power[:, :].bitcast(mybir.dt.uint32),
                                             0x7F800000, None, ALU.bitwise_and))
                link(nc.vector.tensor_scalar(factor[:, :], unit[:, :], QK_BOUND, None, ALU.mult))
                link(nc.vector.tensor_tensor(both[:, :], factor[:, 0:1], factor[:, 1:2], ALU.mult))
                link(nc.vector.reciprocal(exp_scale[:, :], both[:, :]))
                link(nc.vector.tensor_scalar(exp_scale[:, :], exp_scale[:, :], 0.125, None, ALU.mult))
                for t in (w, w_turned):
                    for k, at in ((0, slice(0, q_jobs)), (1, slice(q_jobs, J))):
                        nc.vector.tensor_scalar(t[:, at, :], t[:, at, :], factor[:, k:k + 1], None,
                                                ALU.mult).then_inc(weights_ready, 1)
            dve.wait_ge(w_in, 16 * len(loads))

            def turn(c, n):
                dve.wait_ge(proj_ready, count(c, n + 1))
                after(dve, value_ready, count(c, n - R + 1))
                at = bass.ds(c * CW, CW)
                for dst, bank, bias, table in ((by_cos, n % 2, b, cos), (by_sin, 2 + n % 2, b_turned, sin)):
                    if narrow:
                        ins = nc.vector.scalar_tensor_tensor(dst[:, slot(c, n), :], psum[:, bank, :],
                                                             bias[:, n:n + 1], table[:, at], ALU.add, ALU.mult)
                    else:
                        ins = nc.vector.tensor_tensor(dst[:, slot(c, n), :], psum[:, bank, :], table[:, at], ALU.mult)
                ins.then_inc(turned_done, 1)

            def low(c, n):
                k = slot(c, n)
                if narrow:
                    dve.wait_ge(mid_ready, count(c, n + 1))
                    nc.vector.tensor_tensor(parts[:, k, 2, :], rest[:, k, :], parts[:, k, 1, :],
                                            ALU.subtract).then_inc(low_ready, 1)
                else:
                    dve.wait_ge(high_ready, count(c, n + 1))
                    nc.vector.tensor_tensor(parts[:, k, 1, :], value[:, k, :], parts[:, k, 0, :],
                                            ALU.subtract).then_inc(low_ready, 1)

            over_values(dve, [(turn, 0), (low, LOW_LAG)] if rope is not None else [(low, 0)])

        @block.gpsimd
        def _(pool):
            def add(c, n):
                pool.wait_ge(turned_done, count(c, n + 1))
                after(pool, low_ready, count(c, n - R + 1))
                nc.gpsimd.tensor_tensor(value[:, slot(c, n), :], by_cos[:, slot(c, n), :], by_sin[:, slot(c, n), :],
                                        ALU.add).then_inc(value_ready, 1)

            def subtract(c, n):
                pool.wait_ge(high_ready, count(c, n + 1))
                nc.gpsimd.tensor_tensor(rest[:, slot(c, n), :], value[:, slot(c, n), :], parts[:, slot(c, n), 0, :],
                                        ALU.subtract).then_inc(rest_ready, 1)

            steps = [(add, 0)] if rope is not None else []
            if narrow:
                steps.append((subtract, 1))
            over_values(pool, steps)


def project_out(nc, psum, name, o_dram, d, w_dram, b_dram, b_v_dram, spread_dram, x):
    groups = H * d // P
    per = P // d
    SPLIT = P // H
    with ExitStack() as ctx:
        def sb(n, shape, dt=F32):
            return ctx.enter_context(nc.sbuf_tensor(f"{name}_{n}", shape, dt))

        sem = stage_semaphores(nc, ctx, name)

        w = sb("w", [P, groups, P])
        b = sb("b", [P, 1])
        b_v = sb("b_v", [P, 1])
        b_all = sb("b_all", [P, 1])
        spread = sb("spread", [P, groups * P])
        sums = sb("sums", [P, S // SPLIT])
        inverse = sb("inverse", [P, S // SPLIT])
        inverse_row = sb("inverse_row", [P, S])
        o = sb("o", [P, groups, S])
        o_unit = sb("o_unit", [P, 2, CW])
        sums_in = sem("sums_in")
        consts_in = sem("consts_in")
        w_in = sem("w_in")
        o_in = [sem(f"o_in{g}") for g in range(groups)]
        rows_clear = sem("rows_clear")
        inverse_ready = sem("inverse_ready")
        inverse_in = sem("inverse_in")
        spread_ready = sem("spread_ready")
        o_ready = sem("o_ready")
        y_part = sem("y_part")
        bias_ready = sem("bias_ready")
        b_ready = sem("b_ready")
        x_ready = sem("x_ready")
        n_loads = 1 if b_dram is None else 3
        block = ctx.enter_context(nc.Block())

        @block.sync
        def _(sp):
            for h in range(H):
                sp.dma_start(sums[h * SPLIT:(h + 1) * SPLIT, :],
                             o_dram[h:h + 1, d, :].rearrange("h (a t) -> (h a) t", a=SPLIT)).then_inc(sums_in, 16)
            sp.dma_start(w[:, :, :], w_dram).then_inc(consts_in, 16)
            if b_dram is not None:
                sp.dma_start(b[:, :], b_dram).then_inc(consts_in, 16)
                sp.dma_start(b_v[:, :], b_v_dram).then_inc(consts_in, 16)
            sp.dma_start(spread[:, :], spread_dram).then_inc(w_in, 16)
            for g in range(groups):
                sp.dma_start(o[:, g, :], o_dram[g * per:(g + 1) * per, 0:d, :]).then_inc(o_in[g], 16)

        @block.gpsimd
        def _(pool):
            nc.gpsimd.memset(inverse_row[:, :], 0.0).then_inc(rows_clear, 1)

        @block.scalar
        def _(act):
            act.wait_ge(rows_clear, 1)
            act.wait_ge(inverse_ready, 1)
            for h in range(H):
                act.dma_start(inverse_row[h:h + 1, :],
                              inverse[h * SPLIT:(h + 1) * SPLIT, :]).then_inc(inverse_in, 16)

        @block.tensor
        def _(pe):
            pe.wait_ge(consts_in, 16 * n_loads)
            if b_dram is not None:
                nc.tensor.matmul(psum[:, 3, 0:1], w[:, 0, :], b_v[:, :], start=True, stop=True).then_inc(bias_ready, 1)
            pe.wait_ge(w_in, 16)
            pe.wait_ge(rows_clear, 1)
            pe.wait_ge(inverse_in, 16 * H)
            units = [(c, g) for c in range(CH) for g in range(groups)]

            def spread_sums(n):
                c, g = units[n]
                after(pe, o_ready, n - 1)
                nc.tensor.matmul(psum[:, n % 2, :], spread[:, g * P:(g + 1) * P],
                                 inverse_row[:, c * CW:(c + 1) * CW], start=True, stop=True).then_inc(spread_ready, 1)

            def out(n):
                c, g = units[n]
                pe.wait_ge(o_ready, n + 1)
                nc.tensor.matmul(psum[:, CH + c, :], w[:, g, :], o_unit[:, n % 2, :],
                                 start=g == 0, stop=g == groups - 1).then_inc(y_part, 1)

            spread_sums(0)
            for n in range(len(units)):
                if n + 1 < len(units):
                    spread_sums(n + 1)
                out(n)

        @block.vector
        def _(dve):
            dve.wait_ge(sums_in, 16 * H)
            nc.vector.reciprocal(inverse[:, :], sums[:, :]).then_inc(inverse_ready, 1)
            if b_dram is None:
                nc.vector.memset(b_all[:, :], 0.0).then_inc(b_ready, 1)
            else:
                dve.wait_ge(bias_ready, 1)
                dve.wait_ge(consts_in, 16 * n_loads)
                nc.vector.tensor_tensor(b_all[:, :], psum[:, 3, 0:1], b[:, :], ALU.add).then_inc(b_ready, 1)
            n = 0
            for c in range(CH):
                for g in range(groups):
                    dve.wait_ge(o_in[g], 16)
                    dve.wait_ge(spread_ready, n + 1)
                    after(dve, y_part, n - 1)
                    nc.vector.tensor_tensor(o_unit[:, n % 2, :], o[:, g, c * CW:(c + 1) * CW], psum[:, n % 2, :],
                                            ALU.mult).then_inc(o_ready, 1)
                    n += 1
            dve.wait_ge(b_ready, 1)
            for c in range(CH):
                dve.wait_ge(y_part, groups * (c + 1))
                at = slice(c * CW, (c + 1) * CW)
                nc.vector.scalar_tensor_tensor(x[:, at], psum[:, CH + c, :], b_all[:, 0:1], x[:, at],
                                               ALU.add, ALU.add).then_inc(x_ready, 1)


def mlp(nc, psum, name, xn, w1_dram, b1_dram, w2_dram, b2_dram, x):
    HB = 4
    with ExitStack() as ctx:
        def sb(n, shape, dt=F32):
            return ctx.enter_context(nc.sbuf_tensor(f"{name}_{n}", shape, dt))

        sem = stage_semaphores(nc, ctx, name)

        w1 = sb("w1", [P, HB * P])
        w2 = sb("w2", [P, HB, P])
        b1 = sb("b1", [P, HB])
        b2 = sb("b2", [P, 1])
        hidden = sb("hidden", [P, HB, CW])
        w_in = sem("w_in")
        b_clear = sem("b_clear")
        h_ready = sem("h_ready")
        h_done = sem("h_done")
        y_ready = sem("y_ready")
        y_part = sem("y_part")
        x_ready = sem("x_ready")
        loads = [(w1[:, :], w1_dram), (w2[:, :, :], w2_dram)]
        if b1_dram is not None:
            loads += [(b1[:, :], b1_dram), (b2[:, :], b2_dram)]
        block = ctx.enter_context(nc.Block())

        @block.sync
        def _(sp):
            for dst, src in loads:
                sp.dma_start(dst, src).then_inc(w_in, 16)

        @block.tensor
        def _(pe):
            pe.wait_ge(w_in, 16 * len(loads))
            units = [(c, j) for c in range(CH) for j in range(HB)]

            def out(n):
                c, j = units[n]
                pe.wait_ge(h_done, n + 1)
                nc.tensor.matmul(psum[:, CH + c, :], w2[:, j, :], hidden[:, j, :], start=j == 0,
                                 stop=j == HB - 1).then_inc(y_part, 1)

            for n, (c, j) in enumerate(units):
                after(pe, h_done, n - 1)
                nc.tensor.matmul(psum[:, n % 2, :], w1[:, j * P:(j + 1) * P], xn[:, c * CW:(c + 1) * CW],
                                 start=True, stop=True).then_inc(h_ready, 1)
                if n:
                    out(n - 1)
            out(len(units) - 1)

        @block.scalar
        def _(act):
            act.wait_ge(w_in, 16 * len(loads))
            if b1_dram is None:
                act.wait_ge(b_clear, 1)
            n = 0
            for c in range(CH):
                for j in range(HB):
                    act.wait_ge(h_ready, n + 1)
                    after(act, y_part, n - HB + 1)
                    nc.scalar.activation(hidden[:, j, :], psum[:, n % 2, :], ACT.Gelu,
                                         bias=b1[:, j:j + 1]).then_inc(h_done, 1)
                    n += 1

        @block.vector
        def _(dve):
            dve.wait_ge(w_in, 16 * len(loads))
            if b1_dram is None:
                nc.vector.memset(b2[:, :], 0.0).then_inc(y_ready, 1)
                nc.vector.memset(b1[:, :], 0.0).then_inc(b_clear, 1)
                dve.wait_ge(y_ready, 1)
            for c in range(CH):
                dve.wait_ge(y_part, HB * (c + 1))
                at = slice(c * CW, (c + 1) * CW)
                nc.vector.scalar_tensor_tensor(x[:, at], psum[:, CH + c, :], b2[:, 0:1], x[:, at],
                                               ALU.add, ALU.add).then_inc(x_ready, 1)


def route(nc, psum, name, t, w_dram, b_dram, E, gates_t, ident, kind):
    with ExitStack() as ctx:
        def sb(n, shape, dt=F32):
            return ctx.enter_context(nc.sbuf_tensor(f"{name}_{n}", shape, dt))

        sem = stage_semaphores(nc, ctx, name)

        w = sb("w", [P, E])
        b = sb("b", [P, E])
        logits = sb("logits", [P, TT, E])
        gates = sb("gates", [P, TT, E])
        top = sb("top", [P, TT, 8])
        t1 = sb("t1", [P, TT, E])
        t2 = sb("t2", [P, TT, E])
        t3 = sb("t3", [P, TT, E])
        col = sb("col", [P, TT])
        col2 = sb("col2", [P, TT])
        col3 = sb("col3", [P, TT])
        index = sb("index", [P, TT, 8], mybir.dt.uint32)
        index_f = sb("index_f", [P, TT, 8])
        expert = sb("expert", [P, E])
        w_in = sem("w_in")
        expert_ready = sem("expert_ready")
        logit_ready = sem("logit_ready")
        logit_taken = sem("logit_taken")
        step = sem("step")
        act_in = sem("act_in")
        act_out = sem("act_out")
        gates_ready = sem("gates_ready")
        turned = sem("turned")
        turned_out = sem("turned_out")
        n_loads = 1 + (b_dram is not None)
        block = ctx.enter_context(nc.Block())

        @block.sync
        def _(sp):
            sp.dma_start(w[:, :], w_dram).then_inc(w_in, 16)
            if b_dram is not None:
                sp.dma_start(b[:, :], b_dram.partition_broadcast(P)).then_inc(w_in, 16)

        @block.gpsimd
        def _(pool):
            nc.gpsimd.iota(expert[:, :], pattern=[[1, E]], base=0, channel_multiplier=0,
                           allow_small_or_imprecise_dtypes=True).then_inc(expert_ready, 1)

        @block.tensor
        def _(pe):
            pe.wait_ge(w_in, 16 * n_loads)
            for i in range(TT):
                after(pe, logit_taken, i - 3)
                nc.tensor.matmul(psum[:, i % 4, 0:E], t[:, i * P:(i + 1) * P], w[:, :], start=True,
                                 stop=True).then_inc(logit_ready, 1)
            pe.wait_ge(gates_ready, 1)
            for i in range(TT):
                nc.tensor.transpose(psum[0:E, 4 + i // 4, (i % 4) * P:(i % 4 + 1) * P], gates[:, i, :],
                                    ident[:, :]).then_inc(turned, 1)

        @block.vector
        def _(dve):
            count = [0]

            def link(ins):
                count[0] += 1
                ins.then_inc(step, 1)
                dve.wait_ge(step, count[0])

            dve.wait_ge(w_in, 16 * n_loads)
            for i in range(TT):
                dve.wait_ge(logit_ready, i + 1)
                if b_dram is None:
                    ins = nc.vector.tensor_copy(logits[:, i, :], psum[:, i % 4, 0:E])
                else:
                    ins = nc.vector.tensor_tensor(logits[:, i, :], psum[:, i % 4, 0:E], b[:, :], ALU.add)
                ins.then_inc(logit_taken, 1)
            dve.wait_ge(logit_taken, TT)
            full = [P, TT, E]
            if kind == "latent":
                link(nc.vector.tensor_scalar(t1[:, :, :], logits[:, :, :], 10.0, -10.0, ALU.min, ALU.max))
                link(nc.vector.tensor_scalar(t2[:, :, :], t1[:, :, :], -1.0, None, ALU.mult))
                nc.vector.tensor_tensor(t3[:, :, :], t1[:, :, :], t2[:, :, :], ALU.min).then_inc(act_in, 1)
                dve.wait_ge(act_out, 1)
                link(nc.vector.tensor_scalar(t3[:, :, :], t2[:, :, :], 1.0, None, ALU.add))
                nc.vector.tensor_scalar(logits[:, :, :], t3[:, :, :], -1.0, None, ALU.add).then_inc(act_in, 1)
                dve.wait_ge(act_in, 2)
                link(nc.vector.reciprocal(gates[:, :, :], logits[:, :, :]))
                link(nc.vector.tensor_tensor(logits[:, :, :], t2[:, :, :], gates[:, :, :], ALU.mult))
                dve.wait_ge(act_out, 2)
                link(nc.vector.tensor_tensor(t2[:, :, :], logits[:, :, :], t3[:, :, :], ALU.mult))
                link(nc.vector.tensor_scalar(t3[:, :, :], t1[:, :, :], 0.0, None, ALU.max))
                link(nc.vector.tensor_tensor(t1[:, :, :], t3[:, :, :], t2[:, :, :], ALU.add))
                for i in range(TT):
                    last = nc.vector.max(top[:, i, :], t1[:, i, :])
                link(last)
                for i in range(TT):
                    last = nc.vector.match_replace(t2[:, i, :], top[:, i, :], t1[:, i, :], -1.0)
                link(last)
                link(nc.vector.tensor_tensor(t3[:, :, :], t1[:, :, :], t2[:, :, :], ALU.not_equal))
                link(nc.vector.tensor_tensor(t2[:, :, :], t1[:, :, :], t3[:, :, :], ALU.mult))
                nc.vector.tensor_reduce(col[:, :], top[:, :, :], AX.X, ALU.add).then_inc(act_in, 1)
                dve.wait_ge(act_in, 3)
                link(nc.vector.tensor_scalar(col2[:, :], col[:, :], 1e-6, None, ALU.add))
                link(nc.vector.reciprocal(col3[:, :], col2[:, :]))
                dve.wait_ge(act_out, 3)
                link(nc.vector.tensor_tensor(col2[:, :], col3[:, :], index_f[:, :, 0], ALU.mult))
                nc.vector.tensor_tensor(gates[:, :, :], t2[:, :, :],
                                        col2[:, :].unsqueeze(2).broadcast_to(full), ALU.mult).then_inc(gates_ready, 1)
            else:
                link(nc.vector.tensor_reduce(col[:, :], logits[:, :, :], AX.X, ALU.max))
                nc.vector.tensor_tensor(t1[:, :, :], logits[:, :, :], col[:, :].unsqueeze(2).broadcast_to(full),
                                        ALU.subtract).then_inc(act_in, 1)
                dve.wait_ge(act_out, 1)
                chosen = logits
                if kind == "probs":
                    link(nc.vector.tensor_reduce(col2[:, :], t2[:, :, :], AX.X, ALU.add))
                    link(nc.vector.reciprocal(col3[:, :], col2[:, :]))
                    link(nc.vector.tensor_tensor(t3[:, :, :], t2[:, :, :],
                                                 col3[:, :].unsqueeze(2).broadcast_to(full), ALU.mult))
                    chosen = t3
                for i in range(TT):
                    last = nc.vector.max(top[:, i, :], chosen[:, i, :])
                link(last)
                for i in range(TT):
                    last = nc.vector.max_index(index[:, i, :], top[:, i, :], chosen[:, i, :])
                link(last)
                link(nc.vector.tensor_copy(index_f[:, :, :], index[:, :, :]))
                dve.wait_ge(expert_ready, 1)
                names = expert[:, :].unsqueeze(1).broadcast_to(full)
                link(nc.vector.tensor_tensor(t1[:, :, :], names, index_f[:, :, 0:1].broadcast_to(full),
                                             ALU.is_equal))
                link(nc.vector.tensor_tensor(t3[:, :, :], names, index_f[:, :, 1:2].broadcast_to(full),
                                             ALU.is_equal))
                link(nc.vector.tensor_tensor(logits[:, :, :], t1[:, :, :], t3[:, :, :], ALU.add))
                link(nc.vector.tensor_tensor(t1[:, :, :], logits[:, :, :], t2[:, :, :], ALU.mult))
                link(nc.vector.tensor_reduce(col2[:, :], t1[:, :, :], AX.X, ALU.add))
                link(nc.vector.reciprocal(col3[:, :], col2[:, :]))
                nc.vector.tensor_tensor(gates[:, :, :], t1[:, :, :],
                                        col3[:, :].unsqueeze(2).broadcast_to(full), ALU.mult).then_inc(gates_ready, 1)
            for k in range(4):
                dve.wait_ge(turned, 4 * (k + 1))
                nc.vector.tensor_copy(gates_t[0:E, k * CW:(k + 1) * CW], psum[0:E, 4 + k, :]
                                      ).then_inc(turned_out, 1)

        @block.scalar
        def _(act):
            act.wait_ge(act_in, 1)
            if kind == "latent":
                nc.scalar.activation(t2[:, :, :], t3[:, :, :], ACT.Exp).then_inc(act_out, 1)
                act.wait_ge(act_in, 2)
                nc.scalar.activation(t3[:, :, :], t3[:, :, :], ACT.Ln).then_inc(act_out, 1)
                act.wait_ge(act_in, 3)
                nc.scalar.activation(index_f[:, :, 0], col[:, :], ACT.Tanh).then_inc(act_out, 1)
            else:
                nc.scalar.activation(t2[:, :, :], t1[:, :, :], ACT.Exp).then_inc(act_out, 1)


def latent(nc, psum, name, xn, u_t_dram, u_dram, v_dram, gamma_dram, gates_t, x):
    E = 64
    with ExitStack() as ctx:
        def sb(n, shape, dt=F32):
            return ctx.enter_context(nc.sbuf_tensor(f"{name}_{n}", shape, dt))

        sem = stage_semaphores(nc, ctx, name)

        u_t = sb("u_t", [P, E])
        uv = sb("uv", [E, 2, P])
        squares = sb("squares", [E, 2, P])
        length = sb("length", [E, 2])
        root = sb("root", [E, 2])
        inverse = sb("inverse", [E, 2])
        both = sb("both", [E, 1])
        gamma = sb("gamma", [P, 1])
        mixed = sb("mixed", [E, CH, CW])
        w_in = sem("w_in")
        step = sem("step")
        length_ready = sem("length_ready")
        root_ready = sem("root_ready")
        h_ready = sem("h_ready")
        mixed_ready = sem("mixed_ready")
        y_ready = sem("y_ready")
        x_ready = sem("x_ready")
        block = ctx.enter_context(nc.Block())

        @block.sync
        def _(sp):
            for dst, src in ((u_t[:, :], u_t_dram), (uv[:, 0, :], u_dram), (uv[:, 1, :], v_dram),
                             (gamma[:, :], gamma_dram)):
                sp.dma_start(dst, src).then_inc(w_in, 16)

        @block.tensor
        def _(pe):
            pe.wait_ge(w_in, 64)
            for c in range(CH):
                nc.tensor.matmul(psum[0:E, c, :], u_t[:, :], xn[:, c * CW:(c + 1) * CW], start=True,
                                 stop=True).then_inc(h_ready, 1)
            for c in range(CH):
                pe.wait_ge(mixed_ready, c + 1)
                nc.tensor.matmul(psum[:, CH + c, :], uv[:, 1, :], mixed[:, c, :], start=True,
                                 stop=True).then_inc(y_ready, 1)

        @block.scalar
        def _(act):
            act.wait_ge(length_ready, 1)
            nc.scalar.activation(root[:, :], length[:, :], ACT.Sqrt).then_inc(root_ready, 1)

        @block.vector
        def _(dve):
            count = [0]

            def link(ins):
                count[0] += 1
                ins.then_inc(step, 1)
                dve.wait_ge(step, count[0])

            dve.wait_ge(w_in, 64)
            link(nc.vector.tensor_tensor(squares[:, :, :], uv[:, :, :], uv[:, :, :], ALU.mult))
            nc.vector.tensor_reduce(length[:, :], squares[:, :, :], AX.X, ALU.add).then_inc(length_ready, 1)
            dve.wait_ge(root_ready, 1)
            link(nc.vector.tensor_scalar(length[:, :], root[:, :], 1e-6, None, ALU.max))
            link(nc.vector.reciprocal(inverse[:, :], length[:, :]))
            link(nc.vector.tensor_tensor(both[:, :], inverse[:, 0:1], inverse[:, 1:2], ALU.mult))
            for c in range(CH):
                dve.wait_ge(h_ready, c + 1)
                nc.vector.scalar_tensor_tensor(mixed[:, c, :], psum[0:E, c, :], both[:, 0:1],
                                               gates_t[0:E, c * CW:(c + 1) * CW], ALU.mult,
                                               ALU.mult).then_inc(mixed_ready, 1)
            for c in range(CH):
                dve.wait_ge(y_ready, c + 1)
                at = slice(c * CW, (c + 1) * CW)
                nc.vector.scalar_tensor_tensor(x[:, at], psum[:, CH + c, :], gamma[:, 0:1], x[:, at],
                                               ALU.mult, ALU.add).then_inc(x_ready, 1)


def experts(nc, psum, name, t, residual, gates_t, gates_dram, w1_dram, b1_dram, w2_dram, b2_dram, x, kind):
    E, HB = 8, 4
    OB = 4 if kind == "gelu" else 2
    with ExitStack() as ctx:
        def sb(n, shape, dt=F32):
            return ctx.enter_context(nc.sbuf_tensor(f"{name}_{n}", shape, dt))

        sem = stage_semaphores(nc, ctx, name)

        w1 = sb("w1", [P, E, HB * P])
        w2 = sb("w2", [P, E, OB, P])
        b1 = sb("b1", [P, E * HB])
        b2 = sb("b2", [E, P])
        gate = sb("gate", [P, E, CW])
        hidden = sb("hidden", [P, OB, CW])
        gated = sb("gated", [P, 2, CW])
        total = sb("total", [P, CW])
        extra = sb("extra", [P, CW])
        glu = sb("glu", [P, 2, CW])
        sig = sb("sig", [P, 2, CW])
        lin = sb("lin", [P, 2, CW])
        prod = sb("prod", [P, 2, CW])
        w_in = [sem(f"w_in{e}") for e in range(E)]
        b_in = sem("b_in")
        gates_out = sem("gates_out")
        gate_in = sem("gate_in")
        h_ready = sem("h_ready")
        h_taken = sem("h_taken")
        h_done = sem("h_done")
        y_part = sem("y_part")
        y_taken = sem("y_taken")
        bias_ready = sem("bias_ready")
        total_step = sem("total_step")
        extra_ready = sem("extra_ready")
        x_ready = sem("x_ready")
        glu_ready = sem("glu_ready")
        sig_ready = sem("sig_ready")
        lin_ready = sem("lin_ready")
        prod_ready = sem("prod_ready")
        block = ctx.enter_context(nc.Block())
        order = [0, 1, 2, 3] if kind == "gelu" else [0, 2, 1, 3]
        NY = E * OB
        NH = E * HB

        def over_chunks(eng, body):
            body(0)
            with eng.Fori(1, CH) as c:
                body(c)

        @block.sync
        def _(sp):
            sp.dma_start(gates_dram[:, :], gates_t[0:E, :]).then_inc(gates_out, 16)
            sp.dma_start(b1[:, :], b1_dram).then_inc(b_in, 16)
            sp.dma_start(b2[:, :], b2_dram).then_inc(b_in, 16)
            for e in range(E):
                sp.dma_start(w1[:, e, :], w1_dram[:, e, :]).then_inc(w_in[e], 16)
                sp.dma_start(w2[:, e, :, :], w2_dram[:, e, :, :]).then_inc(w_in[e], 16)
            sp.wait_ge(gates_out, 16)

            def chunk(c):
                after(sp, y_taken, c * E)
                sp.dma_start(gate[:, :, :], gates_dram[:, bass.ds(c * CW, CW)].partition_broadcast(P)
                             ).then_inc(gate_in, 16)
            over_chunks(sp, chunk)

        @block.tensor
        def _(pe):
            def out(c, e, j):
                pe.wait_ge(h_done, c * NY + (e * OB + j + 1))
                if j == 0:
                    after(pe, y_taken, c * E + (e - 1))
                nc.tensor.matmul(psum[:, 4 + e % 2, :], w2[:, e, j, :], hidden[:, j, :], start=j == 0,
                                 stop=j == OB - 1).then_inc(y_part, 1)

            def chunk(c):
                pe.wait_ge(b_in, 32)
                after(pe, extra_ready, c)
                nc.tensor.matmul(psum[:, 6, :], b2[:, :], gates_t[0:E, bass.ds(c * CW, CW)], start=True,
                                 stop=True).then_inc(bias_ready, 1)
                waiting = []
                for e in range(E):
                    pe.wait_ge(w_in[e], 32)
                    for i, j in enumerate(order):
                        k = e * HB + i
                        if kind == "gelu":
                            after(pe, h_done, c * NH + (k - 3))
                        else:
                            after(pe, h_taken, c * (NH // 2) + (k // 2 - 1))
                        nc.tensor.matmul(psum[:, k % 4, :], w1[:, e, j * P:(j + 1) * P],
                                         t[:, bass.ds(c * CW, CW)], start=True, stop=True).then_inc(h_ready, 1)
                        if kind == "gelu":
                            waiting.append((e, j))
                            if len(waiting) > 2:
                                out(c, *waiting.pop(0))
                        else:
                            if j >= 2:
                                waiting.append((e, j - 2))
                                if len(waiting) > 2:
                                    out(c, *waiting.pop(0))
                for e, j in waiting:
                    out(c, e, j)
            over_chunks(pe, chunk)

        @block.scalar
        def _(act):
            act.wait_ge(b_in, 32)

            def chunk(c):
                for e in range(E):
                    if kind == "gelu":
                        for j in range(HB):
                            n = c * NH + (e * HB + j)
                            act.wait_ge(h_ready, n + 1)
                            after(act, y_part, n - HB + 1)
                            nc.scalar.activation(hidden[:, j, :], psum[:, j, :], ACT.Gelu,
                                                 bias=b1[:, e * HB + j:e * HB + j + 1]).then_inc(h_done, 1)
                    else:
                        for j in range(2):
                            n = c * NY + (e * 2 + j)
                            act.wait_ge(glu_ready, n + 1)
                            after(act, prod_ready, n - 1)
                            nc.scalar.activation(sig[:, j, :], glu[:, j, :], ACT.Sigmoid,
                                                 scale=1.702).then_inc(sig_ready, 1)
            over_chunks(act, chunk)

        @block.vector
        def _(dve):
            dve.wait_ge(b_in, 32)

            def take(c, e):
                dve.wait_ge(y_part, c * NY + (e * OB + OB))
                after(dve, total_step, c * E + (e - 1))
                nc.vector.tensor_tensor(gated[:, e % 2, :], psum[:, 4 + e % 2, :], gate[:, e, :],
                                        ALU.mult).then_inc(y_taken, 1)

            def chunk(c):
                at = bass.ds(c * CW, CW)
                dve.wait_ge(bias_ready, c + 1)
                after(dve, total_step, c * E)
                nc.vector.tensor_tensor(extra[:, :], psum[:, 6, :], residual[:, at],
                                        ALU.add).then_inc(extra_ready, 1)
                dve.wait_ge(gate_in, (c + 1) * 16)
                for e in range(E):
                    if kind == "swiglu":
                        for j in range(2):
                            n = c * NY + (e * 2 + j)
                            m = c * NH + (e * HB + 2 * j)
                            bank = (e * HB + 2 * j) % 4
                            dve.wait_ge(h_ready, m + 1)
                            after(dve, prod_ready, n - 1)
                            nc.vector.tensor_scalar(glu[:, j, :], psum[:, bank, :],
                                                    b1[:, e * HB + j:e * HB + j + 1], 7.0, ALU.add,
                                                    ALU.min).then_inc(glu_ready, 1)
                            dve.wait_ge(h_ready, m + 2)
                            dve.wait_ge(glu_ready, n + 1)
                            after(dve, h_done, n - 1)
                            nc.vector.tensor_scalar(lin[:, j, :], psum[:, bank + 1, :],
                                                    b1[:, e * HB + 2 + j:e * HB + 3 + j], 7.0, ALU.add,
                                                    ALU.min).then_inc(h_taken, 1)
                            dve.wait_ge(h_taken, n + 1)
                            nc.vector.tensor_scalar(lin[:, j, :], lin[:, j, :], -7.0, 1.0, ALU.max,
                                                    ALU.add).then_inc(lin_ready, 1)
                            dve.wait_ge(sig_ready, n + 1)
                            nc.vector.tensor_tensor(prod[:, j, :], glu[:, j, :], sig[:, j, :],
                                                    ALU.mult).then_inc(prod_ready, 1)
                    if e:
                        take(c, e - 1)
                take(c, E - 1)
            over_chunks(dve, chunk)

        @block.gpsimd
        def _(pool):
            def add_up(c, e):
                pool.wait_ge(y_taken, c * E + (e + 1))
                if e == 0:
                    pool.wait_ge(extra_ready, c + 1)
                    after(pool, x_ready, c)
                    nc.gpsimd.tensor_tensor(total[:, :], extra[:, :], gated[:, 0, :],
                                            ALU.add).then_inc(total_step, 1)
                else:
                    pool.wait_ge(total_step, c * E + e)
                    nc.gpsimd.tensor_tensor(total[:, :], total[:, :], gated[:, e % 2, :],
                                            ALU.add).then_inc(total_step, 1)

            def chunk(c):
                for e in range(E):
                    if kind == "swiglu":
                        for j in range(2):
                            n = c * NY + (e * 2 + j)
                            pool.wait_ge(prod_ready, n + 1)
                            pool.wait_ge(lin_ready, n + 1)
                            after(pool, y_part, n - 1)
                            nc.gpsimd.tensor_tensor(hidden[:, j, :], prod[:, j, :], lin[:, j, :],
                                                    ALU.mult).then_inc(h_done, 1)
                    if e:
                        add_up(c, e - 1)
                add_up(c, E - 1)
                at = bass.ds(c * CW, CW)
                pool.wait_ge(total_step, (c + 1) * E)
                nc.gpsimd.tensor_tensor(x[:, at], x[:, at], total[:, :], ALU.add).then_inc(x_ready, 1)
            over_chunks(pool, chunk)


def block_stack(nc, a, out):
    with ExitStack() as ctx:
        psum = ctx.enter_context(nc.psum_tensor("psum", [P, 8, CW], F32))
        x = ctx.enter_context(nc.sbuf_tensor("x", [P, S], F32))
        xn = ctx.enter_context(nc.sbuf_tensor("xn", [P, S], F32))
        ident = ctx.enter_context(nc.sbuf_tensor("ident", [P, P], F32))
        mean_w = ctx.enter_context(nc.sbuf_tensor("mean_w", [P, P], F32))
        pick = ctx.enter_context(nc.sbuf_tensor("pick", [P, CH * P], F32))
        loaded = ctx.enter_context(nc.semaphore("loaded"))

        def dram(name, shape, dt=F32):
            return nc.dram_tensor(name, shape, dt).ap()

        with nc.Block() as block:
            @block.sync
            def _(sp):
                sp.dma_start(x[:, :], a["x_t"]).then_inc(loaded, 16)
                sp.dma_start(ident[:, :], a["identity"]).then_inc(loaded, 16)
                sp.dma_start(pick[:, :], a["pick"]).then_inc(loaded, 16)
                sp.wait_ge(loaded, 48)

            @block.vector
            def _(dve):
                nc.vector.memset(mean_w[:, :], 1.0 / P)

        def narrow_attention(n, jobs, rope, q_ring, k_res, q_dram, k_dram):
            o_dram = dram(f"o{n}", (H, 9, S))
            with nc.sbuf_tensor(f"v_all{n}", [P, TT, P], F32) as v_all, \
                    nc.sbuf_tensor(f"w_v{n}", [P, P], F32) as w_v:
                project(nc, psum, f"proj{n}", xn, jobs, rope, w_v[:, :], a[f"l{n}_wv"])
                attend(nc, psum, ident, xn, w_v, P, v_all, q_ring, k_res, q_dram, k_dram, o_dram, False,
                       8 ** -0.5, f"att{n}")
            project_out(nc, psum, f"out{n}", o_dram, 8, a[f"l{n}_wo"], a[f"l{n}_bo"], a[f"l{n}_bv"],
                        a["spread_narrow"], x)

        with nc.sbuf_tensor("q_ring", [P, 4 * S], BF16) as q_ring, nc.sbuf_tensor("k_res", [P, H * S], BF16) as k_res:
            preset(nc, "set0", q_ring, k_res, False)
            normalise(nc, psum, "norm0a", x, xn, mean_w, pick, 1e-5)
            q, k = dram("q0", (3, P, S), BF16), dram("k0", (3, P, S), BF16)
            narrow_attention(0, [(a["l0_wq"], a["l0_bq"], None, None, q), (a["l0_wk"], a["l0_bk"], None, None, k)],
                             None, q_ring, k_res, q, k)
            normalise(nc, psum, "norm0f", x, xn, mean_w, pick, 1e-5)
            with nc.sbuf_tensor("gates0", [64, S], F32) as gates_t:
                with nc.sbuf_tensor("router_in0", [P, S], F32) as router_in:
                    normalise(nc, psum, "norm0r", xn, router_in, mean_w, pick, 1e-5, gain=a["l0_ln_g"],
                              shift=a["l0_ln_b"])
                    route(nc, psum, "route0", router_in, a["l0_router"], a["l0_router_b"], 64, gates_t, ident,
                          "latent")
                latent(nc, psum, "latent0", xn, a["l0_u_t"], a["l0_u"], a["l0_v"], a["l0_gamma"], gates_t, x)
            mlp(nc, psum, "mlp0", xn, a["l0_w1"], None, a["l0_w2"], None, x)

            normalise(nc, psum, "norm1a", x, xn, mean_w, pick, 1e-5)
            q, k = dram("q1", (3, P, S), BF16), dram("k1", (3, P, S), BF16)
            narrow_attention(1, [(a["l1_wq"], a["l1_bq"], a["l1_wq_turned"], a["l1_bq_turned"], q),
                                 (a["l1_wk"], a["l1_bk"], a["l1_wk_turned"], a["l1_bk_turned"], k)],
                             (a["l1_cos"], a["l1_sin"]), q_ring, k_res, q, k)
            normalise(nc, psum, "norm1f", x, xn, mean_w, pick, 1e-5)
            mlp(nc, psum, "mlp1", xn, a["l1_w1"], a["l1_b1"], a["l1_w2"], a["l1_b2"], x)

        normalise(nc, psum, "norm2a", x, xn, mean_w, pick, 1e-5)
        q, k, o = dram("q2", (2, 8 * P, S), F16), dram("k2", (2, 2 * P, S), F16), dram("o2", (H, 65, S))
        jobs = [(a["l2_wq"][:, i * P:(i + 1) * P], None, a["l2_wq_turned"][:, i * P:(i + 1) * P],
                 None, q[:, i * P:(i + 1) * P, :]) for i in range(8)]
        jobs += [(a["l2_wk"][:, i * P:(i + 1) * P], None, a["l2_wk_turned"][:, i * P:(i + 1) * P],
                  None, k[:, i * P:(i + 1) * P, :]) for i in range(2)]
        with nc.sbuf_tensor("v_all2", [P, TT, 2 * P], F32) as v_all, \
                nc.sbuf_tensor("w_v2", [P, 2 * P], F32) as w_v, nc.sbuf_tensor("exp_scale", [P, 1], F32) as exp_scale:
            project(nc, psum, "proj2", xn, jobs, (a["l2_cos"], a["l2_sin"]), w_v[:, :], a["l2_wv"], mean_w,
                    exp_scale, 8)
            with nc.sbuf_tensor("q_ring2", [P, 4 * 2 * S], F16) as q_ring, \
                    nc.sbuf_tensor("k_res2", [P, 4 * 2 * S], F16) as k_res:
                preset(nc, "set2", q_ring, k_res, True)
                attend(nc, psum, ident, xn, w_v, 2 * P, v_all, q_ring, k_res, q, k, o, True, exp_scale[:, :], "att2")
        project_out(nc, psum, "out2", o, 64, a["l2_wo"], None, None, a["spread_wide"], x)
        normalise(nc, psum, "norm2f", x, xn, mean_w, pick, 1e-5)
        with nc.sbuf_tensor("gates2", [8, S], F32) as gates_t, nc.sbuf_tensor("expert_in2", [P, S], F32) as t:
            normalise(nc, psum, "norm2e", xn, t, mean_w, pick, 1e-5, gain=a["l2_gamma"], shift=a["l2_beta"])
            route(nc, psum, "route2", t, a["l2_gate"], None, 8, gates_t, ident, "probs")
            experts(nc, psum, "moe2", t, xn, gates_t, dram("gates2_dram", (8, S)), a["l2_w1"], a["l2_b1"], a["l2_w2"],
                    a["l2_b2"], x, "gelu")

        with nc.sbuf_tensor("q_ring3", [P, 4 * S], BF16) as q_ring, nc.sbuf_tensor("k_res3", [P, H * S], BF16) as k_res:
            preset(nc, "set3", q_ring, k_res, False)
            normalise(nc, psum, "norm3a", x, xn, mean_w, pick, 1e-5)
            q, k = dram("q3", (3, P, S), BF16), dram("k3", (3, P, S), BF16)
            narrow_attention(3, [(a["l3_wq"], a["zero_col"], None, None, q),
                                 (a["identity"], a["zero_col"], None, None, k)], None, q_ring, k_res, q, k)
        normalise(nc, psum, "norm3f", x, xn, mean_w, pick, 1e-5)
        with nc.sbuf_tensor("gates3", [8, S], F32) as gates_t, nc.sbuf_tensor("expert_in3", [P, S], F32) as t:
            normalise(nc, psum, "norm3e", xn, t, mean_w, pick, 1e-5, centre=False, gain=a["l3_norm"])
            route(nc, psum, "route3", t, a["l3_gate"], a["l3_gate_b"], 8, gates_t, ident, "logits")
            experts(nc, psum, "moe3", t, xn, gates_t, dram("gates3_dram", (8, S)), a["l3_w1"], a["l3_b1"], a["l3_w2"],
                    a["l3_b2"], x, "swiglu")

        stored = ctx.enter_context(nc.semaphore("stored"))
        with nc.Block() as block:
            @block.sync
            def _(sp):
                sp.dma_start(out, x[:, :]).then_inc(stored, 16)
                sp.wait_ge(stored, 16)


def rope_tables(dim, rows, turn):
    inv = (1.0 / 10000.0 ** (np.arange(0, dim, 2, dtype=np.float32) / np.float32(dim))).astype(np.float32)
    angle = np.outer(inv, np.arange(S, dtype=np.float32)).astype(np.float32)
    d = np.arange(rows) % dim
    sign = np.where(turn(d), np.float32(-1), np.float32(1))[:, None]
    angle = angle[d % (dim // 2)]
    return np.cos(angle).astype(np.float32), (np.sin(angle) * sign).astype(np.float32)


def layout(i):
    def rows(w):
        return np.ascontiguousarray(w)

    def col(b):
        return rows(np.reshape(b, (P, 1)))

    a = {"x_t": rows(i["L0_attn_x"][0].T), "identity": np.eye(P, dtype=np.float32),
         "zero_col": np.zeros((P, 1), np.float32)}
    h = np.arange(P)[:, None]
    a["pick"] = np.repeat(h == 32 * np.arange(CH)[None, :], P, axis=1).astype(np.float32)
    a["spread_narrow"] = (np.arange(P)[None, :] // 8 == h).astype(np.float32)
    a["spread_wide"] = (np.arange(8 * P)[None, :] // 64 == h).astype(np.float32)
    for n in (0, 1):
        for s in "qkvo":
            a[f"l{n}_w{s}"] = rows(i[f"L{n}_attn_W{s}"].T)
            a[f"l{n}_b{s}"] = col(i[f"L{n}_attn_b{s}"])
    a["l0_w1"] = rows(i["L0_ffn_W1"].T)
    a["l0_w2"] = rows(i["L0_ffn_W2"].T.reshape(4, P, P).transpose(1, 0, 2))
    a["l0_ln_g"], a["l0_ln_b"] = col(i["L0_ffn_ln_g"]), col(i["L0_ffn_ln_b"])
    a["l0_router"], a["l0_router_b"] = rows(i["L0_ffn_router_W"].T), i["L0_ffn_router_b"]
    a["l0_u_t"], a["l0_u"], a["l0_v"] = rows(i["L0_ffn_raw_U"].T), i["L0_ffn_raw_U"], i["L0_ffn_raw_V"]
    a["l0_gamma"] = col(i["L0_ffn_gamma"])
    pair = np.arange(P) ^ 1
    for s in "qk":
        a[f"l1_w{s}_turned"] = rows(i[f"L1_attn_W{s}"][pair].T)
        a[f"l1_b{s}_turned"] = col(i[f"L1_attn_b{s}"][pair])
    a["l1_cos"], a["l1_sin"] = rope_tables(8, P, lambda d: d % 2 == 0)
    a["l1_w1"] = i["L1_ffn_w1"]
    a["l1_b1"] = rows(i["L1_ffn_b1"].reshape(4, P).T)
    a["l1_w2"] = rows(i["L1_ffn_w2"].reshape(4, P, P).transpose(1, 0, 2))
    a["l1_b2"] = col(i["L1_ffn_b2"])
    for s in "qkv":
        a[f"l2_w{s}"] = i[f"L2_attn_W{s}"]
    for s, n in (("q", 1024), ("k", 256)):
        a[f"l2_w{s}_turned"] = rows(i[f"L2_attn_W{s}"][:, np.arange(n) ^ 32])
    a["l2_cos"], a["l2_sin"] = rope_tables(64, P, lambda d: d < 32)
    a["l2_wo"] = rows(i["L2_attn_Wo"].reshape(8, P, P).transpose(1, 0, 2))
    a["l2_gamma"], a["l2_beta"], a["l2_gate"] = col(i["L2_ffn_gamma"]), col(i["L2_ffn_beta"]), i["L2_ffn_gate_w"]
    a["l2_w1"] = rows(i["L2_ffn_w1"].transpose(1, 0, 2))
    a["l2_b1"] = rows(i["L2_ffn_b1"].reshape(8, 4, P).transpose(2, 0, 1).reshape(P, 32))
    a["l2_w2"] = rows(i["L2_ffn_w2"].reshape(8, 4, P, P).transpose(2, 0, 1, 3))
    a["l2_b2"] = i["L2_ffn_b2"]
    wq = np.zeros((P, P), np.float32)
    for n in range(H):
        wq[8 * n:8 * n + 8, 8 * n:8 * n + 8] = i["L3_attn_w_att_val"][n]
    a["l3_wq"] = wq
    a["l3_wv"], a["l3_bv"] = rows(i["L3_attn_wv_w"].T), col(i["L3_attn_wv_b"])
    a["l3_wo"], a["l3_bo"] = rows(i["L3_attn_out_w"].T), col(i["L3_attn_out_b"])
    a["l3_norm"], a["l3_gate"], a["l3_gate_b"] = col(i["L3_ffn_norm_scale"]), i["L3_ffn_gate_w"], i["L3_ffn_gate_b"]
    halves = np.concatenate([np.arange(0, 512, 2), np.arange(1, 512, 2)])
    a["l3_w1"] = rows(i["L3_ffn_mlp1_w"][:, :, halves].transpose(1, 0, 2))
    a["l3_b1"] = rows(i["L3_ffn_mlp1_b"][:, halves].reshape(8, 4, P).transpose(2, 0, 1).reshape(P, 32))
    a["l3_w2"] = rows(i["L3_ffn_mlp2_w"].reshape(8, 2, P, P).transpose(2, 0, 1, 3))
    a["l3_b2"] = i["L3_ffn_mlp2_b"]
    return a


def kernel(**inputs):
    import concourse.bacc as _bacc
    from concourse.bass_utils import run_bass_kernel_spmd as _run

    nc = _bacc.Bacc("TRN2", target_bir_lowering=False, num_devices=1)
    arrays, args = {}, {}
    for name, value in layout({k: np.asarray(v) for k, v in inputs.items()}).items():
        value = np.ascontiguousarray(value)
        arrays[f"in_{name}"] = value
        args[name] = nc.dram_tensor(f"in_{name}", value.shape, mybir.dt.from_np(value.dtype),
                                    kind="ExternalInput").ap()
    out = nc.dram_tensor("out_y_t", (P, S), F32, kind="ExternalOutput").ap()
    block_stack(nc, args, out)
    r = _run(nc, [arrays], core_ids=[0])
    return np.ascontiguousarray(r.results[0]["out_y_t"].T)[None]
```

```python
from contextlib import ExitStack

import numpy as np

import concourse.bass as bass
from concourse import mybir

ALU = mybir.AluOpType
ACT = mybir.ActivationFunctionType
AX = mybir.AxisListType
F32 = mybir.dt.float32
BF16 = mybir.dt.bfloat16
F16 = mybir.dt.float16

P = 128
S = 2048
H = 16
CW = 512
CH = S // CW
TT = S // P
LEAD = 5
FULL = TT - LEAD
TURN = FULL + 1
QK_BOUND = 2.0 ** 10
MAX_UNIT = 2.0 ** 12
ONE_PAIR = float(np.array([0x3F803F80], np.uint32).view(np.float32)[0])


def stage_semaphores(nc, ctx, name):
    taken = []

    def clear():
        nc.clear_and_free_semaphores(taken)
        nc.all_engine_barrier()

    def sem(n):
        taken.append(nc.alloc_semaphore(f"{name}_{n}"))
        return taken[-1]

    ctx.callback(clear)
    return sem


def after(eng, sem, value):
    if not (isinstance(value, int) and value <= 0):
        eng.wait_ge(sem, value)


class Shape:

    def __init__(self, wide, scale, ident, group, blocks, dtype, v_cols, v_dims, order, max_row0, max_scale,
                 max_banks, out_bank0, out_banks, o_rows, q_loads, k_loads):
        self.wide = wide
        self.scale = scale
        self.ident = ident
        self.group = group
        self.groups = H // group
        self.blocks = blocks
        self.dtype = dtype
        self.v_cols = v_cols
        self.v_dims = v_dims
        self.order = order
        self.max_row0 = max_row0
        self.max_scale = max_scale
        self.max_banks = max_banks
        self.out_bank0 = out_bank0
        self.out_banks = out_banks
        self.o_rows = o_rows
        self.q_loads = q_loads
        self.k_loads = k_loads


def attention_core(nc, psum, cfg, q_ring, k_res, xn, w_v, v_width, v_all, load_k, load_q, store_o, name):
    with ExitStack() as ctx:
        def sb(n, shape, dt):
            return ctx.enter_context(nc.sbuf_tensor(f"{name}_{n}", shape, dt))

        sem = stage_semaphores(nc, ctx, name)

        probs = sb("probs", [P, 2 * CH, CW], F32)
        v_head = sb("v_head", [P, TT, cfg.v_cols], F32)
        tile_max = sb("tile_max", [P, TT * CH], F32)
        neg_max = sb("neg_max", [P, TT], F32)
        max_row = sb("max_row", [TT, P], F32)
        max_rest = sb("max_rest", [TT, P], F32)
        max_rest2 = sb("max_rest2", [TT, P], F32)
        scale_row = sb("scale_row", [TT, P], F32)
        max_parts = sb("max_parts", [TT, 3, P], cfg.dtype)
        out_sb = sb("out_sb", [P, cfg.out_banks, CW], F32)
        if cfg.wide:
            ones_v = sb("ones_v", [P, 32], F32)
            sums = sb("sums", [P, CH, CW], F32)
            sum_sb = sb("sum_sb", [P, CW], F32)

        v_ready = sem("v_ready")
        v_copied = sem("v_copied")
        k_loaded = [sem(f"k_loaded{g}") for g in range(cfg.groups)]
        q_loaded = sem("q_loaded")
        scores_ready = sem("scores_ready")
        exp_done = sem("exp_done")
        pv_done = sem("pv_done")
        max_ready = sem("max_ready")
        max_taken = sem("max_taken")
        head_max = sem("head_max")
        max_turned = sem("max_turned")
        max_copied = sem("max_copied")
        split_step = sem("split_step")
        max_rows_in = sem("max_rows_in")
        consts_set = sem("consts_set")
        v_zeroed = sem("v_zeroed")
        v_head_ready = sem("v_head_ready")
        out_copied = sem("out_copied")
        out_stored = sem("out_stored")
        if cfg.wide:
            dve_added = sem("dve_added")
            pool_added = sem("pool_added")
            sum_ready = sem("sum_ready")
            sum_copied = sem("sum_copied")
            sum_stored = sem("sum_stored")

        TURN_BANK = 7
        shared = TURN_BANK in cfg.max_banks
        first_shared = cfg.max_banks.index(TURN_BANK) if shared else None
        V_BANKS = (5, 6)
        FIRST = CH * (TT + LEAD)
        PER = P // cfg.v_cols
        block = ctx.enter_context(nc.Block())

        def max_unit_of(kt):
            u = kt + LEAD
            return (1, u) if u < TT else (2, u - TT)

        def max_bank(c, early):
            return c if early else cfg.max_banks[c]

        def reuse(c):
            return next(k for k in range(1, CH + 1) if cfg.max_banks[(c - k) % CH] == cfg.max_banks[c])

        @block.tensor
        def _(pe):
            def max_tile(hm, qt, c, early=False):
                n = hm * (TT * CH) + (CH * qt + c)
                if qt == 0 and c == 0:
                    pe.wait_ge(q_loaded, (hm + 1) * (16 * cfg.q_loads))
                after(pe, max_taken, n - (CH if early else reuse(c)) + 1)
                for j in range(cfg.blocks):
                    mm = nc.tensor.matmul(
                        psum[:, max_bank(c, early), :],
                        q_ring[:, bass.ds((hm % 4) * (cfg.blocks * S) + (j * S + qt * P), P)],
                        k_res[:, bass.ds((hm // cfg.group) * (cfg.blocks * S) + (j * S + c * CW), CW)],
                        start=j == 0, stop=j == cfg.blocks - 1)
                mm.then_inc(max_ready, 1)

            def turn_max(hm):
                pe.wait_ge(head_max, hm + 1)
                if cfg.wide:
                    after(pe, sum_copied, hm - 1)
                nc.tensor.transpose(psum[0:TT, TURN_BANK, 0:P], neg_max[:, :],
                                    cfg.ident[:, :]).then_inc(max_turned, 1)

            def score_tile(h, kt, c):
                if kt == 0 and c == 0:
                    pe.wait_ge(max_rows_in, (h + 1) * 48)
                n = h * (TT * CH) + (CH * kt + c)
                after(pe, exp_done, n - CH + 1)
                for j in range(cfg.blocks):
                    mm = nc.tensor.matmul(
                        psum[:, c, :],
                        k_res[:, bass.ds((h // cfg.group) * (cfg.blocks * S) + (j * S + kt * P), P)],
                        q_ring[:, bass.ds((h % 4) * (cfg.blocks * S) + (j * S + c * CW), CW)],
                        start=j == 0, stop=j == cfg.blocks - 1)
                mm.then_inc(scores_ready, 1)

            def pv(h, kt, first):
                if kt == 0 and first == 0:
                    pe.wait_ge(v_head_ready, h + 1)
                    after(pe, out_copied, h)
                pe.wait_ge(exp_done, h * (TT * CH) + (CH * kt + first + PER))
                for c in range(first, first + PER):
                    at = cfg.v_cols * (c % PER)
                    mm = nc.tensor.matmul(psum[at:at + cfg.v_cols, cfg.out_bank0 + c // PER, :], v_head[:, kt, :],
                                          probs[:, CH * (kt % 2) + c, :], start=kt == 0, stop=kt == TT - 1)
                if first + PER == CH:
                    mm.then_inc(pv_done, 1)

            def sum_up(h, last=False):
                pe.wait_ge(dve_added, (h + 1) * (2 * (TT - 1)))
                pe.wait_ge(pool_added, (h + 1) * (2 * (TT - 1)))
                pe.wait_ge(max_copied, H if last else h + 2)
                for c in range(CH):
                    mm = nc.tensor.matmul(psum[32 * c:32 * c + 32, TURN_BANK, :], ones_v[:, :], sums[:, c, :],
                                          start=True, stop=True)
                mm.then_inc(sum_ready, 1)

            def head(h, ahead, first=False):
                for kt in range(TT):
                    d, qt = max_unit_of(kt)
                    for what, n in cfg.order:
                        if what == "max" and d <= ahead:
                            if shared and cfg.wide and n == first_shared and kt == 2 and not first:
                                pe.wait_ge(sum_copied, h)
                            if shared and n == first_shared and kt == TURN + 1:
                                pe.wait_ge(max_copied, h + 2)
                            max_tile(h + d, qt, n)
                        elif what == "score":
                            score_tile(h, kt, n)
                        elif what == "pv" and kt > 0:
                            pv(h, kt - 1, n)
                        elif what == "pv" and not first:
                            pv(h - 1, TT - 1, n)
                    tiles = (h + d) * (TT * CH) + (CH * qt + CH)
                    if cfg.wide and kt == 1 and not first:
                        if shared and d <= ahead:
                            pe.wait_ge(max_taken, tiles)
                        sum_up(h - 1)
                    if kt == TURN and ahead >= 1:
                        if shared and d <= ahead:
                            pe.wait_ge(max_taken, tiles)
                        turn_max(h + 1)

            pe.wait_ge(k_loaded[0], 16 * cfg.k_loads)
            for qt in range(TT):
                for c in range(CH):
                    max_tile(0, qt, c, early=True)
                after(pe, v_copied, qt - 1)
                nc.tensor.matmul(psum[:, V_BANKS[qt % 2], 0:v_width], xn[:, qt * P:(qt + 1) * P],
                                 w_v[:, :], start=True, stop=True).then_inc(v_ready, 1)
            if cfg.group == 1:
                pe.wait_ge(k_loaded[1], 16 * cfg.k_loads)
            for qt in range(LEAD):
                for c in range(CH):
                    max_tile(1, qt, c, early=True)
                if qt == TURN - FULL:
                    turn_max(0)
            for g in range(1, cfg.groups):
                pe.wait_ge(k_loaded[g], 16 * cfg.k_loads)
            pe.wait_ge(max_taken, FIRST)
            pe.wait_ge(v_copied, TT)
            if shared:
                pe.wait_ge(max_copied, 1)
            head(0, 2, first=True)
            with pe.Fori(1, H - 2) as h:
                head(h, 2)
            head(H - 2, 1)
            head(H - 1, 0)
            for first in range(0, CH, PER):
                pv(H - 1, TT - 1, first)
            if cfg.wide:
                sum_up(H - 1, last=True)

        @block.scalar
        def _(act):
            for t in range(TT):
                act.wait_ge(v_ready, t + 1)
                nc.scalar.copy(v_all[:, t, :], psum[:, V_BANKS[t % 2], 0:v_width]).then_inc(v_copied, 1)

            def head(h):
                for kt in range(TT):
                    for c in range(CH):
                        act.wait_ge(scores_ready, h * (TT * CH) + (CH * kt + c + 1))
                        if c == 0 and not (isinstance(h, int) and h == 0 and kt < 2):
                            act.wait_ge(pv_done, h * TT + kt - 1)
                            if cfg.wide:
                                added = 2 * (max(kt - 2, 1) if kt > 1 else kt - 1)
                                act.wait_ge(dve_added, h * (2 * (TT - 1)) + added)
                                act.wait_ge(pool_added, h * (2 * (TT - 1)) + added)
                        nc.scalar.activation(probs[:, CH * (kt % 2) + c, :], psum[:, c, :], ACT.Exp,
                                             scale=cfg.scale).then_inc(exp_done, 1)

            head(0)
            with act.Fori(1, H) as h:
                head(h)

        def add_up(eng, engine, h, kt, c, added):
            if kt == 0:
                return
            if kt == 1 and c % 2 == 0:
                after(eng, sum_ready, h)
            eng.wait_ge(exp_done, h * (TT * CH) + (CH * kt + c + 1))
            after(eng, added, h * (2 * (TT - 1)) + 2 * (kt - 2) + c % 2 + 1)
            before = probs[:, c, :] if kt == 1 else sums[:, c, :]
            engine.tensor_tensor(sums[:, c, :], before, probs[:, CH * (kt % 2) + c, :], ALU.add).then_inc(added, 1)

        @block.vector
        def _(dve):
            def take_max(hm, qt, c, early=False):
                n = hm * (TT * CH) + (CH * qt + c)
                dve.wait_ge(max_ready, n + 1)
                if qt == 0 and c == 0:
                    after(dve, head_max, hm)
                nc.vector.reduce_max(tile_max[:, CH * qt + c:CH * qt + c + 1],
                                     psum[:, max_bank(c, early), :], AX.X).then_inc(max_taken, 1)
                if qt == TT - 1 and c == CH - 1:
                    dve.wait_ge(max_taken, n + 1)
                    after(dve, max_turned, hm)
                    nc.vector.tensor_reduce(
                        neg_max[:, :], tile_max[:, :].rearrange("p (t c) -> p t c", c=CH),
                        AX.X, ALU.max, negate=True).then_inc(head_max, 1)

            def copy_row(hm):
                dve.wait_ge(max_turned, hm + 1)
                after(dve, split_step, hm * 5)
                nc.vector.tensor_copy(max_row[:, :], psum[0:TT, TURN_BANK, 0:P]).then_inc(max_copied, 1)

            def copy_out(h):
                dve.wait_ge(pv_done, (h + 1) * TT)
                after(dve, out_stored, h * (16 * CH))
                nc.vector.tensor_copy(out_sb[:, :, :], psum[:, cfg.out_bank0:cfg.out_bank0 + cfg.out_banks, :]
                                      ).then_inc(out_copied, 1)

            def copy_sum(h):
                dve.wait_ge(sum_ready, h + 1)
                after(dve, sum_stored, h * 16)
                nc.vector.tensor_copy(sum_sb[:, :], psum[:, TURN_BANK, :]).then_inc(sum_copied, 1)

            def head(h, ahead, first=False):
                for kt in range(TT):
                    d, qt = max_unit_of(kt)
                    for c in range(CH):
                        if d <= ahead:
                            take_max(h + d, qt, c)
                        if cfg.wide and c < 2:
                            if kt > 0:
                                add_up(dve, nc.vector, h, kt - 1, c, dve_added)
                            elif not first:
                                add_up(dve, nc.vector, h - 1, TT - 1, c, dve_added)
                    if kt == TURN and ahead >= 1:
                        copy_row(h + 1)
                    if kt == 0 and not first:
                        copy_out(h - 1)
                    if cfg.wide and kt == 1 and not first:
                        copy_sum(h - 1)

            for qt in range(TT):
                for c in range(CH):
                    take_max(0, qt, c, early=True)
            for qt in range(LEAD):
                for c in range(CH):
                    take_max(1, qt, c, early=True)
                if qt == TURN - FULL:
                    copy_row(0)
            if cfg.wide:
                dve.wait_ge(consts_set, 2)
            head(0, 2, first=True)
            with dve.Fori(1, H - 2) as h:
                head(h, 2)
            head(H - 2, 1)
            head(H - 1, 0)
            if cfg.wide:
                for c in range(2):
                    add_up(dve, nc.vector, H - 1, TT - 1, c, dve_added)
            copy_out(H - 1)
            if cfg.wide:
                copy_sum(H - 1)

        @block.gpsimd
        def _(pool):
            nc.gpsimd.memset(scale_row[:, :], cfg.max_scale).then_inc(consts_set, 1)
            if cfg.wide:
                nc.gpsimd.memset(ones_v[:, :], 1.0).then_inc(consts_set, 1)
            else:
                nc.gpsimd.memset(v_head[:, :, :], 0.0).then_inc(v_zeroed, 1)
                pool.wait_ge(v_zeroed, 1)
                nc.gpsimd.memset(v_head[:, :, cfg.v_dims:cfg.v_dims + 1], 1.0).then_inc(consts_set, 1)
            pool.wait_ge(consts_set, 2)

            def fill_v(h):
                after(pool, pv_done, h * TT)
                nc.gpsimd.tensor_copy(v_head[:, :, 0:cfg.v_dims],
                                      v_all[:, :, bass.ds((h // cfg.group) * cfg.v_dims, cfg.v_dims)]
                                      ).then_inc(v_head_ready, 1)

            def split_max(hm):
                k = hm * 5
                pool.wait_ge(max_copied, hm + 1)
                after(pool, max_rows_in, hm * 48)
                nc.gpsimd.tensor_tensor(max_parts[:, 0, :], max_row[:, :], scale_row[:, :],
                                        ALU.mult).then_inc(split_step, 1)
                nc.gpsimd.tensor_tensor(max_rest[:, :], max_row[:, :], scale_row[:, :],
                                        ALU.mult).then_inc(split_step, 1)
                pool.wait_ge(split_step, k + 2)
                nc.gpsimd.tensor_tensor(max_rest2[:, :], max_rest[:, :], max_parts[:, 0, :],
                                        ALU.subtract).then_inc(split_step, 1)
                pool.wait_ge(split_step, k + 3)
                nc.gpsimd.tensor_tensor(max_parts[:, 1, :], max_rest[:, :], max_parts[:, 0, :],
                                        ALU.subtract).then_inc(split_step, 1)
                pool.wait_ge(split_step, k + 4)
                nc.gpsimd.tensor_tensor(max_parts[:, 2, :], max_rest2[:, :], max_parts[:, 1, :],
                                        ALU.subtract).then_inc(split_step, 1)

            def adds(h, kt):
                if cfg.wide:
                    for c in range(2, CH):
                        add_up(pool, nc.gpsimd, h, kt, c, pool_added)

            def head(h, ahead):
                for kt in range(TT):
                    adds(h, kt)
                    if kt == TURN and ahead >= 1:
                        split_max(h + 1)
                if ahead >= 1:
                    fill_v(h + 1)

            pool.wait_ge(v_copied, TT)
            fill_v(0)
            split_max(0)
            head(0, 1)
            with pool.Fori(1, H - 1) as h:
                head(h, 1)
            head(H - 1, 0)

        @block.sync
        def _(sp):
            def put_max_rows(hm):
                sp.wait_ge(split_step, (hm + 1) * 5)
                for j in range(3):
                    dst = q_ring[cfg.max_row0 + j:cfg.max_row0 + j + 1,
                                 bass.ds((hm % 4) * (cfg.blocks * S) + (cfg.blocks - 1) * S, S)]
                    sp.dma_start(dst, max_parts[:, j, :]).then_inc(max_rows_in, 16)

            def q_in(h):
                after(sp, exp_done, (h - 3) * (TT * CH))
                after(sp, q_loaded, h * (16 * cfg.q_loads))
                load_q(sp, h, q_loaded)

            def put_out(h):
                sp.wait_ge(out_copied, h + 1)
                for c in range(CH):
                    store_o(sp, h, c, out_sb[cfg.v_cols * (c % PER):cfg.v_cols * (c % PER) + cfg.o_rows,
                                             c // PER, :]).then_inc(out_stored, 16)
                if cfg.wide:
                    sp.wait_ge(sum_copied, h + 1)
                    store_o(sp, h, None, sum_sb[0:P:32, :]).then_inc(sum_stored, 16)

            load_k(sp, 0, k_loaded[0])
            q_in(0)
            load_k(sp, 1, k_loaded[1])
            q_in(1)
            for g in range(2, cfg.groups):
                load_k(sp, g, k_loaded[g])
            q_in(2)
            q_in(3)
            put_max_rows(0)
            put_max_rows(1)
            with sp.Fori(1, H - 3) as h:
                q_in(h + 3)
                put_out(h - 1)
                put_max_rows(h + 1)
            for h in range(H - 3, H - 1):
                put_out(h - 1)
                put_max_rows(h + 1)
            put_out(H - 2)
            put_out(H - 1)
            sp.wait_ge(out_stored, H * 16 * CH)
            if cfg.wide:
                sp.wait_ge(sum_stored, H * 16)


def attend(nc, psum, ident, xn, w_v, v_width, v_all, q_ring, k_res, q_dram, k_dram, o_dram, wide, scale, name):
    if wide:
        order = [("max", 0), ("score", 0), ("score", 1), ("max", 1), ("score", 2), ("score", 3), ("max", 2),
                 ("pv", 0), ("max", 3), ("pv", 2)]
        cfg = Shape(wide=True, scale=scale, ident=ident, group=4, blocks=2, dtype=F16, v_cols=64, v_dims=64,
                    order=order, max_row0=64, max_scale=1.0 / MAX_UNIT, max_banks=(4, 7, 4, 7), out_bank0=5,
                    out_banks=2, o_rows=64, q_loads=3, k_loads=3)

        def load_q(sp, h, loaded):
            at = (h % 4) * (2 * S)
            rows = bass.ds(h * 64, 64)
            sp.dma_start(q_ring[:, bass.ds(at, S)], q_dram[:, rows, :]).then_inc(loaded, 16)
            sp.dma_start(q_ring[0:64, bass.ds(at + S, S)], q_dram[0:1, rows, :]).then_inc(loaded, 16)
            sp.dma_start(q_ring[64:67, bass.ds(at + S, S)], q_ring[96:99, bass.ds(at + S, S)]).then_inc(loaded, 16)

        def load_k(sp, g, loaded):
            at = g * 2 * S
            rows = slice(g * 64, g * 64 + 64)
            sp.dma_start(k_res[0:64, at:at + S], k_dram[0, rows, :]).then_inc(loaded, 16)
            sp.dma_start(k_res[64:128, at:at + S], k_dram[0, rows, :]).then_inc(loaded, 16)
            sp.dma_start(k_res[0:64, at + S:at + 2 * S], k_dram[1, rows, :]).then_inc(loaded, 16)

        def store_o(sp, h, c, src):
            if c is None:
                return sp.dma_start(o_dram[bass.ds(h, 1), 64, :], src)
            return sp.dma_start(o_dram[bass.ds(h, 1), 0:64, c * CW:(c + 1) * CW], src)
    else:
        order = [("max", 0), ("score", 0), ("score", 1), ("max", 1), ("score", 2), ("score", 3), ("max", 2),
                 ("max", 3), ("pv", 0)]
        cfg = Shape(wide=False, scale=scale, ident=ident, group=1, blocks=1, dtype=BF16, v_cols=32, v_dims=8,
                    order=order, max_row0=48, max_scale=1.0, max_banks=(4, 5, 4, 7), out_bank0=6,
                    out_banks=1, o_rows=9, q_loads=4, k_loads=3)

        def load_q(sp, h, loaded):
            at = (h % 4) * S
            rows = bass.ds(h * 8, 8)
            for part, n, r in ((0, 3, 0), (1, 2, 24), (2, 1, 40)):
                sp.dma_start(q_ring[r:r + 8 * n, bass.ds(at, S)],
                             q_dram[part:part + 1, rows, :].broadcast_to([n, 8, S])).then_inc(loaded, 16)
            sp.dma_start(q_ring[48:51, bass.ds(at, S)], q_ring[64:67, bass.ds(at, S)]).then_inc(loaded, 16)

        def load_k(sp, h, loaded):
            rows = slice(h * 8, h * 8 + 8)
            for n, r in ((3, 0), (2, 24), (1, 40)):
                sp.dma_start(k_res[r:r + 8 * n, h * S:(h + 1) * S],
                             k_dram[0:n, rows, :]).then_inc(loaded, 16)

        def store_o(sp, h, c, src):
            return sp.dma_start(o_dram[bass.ds(h, 1), :, c * CW:(c + 1) * CW], src)
    attention_core(nc, psum, cfg, q_ring, k_res, xn, w_v, v_width, v_all, load_k, load_q, store_o, name)


def normalise(nc, psum, name, src, dst, mean_w, pick, eps, centre=True, gain=None, shift=None):
    with ExitStack() as ctx:
        def sb(n, shape, dt=F32):
            return ctx.enter_context(nc.sbuf_tensor(f"{name}_{n}", shape, dt))

        sem = stage_semaphores(nc, ctx, name)

        centred = sb("centred", [P, S]) if centre else src
        squares = sb("squares", [P, S])
        spread = sb("spread", [P, CW])
        scale = sb("scale", [P, CW])
        eps_col = sb("eps_col", [P, 1])
        affine = sb("affine", [P, 2])
        affine_in = sem("affine_in")
        eps_set = sem("eps_set")
        mean_ready = sem("mean_ready")
        centred_ready = sem("centred_ready")
        squares_ready = sem("squares_ready")
        var_ready = sem("var_ready")
        spread_ready = sem("spread_ready")
        scale_ready = sem("scale_ready")
        picked = sem("picked")
        unit_ready = sem("unit_ready")
        VAR_BANK = CH

        def half(k):
            return slice(k * CW // 2, (k + 1) * CW // 2)

        block = ctx.enter_context(nc.Block())

        def part(t, c):
            return t[:, c * CW:(c + 1) * CW]

        @block.sync
        def _(sp):
            if gain is not None:
                sp.dma_start(affine[:, 0:1], gain).then_inc(affine_in, 16)
                if shift is not None:
                    sp.dma_start(affine[:, 1:2], shift).then_inc(affine_in, 16)

        @block.tensor
        def _(pe):
            if centre:
                for c in range(CH):
                    nc.tensor.matmul(psum[:, c, :], mean_w[:, :], part(src, c), start=True,
                                     stop=True).then_inc(mean_ready, 1)
            for c in range(CH):
                pe.wait_ge(squares_ready, c + 1)
                nc.tensor.matmul(psum[32 * c:32 * c + 32, VAR_BANK, :], mean_w[:, 0:32], part(squares, c),
                                 start=True, stop=True).then_inc(var_ready, 1)
            if centre:
                pe.wait_ge(centred_ready, CH)
            for k in range(2):
                pe.wait_ge(scale_ready, k + 1)
                for c in range(CH):
                    nc.tensor.matmul(psum[:, k * CH + c, 0:CW // 2], pick[:, c * P:(c + 1) * P],
                                     scale[:, half(k)], start=True, stop=True).then_inc(picked, 1)

        @block.scalar
        def _(act):
            for c in range(CH):
                if centre:
                    act.wait_ge(centred_ready, c + 1)
                nc.scalar.activation(part(squares, c), part(centred, c), ACT.Square).then_inc(squares_ready, 1)
            act.wait_ge(eps_set, 1)
            act.wait_ge(var_ready, CH)
            nc.scalar.activation(spread[:, :], psum[:, VAR_BANK, :], ACT.Sqrt,
                                 bias=eps_col[:, :]).then_inc(spread_ready, 1)

        @block.vector
        def _(dve):
            nc.vector.memset(eps_col[:, :], eps).then_inc(eps_set, 1)
            if centre:
                for c in range(CH):
                    dve.wait_ge(mean_ready, c + 1)
                    nc.vector.tensor_tensor(part(centred, c), part(src, c), psum[:, c, :],
                                            ALU.subtract).then_inc(centred_ready, 1)
            dve.wait_ge(spread_ready, 1)
            for k in range(2):
                nc.vector.reciprocal(scale[:, half(k)], spread[:, half(k)]).then_inc(scale_ready, 1)
            if gain is not None:
                dve.wait_ge(affine_in, 16 if shift is None else 32)
            if centre:
                dve.wait_ge(centred_ready, CH)
            for k in range(2):
                for c in range(CH):
                    at = slice(c * CW + half(k).start, c * CW + half(k).stop)
                    dve.wait_ge(picked, k * CH + (c + 1))
                    if gain is None:
                        nc.vector.tensor_tensor(dst[:, at], centred[:, at], psum[:, k * CH + c, 0:CW // 2],
                                                ALU.mult).then_inc(unit_ready, 1)
                    else:
                        nc.vector.scalar_tensor_tensor(dst[:, at], centred[:, at], affine[:, 0:1],
                                                       psum[:, k * CH + c, 0:CW // 2], ALU.mult, ALU.mult
                                                       ).then_inc(unit_ready, 1)
            if shift is not None:
                for c in range(CH):
                    dve.wait_ge(unit_ready, CH + c + 1)
                    nc.vector.tensor_scalar(part(dst, c), part(dst, c), affine[:, 1:2], None, ALU.add)


def preset(eng, engine, q_ring, k_res, wide, n, done):
    half = k_res.shape[1] // 2
    q_half = q_ring.shape[1] // 2
    engine.memset(q_ring[:, n * q_half:(n + 1) * q_half].bitcast(F32), 0.0).then_inc(done, 1)
    eng.wait_ge(done, 1)
    if wide:
        for i, at in enumerate(range(n * half + S, (n + 1) * half, 2 * S)):
            engine.memset(k_res[64:P, at:at + S], MAX_UNIT).then_inc(done, 1)
            eng.wait_ge(done, i + 2)
    else:
        engine.memset(k_res[:, n * half:(n + 1) * half].bitcast(F32), ONE_PAIR).then_inc(done, 1)


def project(nc, psum, name, xn, jobs, w_loads, rope, w_v, w_v_dram, rings=None, mean_w=None, exp_scale=None,
            q_jobs=0):
    J = len(jobs)
    narrow = exp_scale is None
    R = 5 if J % 5 == 0 else 4
    n_parts = 3 if narrow else 2
    LOW_LAG = 2
    with ExitStack() as ctx:
        def sb(n, shape, dt=F32):
            return ctx.enter_context(nc.sbuf_tensor(f"{name}_{n}", shape, dt))

        sem = stage_semaphores(nc, ctx, name)

        w = sb("w", [P, J, P])
        b = sb("b", [P, J])
        w_in = sem("w_in")
        if rope is not None:
            w_turned = sb("w_turned", [P, J, P])
            b_turned = sb("b_turned", [P, J])
            cos = sb("cos", [P, S])
            sin = sb("sin", [P, S])
            by_cos = sb("by_cos", [P, R, CW])
            by_sin = sb("by_sin", [P, R, CW])
        value = sb("value", [P, R, CW])
        if narrow:
            rest = sb("rest", [P, R, CW])
        else:
            squares = sb("squares", [P, J, P])
            bound = sb("bound", [P, 2])
            power = sb("power", [P, 2])
            inverse = sb("inverse", [P, 2])
            unit = sb("unit", [P, 2])
            factor = sb("factor", [P, 2])
            both = sb("both", [P, 1])
            step = sem("step")
            squares_ready = sem("squares_ready")
            norms_ready = sem("norms_ready")
            root_ready = sem("root_ready")
        parts = sb("parts", [P, R, n_parts, CW], BF16 if narrow else F16)
        proj_ready = sem("proj_ready")
        turned_done = sem("turned_done")
        value_ready = sem("value_ready")
        high_ready = sem("high_ready")
        rest_ready = sem("rest_ready")
        mid_ready = sem("mid_ready")
        low_ready = sem("low_ready")
        weights_ready = sem("weights_ready")
        tables_in = sem("tables_in")
        v_in = sem("v_in")
        dve_set = sem("dve_set")
        pool_set = sem("pool_set")
        stored = [sem(f"stored{k}") for k in range(R)]
        block = ctx.enter_context(nc.Block())

        def count(c, n):
            return c * J + n

        def slot(c, n):
            return (c * J + n) % R if isinstance(c, int) else n % R

        def turns(c, n):
            return (c * J + n) // R if isinstance(c, int) else c * (J // R) + n // R

        def over_values(eng, steps):
            def chunk(c):
                for n in range(J):
                    for do, lag in steps:
                        if not isinstance(c, int) or c * J + n >= lag:
                            do(c, n - lag)

            if J % R == 0:
                chunk(0)
                with eng.Fori(1, CH) as c:
                    chunk(c)
            else:
                for c in range(CH):
                    chunk(c)
            for n in range(max(lag for do, lag in steps)):
                for do, lag in steps:
                    if n < lag:
                        do(CH, n - lag)

        loads = [(w[:, first:first + n, :], src) for first, n, src, turned in w_loads]
        if rope is not None:
            loads += [(w_turned[:, first:first + n, :], turned) for first, n, src, turned in w_loads]
        if narrow:
            loads += [(b[:, j:j + 1], jobs[j][0]) for j in range(J)]
            if rope is not None:
                loads += [(b_turned[:, j:j + 1], jobs[j][1]) for j in range(J)]

        @block.sync
        def _(sp):
            for dst, src in loads:
                sp.dma_start(dst, src).then_inc(w_in, 16)
            if rope is not None:
                sp.dma_start(cos[:, :], rope[0]).then_inc(tables_in, 16)
                sp.dma_start(sin[:, :], rope[1]).then_inc(tables_in, 16)
            sp.dma_start(w_v, w_v_dram).then_inc(v_in, 16)
            sp.wait_ge(v_in, 16)

            def store(c, n):
                sp.wait_ge(low_ready, count(c, n + 1))
                sp.dma_start(jobs[n % J][2][:, :, bass.ds(c * CW, CW)].rearrange("n p w -> p n w"),
                             parts[:, slot(c, n), :, :]).then_inc(stored[slot(c, n)], 16)
            over_values(sp, [(store, 0)])
            for k in range(R):
                sp.wait_ge(stored[k], 16 * ((CH * J - k + R - 1) // R))

        @block.tensor
        def _(pe):
            pe.wait_ge(w_in, 16 * len(loads))
            if not narrow:
                pe.wait_ge(squares_ready, 1)
                for first in range(0, J, 4):
                    last = min(first + 4, J)
                    mm = nc.tensor.matmul(psum[:, first // 4, 0:(last - first) * P], mean_w[:, :],
                                          squares[:, first:last, :], start=True, stop=True)
                mm.then_inc(norms_ready, 1)
                pe.wait_ge(weights_ready, 4)

            def matmul(c, n):
                after(pe, turned_done if rope is not None else value_ready, count(c, n - 1))
                x_c = xn[:, bass.ds(c * CW, CW)]
                mm = nc.tensor.matmul(psum[:, n % 2, :], w[:, n, :], x_c, start=True, stop=True)
                if rope is not None:
                    mm = nc.tensor.matmul(psum[:, 2 + n % 2, :], w_turned[:, n, :], x_c, start=True, stop=True)
                mm.then_inc(proj_ready, 1)
            over_values(pe, [(matmul, 0)])

        @block.scalar
        def _(act):
            act.wait_ge(w_in, 16 * len(loads))
            if not narrow:
                nc.scalar.activation(squares[:, :, :], w[:, :, :], ACT.Square).then_inc(squares_ready, 1)
                act.wait_ge(step, 2)
                nc.scalar.activation(bound[:, :], bound[:, :], ACT.Sqrt, scale=2.0 * P * P).then_inc(root_ready, 1)

            def biased(c, n):
                act.wait_ge(proj_ready, count(c, n + 1))
                after(act, low_ready, count(c, n - R + 1))
                nc.scalar.activation(value[:, slot(c, n), :], psum[:, n % 2, :], ACT.Identity,
                                     bias=b[:, n:n + 1]).then_inc(value_ready, 1)

            def high(c, n):
                act.wait_ge(value_ready, count(c, n + 1))
                after(act, stored[slot(c, n)], turns(c, n) * 16)
                nc.scalar.copy(parts[:, slot(c, n), 0, :], value[:, slot(c, n), :]).then_inc(high_ready, 1)

            def mid(c, n):
                act.wait_ge(rest_ready, count(c, n + 1))
                nc.scalar.copy(parts[:, slot(c, n), 1, :], rest[:, slot(c, n), :]).then_inc(mid_ready, 1)

            over_values(act, ([(biased, 0)] if rope is None else []) + [(high, 0)] + ([(mid, 1)] if narrow else []))

        @block.vector
        def _(dve):
            if rings is not None:
                preset(dve, nc.vector, *rings, not narrow, 0, dve_set)
            if not narrow:
                done = [0]

                def link(ins):
                    done[0] += 1
                    ins.then_inc(step, 1)
                    dve.wait_ge(step, done[0])

                dve.wait_ge(norms_ready, 1)
                nc.vector.reduce_max(bound[:, 0:1], psum[:, 0:2, :], AX.XY).then_inc(step, 1)
                nc.vector.reduce_max(bound[:, 1:2], psum[:, 2, 0:(J - q_jobs) * P], AX.X).then_inc(step, 1)
                done[0] = 2
                dve.wait_ge(root_ready, 1)
                link(nc.vector.tensor_scalar(inverse[:, :], bound[:, :], 1e-15, None, ALU.max))
                link(nc.vector.reciprocal(power[:, :], inverse[:, :]))
                link(nc.vector.tensor_scalar(unit[:, :].bitcast(mybir.dt.uint32), power[:, :].bitcast(mybir.dt.uint32),
                                             0x7F800000, None, ALU.bitwise_and))
                link(nc.vector.tensor_scalar(factor[:, :], unit[:, :], QK_BOUND, None, ALU.mult))
                link(nc.vector.tensor_tensor(both[:, :], factor[:, 0:1], factor[:, 1:2], ALU.mult))
                link(nc.vector.reciprocal(exp_scale[:, :], both[:, :]))
                link(nc.vector.tensor_scalar(exp_scale[:, :], exp_scale[:, :], 0.125, None, ALU.mult))
                for t in (w, w_turned):
                    for k, at in ((0, slice(0, q_jobs)), (1, slice(q_jobs, J))):
                        nc.vector.tensor_scalar(t[:, at, :], t[:, at, :], factor[:, k:k + 1], None,
                                                ALU.mult).then_inc(weights_ready, 1)
            dve.wait_ge(w_in, 16 * len(loads))
            if rope is not None:
                dve.wait_ge(tables_in, 32)

            def turn(c, n):
                dve.wait_ge(proj_ready, count(c, n + 1))
                after(dve, value_ready, count(c, n - R + 1))
                at = bass.ds(c * CW, CW)
                for dst, bank, bias, table in ((by_cos, n % 2, b, cos), (by_sin, 2 + n % 2, b_turned, sin)):
                    if narrow:
                        ins = nc.vector.scalar_tensor_tensor(dst[:, slot(c, n), :], psum[:, bank, :],
                                                             bias[:, n:n + 1], table[:, at], ALU.add, ALU.mult)
                    else:
                        ins = nc.vector.tensor_tensor(dst[:, slot(c, n), :], psum[:, bank, :], table[:, at], ALU.mult)
                ins.then_inc(turned_done, 1)

            def low(c, n):
                k = slot(c, n)
                if narrow:
                    dve.wait_ge(mid_ready, count(c, n + 1))
                    nc.vector.tensor_tensor(parts[:, k, 2, :], rest[:, k, :], parts[:, k, 1, :],
                                            ALU.subtract).then_inc(low_ready, 1)
                else:
                    dve.wait_ge(high_ready, count(c, n + 1))
                    nc.vector.tensor_tensor(parts[:, k, 1, :], value[:, k, :], parts[:, k, 0, :],
                                            ALU.subtract).then_inc(low_ready, 1)

            over_values(dve, [(turn, 0), (low, LOW_LAG)] if rope is not None else [(low, 0)])

        @block.gpsimd
        def _(pool):
            if rings is not None:
                preset(pool, nc.gpsimd, *rings, not narrow, 1, pool_set)

            def add(c, n):
                pool.wait_ge(turned_done, count(c, n + 1))
                after(pool, low_ready, count(c, n - R + 1))
                nc.gpsimd.tensor_tensor(value[:, slot(c, n), :], by_cos[:, slot(c, n), :], by_sin[:, slot(c, n), :],
                                        ALU.add).then_inc(value_ready, 1)

            def subtract(c, n):
                pool.wait_ge(high_ready, count(c, n + 1))
                nc.gpsimd.tensor_tensor(rest[:, slot(c, n), :], value[:, slot(c, n), :], parts[:, slot(c, n), 0, :],
                                        ALU.subtract).then_inc(rest_ready, 1)

            steps = [(add, 0)] if rope is not None else []
            if narrow:
                steps.append((subtract, 1))
            over_values(pool, steps)


def project_out(nc, psum, name, o_dram, d, w_dram, b_dram, b_v_dram, spread_dram, x):
    groups = H * d // P
    per = P // d
    SPLIT = P // H
    with ExitStack() as ctx:
        def sb(n, shape, dt=F32):
            return ctx.enter_context(nc.sbuf_tensor(f"{name}_{n}", shape, dt))

        sem = stage_semaphores(nc, ctx, name)

        w = sb("w", [P, groups, P])
        b = sb("b", [P, 1])
        b_v = sb("b_v", [P, 1])
        b_all = sb("b_all", [P, 1])
        spread_f = sb("spread_f", [P, groups * P])
        spread = sb("spread", [P, groups * P], BF16)
        sums = sb("sums", [P, S // SPLIT])
        inverse = sb("inverse", [P, S // SPLIT])
        rest = sb("rest", [P, 2, S // SPLIT])
        parts = sb("parts", [P, 3, S // SPLIT], BF16)
        inverse_row = sb("inverse_row", [P, S], BF16)
        o = sb("o", [P, groups, S])
        o_unit = sb("o_unit", [P, 2, CW])
        sums_in = sem("sums_in")
        consts_in = sem("consts_in")
        w_in = sem("w_in")
        o_in = [sem(f"o_in{g}") for g in range(groups)]
        rows_clear = sem("rows_clear")
        inverse_ready = sem("inverse_ready")
        inverse_in = sem("inverse_in")
        part_ready = sem("part_ready")
        rest_ready = sem("rest_ready")
        spread_set = sem("spread_set")
        spread_ready = sem("spread_ready")
        o_ready = sem("o_ready")
        y_part = sem("y_part")
        bias_ready = sem("bias_ready")
        b_ready = sem("b_ready")
        x_ready = sem("x_ready")
        n_loads = 1 if b_dram is None else 3
        block = ctx.enter_context(nc.Block())

        @block.sync
        def _(sp):
            sp.dma_start(sums[:, :], o_dram[:, d, :].rearrange("h (a t) -> h a t", a=SPLIT)).then_inc(sums_in, 16)
            sp.dma_start(w[:, :, :], w_dram).then_inc(consts_in, 16)
            if b_dram is not None:
                sp.dma_start(b[:, :], b_dram).then_inc(consts_in, 16)
                sp.dma_start(b_v[:, :], b_v_dram).then_inc(consts_in, 16)
            sp.dma_start(spread_f[:, :], spread_dram).then_inc(w_in, 16)
            for g in range(groups):
                if g == 1:
                    sp.wait_ge(inverse_in, 48)
                sp.dma_start(o[:, g, :], o_dram[g * per:(g + 1) * per, 0:d, :]).then_inc(o_in[g], 16)

        @block.gpsimd
        def _(pool):
            nc.gpsimd.memset(inverse_row[:, :], 0.0).then_inc(rows_clear, 1)

        @block.scalar
        def _(act):
            act.wait_ge(w_in, 16)
            nc.scalar.copy(spread[:, :], spread_f[:, :]).then_inc(spread_set, 1)
            act.wait_ge(rows_clear, 1)
            for k in range(3):
                act.wait_ge(part_ready, k + 1)
                act.dma_start(inverse_row[k * H:(k + 1) * H, :].rearrange("h (a t) -> h a t", a=SPLIT),
                              parts[:, k, :]).then_inc(inverse_in, 16)

        @block.tensor
        def _(pe):
            pe.wait_ge(consts_in, 16 * n_loads)
            if b_dram is not None:
                nc.tensor.matmul(psum[:, 3, 0:1], w[:, 0, :], b_v[:, :], start=True, stop=True).then_inc(bias_ready, 1)
            pe.wait_ge(spread_set, 1)
            pe.wait_ge(inverse_in, 48)
            units = [(g, c) for g in range(groups) for c in range(CH)]

            def spread_sums(n):
                g, c = units[n]
                after(pe, o_ready, n - 1)
                nc.tensor.matmul(psum[:, n % 2, :], spread[:, g * P:(g + 1) * P],
                                 inverse_row[:, c * CW:(c + 1) * CW], start=True, stop=True).then_inc(spread_ready, 1)

            def out(n):
                g, c = units[n]
                pe.wait_ge(o_ready, n + 1)
                nc.tensor.matmul(psum[:, CH + c, :], w[:, g, :], o_unit[:, n % 2, :],
                                 start=g == 0, stop=g == groups - 1).then_inc(y_part, 1)

            spread_sums(0)
            for n in range(len(units)):
                if n + 1 < len(units):
                    spread_sums(n + 1)
                out(n)

        @block.vector
        def _(dve):
            dve.wait_ge(sums_in, 16)
            nc.vector.reciprocal(inverse[:, :], sums[:, :]).then_inc(inverse_ready, 1)
            dve.wait_ge(inverse_ready, 1)
            nc.vector.tensor_copy(parts[:, 0, :], inverse[:, :]).then_inc(part_ready, 1)
            left = inverse[:, :]
            for k in range(2):
                dve.wait_ge(part_ready, k + 1)
                nc.vector.tensor_tensor(rest[:, k, :], left, parts[:, k, :], ALU.subtract).then_inc(rest_ready, 1)
                left = rest[:, k, :]
                dve.wait_ge(rest_ready, k + 1)
                nc.vector.tensor_copy(parts[:, k + 1, :], left).then_inc(part_ready, 1)
            if b_dram is None:
                nc.vector.memset(b_all[:, :], 0.0).then_inc(b_ready, 1)
            else:
                dve.wait_ge(bias_ready, 1)
                dve.wait_ge(consts_in, 16 * n_loads)
                nc.vector.tensor_tensor(b_all[:, :], psum[:, 3, 0:1], b[:, :], ALU.add).then_inc(b_ready, 1)
            n = 0
            for g in range(groups):
                for c in range(CH):
                    dve.wait_ge(o_in[g], 16)
                    dve.wait_ge(spread_ready, n + 1)
                    after(dve, y_part, n - 1)
                    nc.vector.tensor_tensor(o_unit[:, n % 2, :], o[:, g, c * CW:(c + 1) * CW], psum[:, n % 2, :],
                                            ALU.mult).then_inc(o_ready, 1)
                    n += 1
            dve.wait_ge(b_ready, 1)
            for c in range(CH):
                dve.wait_ge(y_part, (groups - 1) * CH + c + 1)
                at = slice(c * CW, (c + 1) * CW)
                nc.vector.scalar_tensor_tensor(x[:, at], psum[:, CH + c, :], b_all[:, 0:1], x[:, at],
                                               ALU.add, ALU.add).then_inc(x_ready, 1)


def mlp(nc, psum, name, xn, w1_dram, b1_dram, w2_dram, b2_dram, x):
    HB = 4
    with ExitStack() as ctx:
        def sb(n, shape, dt=F32):
            return ctx.enter_context(nc.sbuf_tensor(f"{name}_{n}", shape, dt))

        sem = stage_semaphores(nc, ctx, name)

        w1 = sb("w1", [P, HB * P])
        w2 = sb("w2", [P, HB, P])
        b1 = sb("b1", [P, HB])
        b2 = sb("b2", [P, 1])
        hidden = sb("hidden", [P, HB, CW])
        w_in = sem("w_in")
        b_clear = sem("b_clear")
        h_ready = sem("h_ready")
        h_done = sem("h_done")
        y_ready = sem("y_ready")
        y_part = sem("y_part")
        x_ready = sem("x_ready")
        loads = [(w1[:, :], w1_dram), (w2[:, :, :], w2_dram)]
        if b1_dram is not None:
            loads += [(b1[:, :], b1_dram), (b2[:, :], b2_dram)]
        block = ctx.enter_context(nc.Block())

        @block.sync
        def _(sp):
            for dst, src in loads:
                sp.dma_start(dst, src).then_inc(w_in, 16)

        @block.tensor
        def _(pe):
            pe.wait_ge(w_in, 16 * len(loads))
            units = [(c, j) for c in range(CH) for j in range(HB)]

            def out(n):
                c, j = units[n]
                pe.wait_ge(h_done, n + 1)
                nc.tensor.matmul(psum[:, CH + c, :], w2[:, j, :], hidden[:, j, :], start=j == 0,
                                 stop=j == HB - 1).then_inc(y_part, 1)

            for n, (c, j) in enumerate(units):
                after(pe, h_done, n - 1)
                nc.tensor.matmul(psum[:, n % 2, :], w1[:, j * P:(j + 1) * P], xn[:, c * CW:(c + 1) * CW],
                                 start=True, stop=True).then_inc(h_ready, 1)
                if n:
                    out(n - 1)
            out(len(units) - 1)

        @block.scalar
        def _(act):
            act.wait_ge(w_in, 16 * len(loads))
            if b1_dram is None:
                act.wait_ge(b_clear, 1)
            n = 0
            for c in range(CH):
                for j in range(HB):
                    act.wait_ge(h_ready, n + 1)
                    after(act, y_part, n - HB + 1)
                    nc.scalar.activation(hidden[:, j, :], psum[:, n % 2, :], ACT.Gelu,
                                         bias=b1[:, j:j + 1]).then_inc(h_done, 1)
                    n += 1

        @block.vector
        def _(dve):
            dve.wait_ge(w_in, 16 * len(loads))
            if b1_dram is None:
                nc.vector.memset(b2[:, :], 0.0).then_inc(y_ready, 1)
                nc.vector.memset(b1[:, :], 0.0).then_inc(b_clear, 1)
                dve.wait_ge(y_ready, 1)
            for c in range(CH):
                dve.wait_ge(y_part, HB * (c + 1))
                at = slice(c * CW, (c + 1) * CW)
                nc.vector.scalar_tensor_tensor(x[:, at], psum[:, CH + c, :], b2[:, 0:1], x[:, at],
                                               ALU.add, ALU.add).then_inc(x_ready, 1)


def route(nc, psum, name, t, w_dram, b_dram, E, gates_t, ident, kind):
    with ExitStack() as ctx:
        def sb(n, shape, dt=F32):
            return ctx.enter_context(nc.sbuf_tensor(f"{name}_{n}", shape, dt))

        sem = stage_semaphores(nc, ctx, name)

        w = sb("w", [P, E])
        b = sb("b", [P, E])
        logits = sb("logits", [P, TT, E])
        gates = sb("gates", [P, TT, E])
        top = sb("top", [P, TT, 8])
        t1 = sb("t1", [P, TT, E])
        t2 = sb("t2", [P, TT, E])
        t3 = sb("t3", [P, TT, E])
        col = sb("col", [P, TT])
        col2 = sb("col2", [P, TT])
        col3 = sb("col3", [P, TT])
        index = sb("index", [P, TT, 8], mybir.dt.uint32)
        index_f = sb("index_f", [P, TT, 8])
        expert = sb("expert", [P, E])
        w_in = sem("w_in")
        expert_ready = sem("expert_ready")
        logit_ready = sem("logit_ready")
        logit_taken = sem("logit_taken")
        step = sem("step")
        act_in = sem("act_in")
        act_out = sem("act_out")
        gates_ready = sem("gates_ready")
        turned = sem("turned")
        turned_out = sem("turned_out")
        n_loads = 1 + (b_dram is not None)
        block = ctx.enter_context(nc.Block())

        @block.sync
        def _(sp):
            sp.dma_start(w[:, :], w_dram).then_inc(w_in, 16)
            if b_dram is not None:
                sp.dma_start(b[:, :], b_dram.partition_broadcast(P)).then_inc(w_in, 16)

        @block.gpsimd
        def _(pool):
            nc.gpsimd.iota(expert[:, :], pattern=[[1, E]], base=0, channel_multiplier=0,
                           allow_small_or_imprecise_dtypes=True).then_inc(expert_ready, 1)

        @block.tensor
        def _(pe):
            pe.wait_ge(w_in, 16 * n_loads)
            for i in range(TT):
                after(pe, logit_taken, i - 3)
                nc.tensor.matmul(psum[:, i % 4, 0:E], t[:, i * P:(i + 1) * P], w[:, :], start=True,
                                 stop=True).then_inc(logit_ready, 1)
            pe.wait_ge(gates_ready, 1)
            for i in range(TT):
                nc.tensor.transpose(psum[0:E, 4 + i // 4, (i % 4) * P:(i % 4 + 1) * P], gates[:, i, :],
                                    ident[:, :]).then_inc(turned, 1)

        @block.vector
        def _(dve):
            count = [0]

            def link(ins):
                count[0] += 1
                ins.then_inc(step, 1)
                dve.wait_ge(step, count[0])

            dve.wait_ge(w_in, 16 * n_loads)
            for i in range(TT):
                dve.wait_ge(logit_ready, i + 1)
                if b_dram is None:
                    ins = nc.vector.tensor_copy(logits[:, i, :], psum[:, i % 4, 0:E])
                else:
                    ins = nc.vector.tensor_tensor(logits[:, i, :], psum[:, i % 4, 0:E], b[:, :], ALU.add)
                ins.then_inc(logit_taken, 1)
            dve.wait_ge(logit_taken, TT)
            full = [P, TT, E]
            if kind == "latent":
                link(nc.vector.tensor_scalar(t1[:, :, :], logits[:, :, :], 10.0, -10.0, ALU.min, ALU.max))
                link(nc.vector.tensor_scalar(t2[:, :, :], t1[:, :, :], -1.0, None, ALU.mult))
                nc.vector.tensor_tensor(t3[:, :, :], t1[:, :, :], t2[:, :, :], ALU.min).then_inc(act_in, 1)
                dve.wait_ge(act_out, 1)
                link(nc.vector.tensor_scalar(t3[:, :, :], t2[:, :, :], 1.0, None, ALU.add))
                nc.vector.tensor_scalar(logits[:, :, :], t3[:, :, :], -1.0, None, ALU.add).then_inc(act_in, 1)
                dve.wait_ge(act_in, 2)
                link(nc.vector.reciprocal(gates[:, :, :], logits[:, :, :]))
                link(nc.vector.tensor_tensor(logits[:, :, :], t2[:, :, :], gates[:, :, :], ALU.mult))
                dve.wait_ge(act_out, 2)
                link(nc.vector.tensor_tensor(t2[:, :, :], logits[:, :, :], t3[:, :, :], ALU.mult))
                link(nc.vector.tensor_scalar(t3[:, :, :], t1[:, :, :], 0.0, None, ALU.max))
                link(nc.vector.tensor_tensor(t1[:, :, :], t3[:, :, :], t2[:, :, :], ALU.add))
                for i in range(TT):
                    last = nc.vector.max(top[:, i, :], t1[:, i, :])
                link(last)
                for i in range(TT):
                    last = nc.vector.match_replace(t2[:, i, :], top[:, i, :], t1[:, i, :], -1.0)
                link(last)
                link(nc.vector.tensor_tensor(t3[:, :, :], t1[:, :, :], t2[:, :, :], ALU.not_equal))
                link(nc.vector.tensor_tensor(t2[:, :, :], t1[:, :, :], t3[:, :, :], ALU.mult))
                nc.vector.tensor_reduce(col[:, :], top[:, :, :], AX.X, ALU.add).then_inc(act_in, 1)
                dve.wait_ge(act_in, 3)
                link(nc.vector.tensor_scalar(col2[:, :], col[:, :], 1e-6, None, ALU.add))
                link(nc.vector.reciprocal(col3[:, :], col2[:, :]))
                dve.wait_ge(act_out, 3)
                link(nc.vector.tensor_tensor(col2[:, :], col3[:, :], index_f[:, :, 0], ALU.mult))
                nc.vector.tensor_tensor(gates[:, :, :], t2[:, :, :],
                                        col2[:, :].unsqueeze(2).broadcast_to(full), ALU.mult).then_inc(gates_ready, 1)
            else:
                link(nc.vector.tensor_reduce(col[:, :], logits[:, :, :], AX.X, ALU.max))
                nc.vector.tensor_tensor(t1[:, :, :], logits[:, :, :], col[:, :].unsqueeze(2).broadcast_to(full),
                                        ALU.subtract).then_inc(act_in, 1)
                dve.wait_ge(act_out, 1)
                chosen = logits
                if kind == "probs":
                    link(nc.vector.tensor_reduce(col2[:, :], t2[:, :, :], AX.X, ALU.add))
                    link(nc.vector.reciprocal(col3[:, :], col2[:, :]))
                    link(nc.vector.tensor_tensor(t3[:, :, :], t2[:, :, :],
                                                 col3[:, :].unsqueeze(2).broadcast_to(full), ALU.mult))
                    chosen = t3
                for i in range(TT):
                    last = nc.vector.max(top[:, i, :], chosen[:, i, :])
                link(last)
                for i in range(TT):
                    last = nc.vector.max_index(index[:, i, :], top[:, i, :], chosen[:, i, :])
                link(last)
                link(nc.vector.tensor_copy(index_f[:, :, :], index[:, :, :]))
                dve.wait_ge(expert_ready, 1)
                names = expert[:, :].unsqueeze(1).broadcast_to(full)
                link(nc.vector.tensor_tensor(t1[:, :, :], names, index_f[:, :, 0:1].broadcast_to(full),
                                             ALU.is_equal))
                link(nc.vector.tensor_tensor(t3[:, :, :], names, index_f[:, :, 1:2].broadcast_to(full),
                                             ALU.is_equal))
                link(nc.vector.tensor_tensor(logits[:, :, :], t1[:, :, :], t3[:, :, :], ALU.add))
                link(nc.vector.tensor_tensor(t1[:, :, :], logits[:, :, :], t2[:, :, :], ALU.mult))
                link(nc.vector.tensor_reduce(col2[:, :], t1[:, :, :], AX.X, ALU.add))
                link(nc.vector.reciprocal(col3[:, :], col2[:, :]))
                nc.vector.tensor_tensor(gates[:, :, :], t1[:, :, :],
                                        col3[:, :].unsqueeze(2).broadcast_to(full), ALU.mult).then_inc(gates_ready, 1)
            for k in range(4):
                dve.wait_ge(turned, 4 * (k + 1))
                nc.vector.tensor_copy(gates_t[0:E, k * CW:(k + 1) * CW], psum[0:E, 4 + k, :]
                                      ).then_inc(turned_out, 1)

        @block.scalar
        def _(act):
            act.wait_ge(act_in, 1)
            if kind == "latent":
                nc.scalar.activation(t2[:, :, :], t3[:, :, :], ACT.Exp).then_inc(act_out, 1)
                act.wait_ge(act_in, 2)
                nc.scalar.activation(t3[:, :, :], t3[:, :, :], ACT.Ln).then_inc(act_out, 1)
                act.wait_ge(act_in, 3)
                nc.scalar.activation(index_f[:, :, 0], col[:, :], ACT.Tanh).then_inc(act_out, 1)
            else:
                nc.scalar.activation(t2[:, :, :], t1[:, :, :], ACT.Exp).then_inc(act_out, 1)


def latent(nc, psum, name, xn, u_t_dram, u_dram, v_dram, gamma_dram, gates_t, x):
    E = 64
    with ExitStack() as ctx:
        def sb(n, shape, dt=F32):
            return ctx.enter_context(nc.sbuf_tensor(f"{name}_{n}", shape, dt))

        sem = stage_semaphores(nc, ctx, name)

        u_t = sb("u_t", [P, E])
        uv = sb("uv", [E, 2, P])
        squares = sb("squares", [E, 2, P])
        length = sb("length", [E, 2])
        root = sb("root", [E, 2])
        inverse = sb("inverse", [E, 2])
        both = sb("both", [E, 1])
        gamma = sb("gamma", [P, 1])
        mixed = sb("mixed", [E, CH, CW])
        w_in = sem("w_in")
        step = sem("step")
        length_ready = sem("length_ready")
        root_ready = sem("root_ready")
        h_ready = sem("h_ready")
        mixed_ready = sem("mixed_ready")
        y_ready = sem("y_ready")
        x_ready = sem("x_ready")
        block = ctx.enter_context(nc.Block())

        @block.sync
        def _(sp):
            for dst, src in ((u_t[:, :], u_t_dram), (uv[:, 0, :], u_dram), (uv[:, 1, :], v_dram),
                             (gamma[:, :], gamma_dram)):
                sp.dma_start(dst, src).then_inc(w_in, 16)

        @block.tensor
        def _(pe):
            pe.wait_ge(w_in, 64)
            for c in range(CH):
                nc.tensor.matmul(psum[0:E, c, :], u_t[:, :], xn[:, c * CW:(c + 1) * CW], start=True,
                                 stop=True).then_inc(h_ready, 1)
            for c in range(CH):
                pe.wait_ge(mixed_ready, c + 1)
                nc.tensor.matmul(psum[:, CH + c, :], uv[:, 1, :], mixed[:, c, :], start=True,
                                 stop=True).then_inc(y_ready, 1)

        @block.scalar
        def _(act):
            act.wait_ge(length_ready, 1)
            nc.scalar.activation(root[:, :], length[:, :], ACT.Sqrt).then_inc(root_ready, 1)

        @block.vector
        def _(dve):
            count = [0]

            def link(ins):
                count[0] += 1
                ins.then_inc(step, 1)
                dve.wait_ge(step, count[0])

            dve.wait_ge(w_in, 64)
            link(nc.vector.tensor_tensor(squares[:, :, :], uv[:, :, :], uv[:, :, :], ALU.mult))
            nc.vector.tensor_reduce(length[:, :], squares[:, :, :], AX.X, ALU.add).then_inc(length_ready, 1)
            dve.wait_ge(root_ready, 1)
            link(nc.vector.tensor_scalar(length[:, :], root[:, :], 1e-6, None, ALU.max))
            link(nc.vector.reciprocal(inverse[:, :], length[:, :]))
            link(nc.vector.tensor_tensor(both[:, :], inverse[:, 0:1], inverse[:, 1:2], ALU.mult))
            for c in range(CH):
                dve.wait_ge(h_ready, c + 1)
                nc.vector.scalar_tensor_tensor(mixed[:, c, :], psum[0:E, c, :], both[:, 0:1],
                                               gates_t[0:E, c * CW:(c + 1) * CW], ALU.mult,
                                               ALU.mult).then_inc(mixed_ready, 1)
            for c in range(CH):
                dve.wait_ge(y_ready, c + 1)
                at = slice(c * CW, (c + 1) * CW)
                nc.vector.scalar_tensor_tensor(x[:, at], psum[:, CH + c, :], gamma[:, 0:1], x[:, at],
                                               ALU.mult, ALU.add).then_inc(x_ready, 1)


def experts(nc, psum, name, t, residual, gates_t, gates_dram, w1_dram, b1_dram, w2_dram, b2_dram, x, kind):
    E, HB = 8, 4
    OB = 4 if kind == "gelu" else 2
    with ExitStack() as ctx:
        def sb(n, shape, dt=F32):
            return ctx.enter_context(nc.sbuf_tensor(f"{name}_{n}", shape, dt))

        sem = stage_semaphores(nc, ctx, name)

        w1 = sb("w1", [P, E, HB * P])
        w2 = sb("w2", [P, E, OB, P])
        b1 = sb("b1", [P, E * HB])
        b2 = sb("b2", [E, P])
        gate = sb("gate", [P, E, CW])
        hidden = sb("hidden", [P, 4, CW])
        gated = sb("gated", [P, 2, CW])
        total = sb("total", [P, CW])
        extra = sb("extra", [P, CW])
        glu = sb("glu", [P, 4, CW])
        sig = sb("sig", [P, 4, CW])
        lin = sb("lin", [P, 4, CW])
        prod = sb("prod", [P, 4, CW])
        w_in = [sem(f"w_in{e}") for e in range(E)]
        b_in = sem("b_in")
        gates_out = sem("gates_out")
        gate_in = [sem(f"gate_in{e}") for e in range(E)]
        h_ready = sem("h_ready")
        raw_ready = sem("raw_ready")
        h_done = sem("h_done")
        y_part = sem("y_part")
        y_taken = sem("y_taken")
        bias_ready = sem("bias_ready")
        total_step = sem("total_step")
        extra_ready = sem("extra_ready")
        x_ready = sem("x_ready")
        glu_ready = sem("glu_ready")
        sig_ready = sem("sig_ready")
        lin_ready = sem("lin_ready")
        prod_ready = sem("prod_ready")
        block = ctx.enter_context(nc.Block())
        order = [0, 1, 2, 3] if kind == "gelu" else [0, 2, 1, 3]
        NY = E * OB
        NH = E * HB
        OUT_LAG = 2 if kind == "gelu" else 3

        def over_chunks(eng, body):
            body(0)
            with eng.Fori(1, CH) as c:
                body(c)

        @block.sync
        def _(sp):
            sp.dma_start(gates_dram[:, :], gates_t[0:E, :]).then_inc(gates_out, 16)
            sp.dma_start(b1[:, :], b1_dram).then_inc(b_in, 16)
            sp.dma_start(b2[:, :], b2_dram).then_inc(b_in, 16)
            for e in range(E):
                sp.dma_start(w1[:, e, :], w1_dram[:, e, :]).then_inc(w_in[e], 16)
                sp.dma_start(w2[:, e, :, :], w2_dram[:, e, :, :]).then_inc(w_in[e], 16)
            sp.wait_ge(gates_out, 16)

            def chunk(c):
                for e in range(E):
                    after(sp, y_taken, c * E + (e + 1 - E))
                    sp.dma_start(gate[:, e, :], gates_dram[e, bass.ds(c * CW, CW)].partition_broadcast(P)
                                 ).then_inc(gate_in[e], 16)
            over_chunks(sp, chunk)

        @block.tensor
        def _(pe):
            def out(c, k):
                e, j = k // OB, k % OB
                pe.wait_ge(h_done, c * NY + (k + 1))
                if j == 0:
                    after(pe, y_taken, c * E + (e - 1))
                nc.tensor.matmul(psum[:, 4 + e % 2, :], w2[:, e % E, j, :], hidden[:, k % 4, :],
                                 start=j == 0, stop=j == OB - 1).then_inc(y_part, 1)

            def chunk(c):
                pe.wait_ge(b_in, 32)
                after(pe, extra_ready, c)
                nc.tensor.matmul(psum[:, 6, :], b2[:, :], gates_t[0:E, bass.ds(c * CW, CW)], start=True,
                                 stop=True).then_inc(bias_ready, 1)
                for e in range(E):
                    pe.wait_ge(w_in[e], 32)
                    for i, j in enumerate(order):
                        k = e * HB + i
                        if kind == "gelu":
                            after(pe, h_done, c * NH + (k - 3))
                        else:
                            after(pe, raw_ready, c * NH + 2 * (k // 2 - 1))
                        nc.tensor.matmul(psum[:, k % 4, :], w1[:, e, j * P:(j + 1) * P],
                                         t[:, bass.ds(c * CW, CW)], start=True, stop=True).then_inc(h_ready, 1)
                        done = k + 1 if kind == "gelu" else k // 2 + 1
                        if (kind == "gelu" or j >= 2) and (not isinstance(c, int) or done > OUT_LAG):
                            out(c, done - 1 - OUT_LAG)
            over_chunks(pe, chunk)
            for k in range(-OUT_LAG, 0):
                out(CH, k)

        @block.scalar
        def _(act):
            act.wait_ge(b_in, 32)

            def gate_half(c, k):
                act.wait_ge(glu_ready, c * NY + (k + 1))
                after(act, h_done, c * NY + (k - 3))
                nc.scalar.activation(sig[:, k % 4, :], glu[:, k % 4, :], ACT.Sigmoid,
                                     scale=1.702).then_inc(sig_ready, 1)

            def chunk(c):
                for e in range(E):
                    if kind == "gelu":
                        for j in range(HB):
                            n = c * NH + (e * HB + j)
                            act.wait_ge(h_ready, n + 1)
                            after(act, y_part, n - HB + 1)
                            nc.scalar.activation(hidden[:, j, :], psum[:, j, :], ACT.Gelu,
                                                 bias=b1[:, e * HB + j:e * HB + j + 1]).then_inc(h_done, 1)
                    else:
                        for j in range(2):
                            k = e * 2 + j
                            n = c * NY + k
                            after(act, prod_ready, c * NY + (k - 3))
                            for i, dst in ((0, glu), (1, lin)):
                                b = e * HB + 2 * i + j
                                act.wait_ge(h_ready, c * NH + (2 * k + i + 1))
                                nc.scalar.activation(dst[:, k % 4, :], psum[:, (2 * k + i) % 4, :], ACT.Identity,
                                                     bias=b1[:, b:b + 1]).then_inc(raw_ready, 1)
                            if k:
                                gate_half(c, k - 1)
                if kind == "swiglu":
                    gate_half(c, NY - 1)
            over_chunks(act, chunk)

        @block.vector
        def _(dve):
            dve.wait_ge(b_in, 32)

            def take(c, e):
                dve.wait_ge(gate_in[e], c * 16 + 16)
                dve.wait_ge(y_part, c * NY + (e * OB + OB))
                after(dve, total_step, c * E + (e - 1))
                nc.vector.tensor_tensor(gated[:, e % 2, :], psum[:, 4 + e % 2, :], gate[:, e, :],
                                        ALU.mult).then_inc(y_taken, 1)

            def chunk(c):
                at = bass.ds(c * CW, CW)
                dve.wait_ge(bias_ready, c + 1)
                after(dve, total_step, c * E)
                nc.vector.tensor_tensor(extra[:, :], psum[:, 6, :], residual[:, at],
                                        ALU.add).then_inc(extra_ready, 1)
                for e in range(E):
                    if kind == "swiglu":
                        for j in range(2):
                            k = e * 2 + j
                            dve.wait_ge(raw_ready, c * NH + (2 * k + 1))
                            nc.vector.tensor_scalar(glu[:, k % 4, :], glu[:, k % 4, :], 7.0, None,
                                                    ALU.min).then_inc(glu_ready, 1)
                            dve.wait_ge(raw_ready, c * NH + (2 * k + 2))
                            nc.vector.tensor_scalar(lin[:, k % 4, :], lin[:, k % 4, :], 7.0, -7.0, ALU.min,
                                                    ALU.max).then_inc(lin_ready, 1)
                            dve.wait_ge(glu_ready, c * NY + (k + 1))
                            dve.wait_ge(lin_ready, c * NY + (k + 1))
                            after(dve, h_done, c * NY + (k - 3))
                            nc.vector.scalar_tensor_tensor(prod[:, k % 4, :], lin[:, k % 4, :], 1.0,
                                                           glu[:, k % 4, :], ALU.add, ALU.mult
                                                           ).then_inc(prod_ready, 1)
                    if e >= 2:
                        take(c, e - 2)
                take(c, E - 2)
                take(c, E - 1)
            over_chunks(dve, chunk)

        @block.gpsimd
        def _(pool):
            def add_up(c, e):
                pool.wait_ge(y_taken, c * E + (e + 1))
                if e == 0:
                    pool.wait_ge(extra_ready, c + 1)
                    after(pool, x_ready, c)
                    nc.gpsimd.tensor_tensor(total[:, :], extra[:, :], gated[:, 0, :],
                                            ALU.add).then_inc(total_step, 1)
                else:
                    pool.wait_ge(total_step, c * E + e)
                    nc.gpsimd.tensor_tensor(total[:, :], total[:, :], gated[:, e % 2, :],
                                            ALU.add).then_inc(total_step, 1)

            def chunk(c):
                for e in range(E):
                    if kind == "swiglu":
                        for j in range(2):
                            k = e * 2 + j
                            pool.wait_ge(prod_ready, c * NY + (k + 1))
                            pool.wait_ge(sig_ready, c * NY + (k + 1))
                            after(pool, y_part, c * NY + (k - 3))
                            nc.gpsimd.tensor_tensor(hidden[:, k % 4, :], prod[:, k % 4, :], sig[:, k % 4, :],
                                                    ALU.mult).then_inc(h_done, 1)
                    if e >= 2:
                        add_up(c, e - 2)
                add_up(c, E - 2)
                add_up(c, E - 1)
                at = bass.ds(c * CW, CW)
                pool.wait_ge(total_step, (c + 1) * E)
                nc.gpsimd.tensor_tensor(x[:, at], x[:, at], total[:, :], ALU.add).then_inc(x_ready, 1)
            over_chunks(pool, chunk)


def block_stack(nc, a, out):
    with ExitStack() as ctx:
        psum = ctx.enter_context(nc.psum_tensor("psum", [P, 8, CW], F32))
        x = ctx.enter_context(nc.sbuf_tensor("x", [P, S], F32))
        xn = ctx.enter_context(nc.sbuf_tensor("xn", [P, S], F32))
        ident = ctx.enter_context(nc.sbuf_tensor("ident", [P, P], F32))
        mean_w = ctx.enter_context(nc.sbuf_tensor("mean_w", [P, P], F32))
        pick = ctx.enter_context(nc.sbuf_tensor("pick", [P, CH * P], F32))
        loaded = ctx.enter_context(nc.semaphore("loaded"))
        dve_set = ctx.enter_context(nc.semaphore("dve_set"))
        pool_set = ctx.enter_context(nc.semaphore("pool_set"))

        def dram(name, shape, dt=F32):
            return nc.dram_tensor(name, shape, dt).ap()

        def narrow_attention(n, jobs, w_loads, rope, q_ring, k_res, q_dram, k_dram, rings=None):
            o_dram = dram(f"o{n}", (H, 9, S))
            with nc.sbuf_tensor(f"v_all{n}", [P, TT, P], F32) as v_all, \
                    nc.sbuf_tensor(f"w_v{n}", [P, P], F32) as w_v:
                project(nc, psum, f"proj{n}", xn, jobs, w_loads, rope, w_v[:, :], a[f"l{n}_wv"], rings)
                attend(nc, psum, ident, xn, w_v, P, v_all, q_ring, k_res, q_dram, k_dram, o_dram, False,
                       8 ** -0.5, f"att{n}")
            project_out(nc, psum, f"out{n}", o_dram, 8, a[f"l{n}_wo"], a[f"l{n}_bo"], a[f"l{n}_bv"],
                        a["spread_narrow"], x)

        with nc.sbuf_tensor("q_ring", [P, 4 * S], BF16) as q_ring, nc.sbuf_tensor("k_res", [P, H * S], BF16) as k_res:
            with nc.Block() as block:
                @block.sync
                def _(sp):
                    for c in range(CH):
                        at = slice(c * CW, (c + 1) * CW)
                        sp.dma_start(x[:, at], a["x_t"][:, at]).then_inc(loaded, 16)
                    sp.dma_start(ident[:, :], a["identity"]).then_inc(loaded, 16)
                    sp.dma_start(pick[:, :], a["pick"]).then_inc(loaded, 16)
                    sp.wait_ge(loaded, 16 * (CH + 2))

                @block.vector
                def _(dve):
                    nc.vector.memset(mean_w[:, :], 1.0 / P)
                    preset(dve, nc.vector, q_ring, k_res, False, 0, dve_set)

                @block.gpsimd
                def _(pool):
                    preset(pool, nc.gpsimd, q_ring, k_res, False, 1, pool_set)
            normalise(nc, psum, "norm0a", x, xn, mean_w, pick, 1e-5)
            q, k = dram("q0", (3, P, S), BF16), dram("k0", (3, P, S), BF16)
            narrow_attention(0, [(a["l0_bq"], None, q), (a["l0_bk"], None, k)],
                             [(0, 1, a["l0_wq"], None), (1, 1, a["l0_wk"], None)], None, q_ring, k_res, q, k)
            normalise(nc, psum, "norm0f", x, xn, mean_w, pick, 1e-5)
            with nc.sbuf_tensor("gates0", [64, S], F32) as gates_t:
                with nc.sbuf_tensor("router_in0", [P, S], F32) as router_in:
                    normalise(nc, psum, "norm0r", xn, router_in, mean_w, pick, 1e-5, gain=a["l0_ln_g"],
                              shift=a["l0_ln_b"])
                    route(nc, psum, "route0", router_in, a["l0_router"], a["l0_router_b"], 64, gates_t, ident,
                          "latent")
                latent(nc, psum, "latent0", xn, a["l0_u_t"], a["l0_u"], a["l0_v"], a["l0_gamma"], gates_t, x)
            mlp(nc, psum, "mlp0", xn, a["l0_w1"], None, a["l0_w2"], None, x)

            normalise(nc, psum, "norm1a", x, xn, mean_w, pick, 1e-5)
            q, k = dram("q1", (3, P, S), BF16), dram("k1", (3, P, S), BF16)
            narrow_attention(1, [(a["l1_bq"], a["l1_bq_turned"], q), (a["l1_bk"], a["l1_bk_turned"], k)],
                             [(0, 1, a["l1_wq"], a["l1_wq_turned"]), (1, 1, a["l1_wk"], a["l1_wk_turned"])],
                             (a["l1_cos"], a["l1_sin"]), q_ring, k_res, q, k)
            normalise(nc, psum, "norm1f", x, xn, mean_w, pick, 1e-5)
            mlp(nc, psum, "mlp1", xn, a["l1_w1"], a["l1_b1"], a["l1_w2"], a["l1_b2"], x)

        normalise(nc, psum, "norm2a", x, xn, mean_w, pick, 1e-5)
        q, k, o = dram("q2", (2, 8 * P, S), F16), dram("k2", (2, 2 * P, S), F16), dram("o2", (H, 65, S))
        jobs = [(None, None, q[:, i * P:(i + 1) * P, :]) for i in range(8)]
        jobs += [(None, None, k[:, i * P:(i + 1) * P, :]) for i in range(2)]
        w_loads = [(0, 8, a["l2_wq"], a["l2_wq_turned"]), (8, 2, a["l2_wk"], a["l2_wk_turned"])]
        with nc.sbuf_tensor("v_all2", [P, TT, 2 * P], F32) as v_all, \
                nc.sbuf_tensor("w_v2", [P, 2 * P], F32) as w_v, nc.sbuf_tensor("exp_scale", [P, 1], F32) as exp_scale, \
                nc.sbuf_tensor("q_ring2", [P, 4 * 2 * S], F16) as q_ring, \
                nc.sbuf_tensor("k_res2", [P, 4 * 2 * S], F16) as k_res:
            project(nc, psum, "proj2", xn, jobs, w_loads, (a["l2_cos"], a["l2_sin"]), w_v[:, :], a["l2_wv"],
                    (q_ring, k_res), mean_w, exp_scale, 8)
            attend(nc, psum, ident, xn, w_v, 2 * P, v_all, q_ring, k_res, q, k, o, True, exp_scale[:, :], "att2")
        project_out(nc, psum, "out2", o, 64, a["l2_wo"], None, None, a["spread_wide"], x)
        normalise(nc, psum, "norm2f", x, xn, mean_w, pick, 1e-5)
        with nc.sbuf_tensor("gates2", [8, S], F32) as gates_t, nc.sbuf_tensor("expert_in2", [P, S], F32) as t:
            normalise(nc, psum, "norm2e", xn, t, mean_w, pick, 1e-5, gain=a["l2_gamma"], shift=a["l2_beta"])
            route(nc, psum, "route2", t, a["l2_gate"], None, 8, gates_t, ident, "probs")
            experts(nc, psum, "moe2", t, xn, gates_t, dram("gates2_dram", (8, S)), a["l2_w1"], a["l2_b1"], a["l2_w2"],
                    a["l2_b2"], x, "gelu")

        with nc.sbuf_tensor("q_ring3", [P, 4 * S], BF16) as q_ring, nc.sbuf_tensor("k_res3", [P, H * S], BF16) as k_res:
            normalise(nc, psum, "norm3a", x, xn, mean_w, pick, 1e-5)
            q, k = dram("q3", (3, P, S), BF16), dram("k3", (3, P, S), BF16)
            narrow_attention(3, [(a["zero_col"], None, q), (a["zero_col"], None, k)],
                             [(0, 1, a["l3_wq"], None), (1, 1, a["identity"], None)], None, q_ring, k_res, q, k,
                             (q_ring, k_res))
        normalise(nc, psum, "norm3f", x, xn, mean_w, pick, 1e-5)
        with nc.sbuf_tensor("gates3", [8, S], F32) as gates_t, nc.sbuf_tensor("expert_in3", [P, S], F32) as t:
            normalise(nc, psum, "norm3e", xn, t, mean_w, pick, 1e-5, centre=False, gain=a["l3_norm"])
            route(nc, psum, "route3", t, a["l3_gate"], a["l3_gate_b"], 8, gates_t, ident, "logits")
            experts(nc, psum, "moe3", t, xn, gates_t, dram("gates3_dram", (8, S)), a["l3_w1"], a["l3_b1"], a["l3_w2"],
                    a["l3_b2"], x, "swiglu")

        stored = ctx.enter_context(nc.semaphore("stored"))
        with nc.Block() as block:
            @block.sync
            def _(sp):
                sp.dma_start(out, x[:, :]).then_inc(stored, 16)
                sp.wait_ge(stored, 16)


def rope_tables(dim, rows, turn):
    inv = (1.0 / 10000.0 ** (np.arange(0, dim, 2, dtype=np.float32) / np.float32(dim))).astype(np.float32)
    angle = np.outer(inv, np.arange(S, dtype=np.float32)).astype(np.float32)
    d = np.arange(rows) % dim
    sign = np.where(turn(d), np.float32(-1), np.float32(1))[:, None]
    angle = angle[d % (dim // 2)]
    return np.cos(angle).astype(np.float32), (np.sin(angle) * sign).astype(np.float32)


def layout(i):
    def rows(w):
        return np.ascontiguousarray(w)

    def col(b):
        return rows(np.reshape(b, (P, 1)))

    a = {"x_t": rows(i["L0_attn_x"][0].T), "identity": np.eye(P, dtype=np.float32),
         "zero_col": np.zeros((P, 1), np.float32)}
    h = np.arange(P)[:, None]
    a["pick"] = np.repeat(h == 32 * np.arange(CH)[None, :], P, axis=1).astype(np.float32)
    head = np.where(h < 3 * H, h % H, -1)
    a["spread_narrow"] = (np.arange(P)[None, :] // 8 == head).astype(np.float32)
    a["spread_wide"] = (np.arange(8 * P)[None, :] // 64 == head).astype(np.float32)
    for n in (0, 1):
        for s in "qkvo":
            a[f"l{n}_w{s}"] = rows(i[f"L{n}_attn_W{s}"].T)
            a[f"l{n}_b{s}"] = col(i[f"L{n}_attn_b{s}"])
    a["l0_w1"] = rows(i["L0_ffn_W1"].T)
    a["l0_w2"] = rows(i["L0_ffn_W2"].T.reshape(4, P, P).transpose(1, 0, 2))
    a["l0_ln_g"], a["l0_ln_b"] = col(i["L0_ffn_ln_g"]), col(i["L0_ffn_ln_b"])
    a["l0_router"], a["l0_router_b"] = rows(i["L0_ffn_router_W"].T), i["L0_ffn_router_b"]
    a["l0_u_t"], a["l0_u"], a["l0_v"] = rows(i["L0_ffn_raw_U"].T), i["L0_ffn_raw_U"], i["L0_ffn_raw_V"]
    a["l0_gamma"] = col(i["L0_ffn_gamma"])
    pair = np.arange(P) ^ 1
    for s in "qk":
        a[f"l1_w{s}_turned"] = rows(i[f"L1_attn_W{s}"][pair].T)
        a[f"l1_b{s}_turned"] = col(i[f"L1_attn_b{s}"][pair])
    a["l1_cos"], a["l1_sin"] = rope_tables(8, P, lambda d: d % 2 == 0)
    a["l1_w1"] = i["L1_ffn_w1"]
    a["l1_b1"] = rows(i["L1_ffn_b1"].reshape(4, P).T)
    a["l1_w2"] = rows(i["L1_ffn_w2"].reshape(4, P, P).transpose(1, 0, 2))
    a["l1_b2"] = col(i["L1_ffn_b2"])
    for s in "qkv":
        a[f"l2_w{s}"] = i[f"L2_attn_W{s}"]
    for s, n in (("q", 1024), ("k", 256)):
        a[f"l2_w{s}_turned"] = rows(i[f"L2_attn_W{s}"][:, np.arange(n) ^ 32])
    a["l2_cos"], a["l2_sin"] = rope_tables(64, P, lambda d: d < 32)
    a["l2_wo"] = rows(i["L2_attn_Wo"].reshape(8, P, P).transpose(1, 0, 2))
    a["l2_gamma"], a["l2_beta"], a["l2_gate"] = col(i["L2_ffn_gamma"]), col(i["L2_ffn_beta"]), i["L2_ffn_gate_w"]
    a["l2_w1"] = rows(i["L2_ffn_w1"].transpose(1, 0, 2))
    a["l2_b1"] = rows(i["L2_ffn_b1"].reshape(8, 4, P).transpose(2, 0, 1).reshape(P, 32))
    a["l2_w2"] = rows(i["L2_ffn_w2"].reshape(8, 4, P, P).transpose(2, 0, 1, 3))
    a["l2_b2"] = i["L2_ffn_b2"]
    wq = np.zeros((P, P), np.float32)
    for n in range(H):
        wq[8 * n:8 * n + 8, 8 * n:8 * n + 8] = i["L3_attn_w_att_val"][n]
    a["l3_wq"] = wq
    a["l3_wv"], a["l3_bv"] = rows(i["L3_attn_wv_w"].T), col(i["L3_attn_wv_b"])
    a["l3_wo"], a["l3_bo"] = rows(i["L3_attn_out_w"].T), col(i["L3_attn_out_b"])
    a["l3_norm"], a["l3_gate"], a["l3_gate_b"] = col(i["L3_ffn_norm_scale"]), i["L3_ffn_gate_w"], i["L3_ffn_gate_b"]
    halves = np.concatenate([np.arange(0, 512, 2), np.arange(1, 512, 2)])
    a["l3_w1"] = rows(i["L3_ffn_mlp1_w"][:, :, halves].transpose(1, 0, 2))
    a["l3_b1"] = rows(i["L3_ffn_mlp1_b"][:, halves].reshape(8, 4, P).transpose(2, 0, 1).reshape(P, 32))
    a["l3_w2"] = rows(i["L3_ffn_mlp2_w"].reshape(8, 2, P, P).transpose(2, 0, 1, 3))
    a["l3_b2"] = i["L3_ffn_mlp2_b"]
    return a


def kernel(**inputs):
    import concourse.bacc as _bacc
    from concourse.bass_utils import run_bass_kernel_spmd as _run

    nc = _bacc.Bacc("TRN2", target_bir_lowering=False, num_devices=1)
    arrays, args = {}, {}
    for name, value in layout({k: np.asarray(v) for k, v in inputs.items()}).items():
        value = np.ascontiguousarray(value)
        arrays[f"in_{name}"] = value
        args[name] = nc.dram_tensor(f"in_{name}", value.shape, mybir.dt.from_np(value.dtype),
                                    kind="ExternalInput").ap()
    out = nc.dram_tensor("out_y_t", (P, S), F32, kind="ExternalOutput").ap()
    block_stack(nc, args, out)
    r = _run(nc, [arrays], core_ids=[0])
    return np.ascontiguousarray(r.results[0]["out_y_t"].T)[None]
```
